# Optimizing a Trainium2 kernel written in Bass

```python
import numpy as np
import jax
import jax.numpy as jnp

def _softmax(x, axis=-1):
    return jax.nn.softmax(x, axis=axis)

def _gelu(x):
    return jax.nn.gelu(x, approximate=True)

def _silu(x):
    return jax.nn.silu(x)

def _sigmoid(x):
    return jax.nn.sigmoid(x)

def _layernorm(x, axis=-1, eps=1e-05):
    m = jnp.mean(x, axis=axis, keepdims=True)
    v = jnp.var(x, axis=axis, keepdims=True)
    return (x - m) / jnp.sqrt(v + eps)

def _scatter_add(tgt, idx, src, axis=0):
    return tgt.at[idx].add(src)

def _segment_sum(src, seg, n):
    return jax.ops.segment_sum(src, seg, n)
kernel_name = 'mk_perceiver_d2_seqx_r4_a836a7'

def setup_inputs(seed: int=0):
    np.random.seed(seed)
    _w = jnp.asarray

    def _rec_inputs():
        import jax
        import jax.numpy as jnp
        _rk = jax.random.key(seed)
        x = 7.22e-05 + 1 * jax.random.normal(jax.random.fold_in(_rk, 1), (4, 256, 256), jnp.float32)
        _lenS = 256 - jax.random.randint(jax.random.fold_in(_rk, 7), (4,), 0, max(1, 256 // 4) + 1, jnp.int32)
        _lenS2 = 4096 - jax.random.randint(jax.random.fold_in(_rk, 8), (4,), 0, max(1, 4096 // 4) + 1, jnp.int32)
        _ctx_1024P = jax.random.normal(jax.random.fold_in(_rk, 11), (4, 16, 256), jnp.float32)
        _ctx_1024c = jax.random.dirichlet(jax.random.fold_in(_rk, 511), 0.3 * jnp.ones((16,), jnp.float32), (4, 4096))
        _ctx_1024t = jnp.einsum('bsk,bkd->bsd', _ctx_1024c, _ctx_1024P)
        _ctx_1024t = _ctx_1024t * jax.lax.rsqrt(jnp.mean(jnp.square(_ctx_1024t)) + 1e-12) * 0.953939
        ctx_1024 = 4.13588e-05 + 0.999923 * (_ctx_1024t + 0.3 * jax.random.normal(jax.random.fold_in(_rk, 611), (4, 4096, 256), jnp.float32))
        _validS = jnp.arange(256)[None, :] < _lenS[:, None]
        _validS2 = jnp.arange(4096)[None, :] < _lenS2[:, None]
        _causal = jnp.tril(jnp.ones((256, 256), dtype=bool))
        mask_1x1xSxS2_fk1 = jnp.where(jnp.broadcast_to(_validS2[0:1, None, None, :], (1, 1, 256, 4096)), 1.0, 0.0).astype(jnp.float32)
        return (x, ctx_1024, mask_1x1xSxS2_fk1)
    x, ctx_1024, mask_1x1xSxS2_fk1 = _rec_inputs()

    def _L0_xattn_setup():
        import jax, jax.numpy as jnp
        import numpy as np
        D_MODEL = 256
        NUM_HEADS = 16
        DEPTH = D_MODEL // NUM_HEADS
        B, S = (4, 512)

        def _split_heads(x):
            b, s, _ = x.shape
            return x.reshape(b, s, NUM_HEADS, DEPTH).transpose(0, 2, 1, 3)
        key = jax.random.key(seed)
        ks = jax.random.split(key, 12)
        scale = 1.0 / np.sqrt(D_MODEL)
        inp = {'q': jax.random.normal(ks[0], (B, S, D_MODEL), jnp.float32), 'k': jax.random.normal(ks[1], (B, S, D_MODEL), jnp.float32), 'v': jax.random.normal(ks[2], (B, S, D_MODEL), jnp.float32), 'mask': jnp.triu(jnp.ones((S, S), jnp.float32), k=1)[None, None, :, :], 'wq': jax.random.normal(ks[3], (D_MODEL, D_MODEL), jnp.float32) * scale, 'bq': jnp.zeros((D_MODEL,), jnp.float32), 'wk': jax.random.normal(ks[4], (D_MODEL, D_MODEL), jnp.float32) * scale, 'bk': jnp.zeros((D_MODEL,), jnp.float32), 'wv': jax.random.normal(ks[5], (D_MODEL, D_MODEL), jnp.float32) * scale, 'bv': jnp.zeros((D_MODEL,), jnp.float32), 'wo': jax.random.normal(ks[6], (D_MODEL, D_MODEL), jnp.float32) * scale, 'bo': jnp.zeros((D_MODEL,), jnp.float32)}
        return inp
    _L0_xattn_all = _L0_xattn_setup()
    _L0_xattn_in = {k: v for k, v in _L0_xattn_all.items() if k in ('wq', 'bq', 'wk', 'bk', 'wv', 'bv', 'wo', 'bo')}
    del _L0_xattn_all

    def _L0_attn_setup():
        import jax, jax.numpy as jnp
        import numpy as np
        import math
        B, N, D, H = (8, 1024, 256, 16)
        DH = D // H
        key = jax.random.key(seed)
        k1, k2, k3, k4 = jax.random.split(key, 4)
        s = 1.0 / math.sqrt(D)
        return {'x': jax.random.normal(k1, (B, N, D), dtype=jnp.float32), 'Wqk': jax.random.normal(k2, (D, D), dtype=jnp.float32) * s, 'Wv': jax.random.normal(k3, (D, D), dtype=jnp.float32) * s, 'Wo': jax.random.normal(k4, (D, D), dtype=jnp.float32) * s, 'tau': jnp.ones((H, 1, 1), dtype=jnp.float32)}
    _L0_attn_all = _L0_attn_setup()
    _L0_attn_in = {k: v for k, v in _L0_attn_all.items() if k in ('Wqk', 'Wv', 'Wo', 'tau')}
    del _L0_attn_all

    def _L0_ffn_setup():
        import math
        import jax, jax.numpy as jnp
        import numpy as np
        B, T, H = (4, 512, 256)
        E, K, F = (8, 2, 512)
        CAP_FACTOR = 1.25

        def _moe_forward(x, Wg, W_in, W_out):
            b, t, h = x.shape
            xf = x.reshape(-1, h)
            S = xf.shape[0]
            C = int(math.ceil(K * S / E * CAP_FACTOR))
            logits = xf @ Wg
            probs = jax.nn.softmax(logits, axis=-1)
            top_vals, top_idx = jax.lax.top_k(probs, K)
            flat_idx = top_idx.T.reshape(-1)
            onehot = jax.nn.one_hot(flat_idx, E, dtype=jnp.int32)
            cum = jnp.cumsum(onehot, axis=0) - 1
            loc = jnp.take_along_axis(cum, flat_idx[:, None], axis=1)[:, 0]
            loc = loc.reshape(K, S).T
            keep = loc < C
            gates = top_vals * keep.astype(top_vals.dtype)
            denom = jnp.maximum(gates.sum(-1, keepdims=True), 1e-09)
            gates = gates / denom
            loc_c = jnp.where(keep, loc, C)
            e_flat = top_idx.reshape(-1)
            l_flat = loc_c.reshape(-1)
            xk = jnp.broadcast_to(xf[:, None, :], (S, K, h)).reshape(-1, h)
            xk = jnp.where(keep.reshape(-1, 1), xk, 0.0)
            buf = jnp.zeros((E, C + 1, h), x.dtype).at[e_flat, l_flat].set(xk)
            inp = buf[:, :C]
            hid = jnp.einsum('ech,ehf->ecf', inp, W_in)
            a, g = jnp.split(hid, 2, axis=-1)
            hid = jax.nn.gelu(a, approximate=False) * g
            out_e = jnp.einsum('ecf,efh->ech', hid, W_out)
            out_pad = jnp.concatenate([out_e, jnp.zeros((E, 1, h), out_e.dtype)], axis=1)
            gathered = out_pad[e_flat, l_flat].reshape(S, K, h)
            y = (gathered * gates[..., None]).sum(axis=1)
            return y.reshape(b, t, h)
        key = jax.random.key(seed)
        k1, k2, k3, k4 = jax.random.split(key, 4)
        x = jax.random.normal(k1, (B, T, H), dtype=jnp.float32)
        Wg = jax.random.normal(k2, (H, E), dtype=jnp.float32) * 0.02
        W_in = jax.random.normal(k3, (E, H, 2 * F), dtype=jnp.float32) * (1.0 / math.sqrt(H))
        W_out = jax.random.normal(k4, (E, F, H), dtype=jnp.float32) * (1.0 / math.sqrt(F))
        return {'x': x, 'Wg': Wg, 'W_in': W_in, 'W_out': W_out}
    _L0_ffn_all = _L0_ffn_setup()
    _L0_ffn_in = {k: v for k, v in _L0_ffn_all.items() if k in ('Wg', 'W_in', 'W_out')}
    del _L0_ffn_all

    def _L1_xattn_setup():
        import jax, jax.numpy as jnp
        import numpy as np
        HEADS = 8
        DIM_HEAD = 64
        DIM = 256
        CTX_DIM = 256
        HIDDEN = HEADS * DIM_HEAD
        key = jax.random.key(seed)
        ks = jax.random.split(key, 7)
        b, n, m = (2, 512, 512)
        x = jax.random.normal(ks[0], (b, n, DIM), dtype=jnp.float32)
        context = jax.random.normal(ks[1], (b, m, CTX_DIM), dtype=jnp.float32)
        Wq = jax.random.normal(ks[2], (DIM, HIDDEN), dtype=jnp.float32) * (1.0 / np.sqrt(DIM))
        Wk = jax.random.normal(ks[3], (CTX_DIM, HIDDEN), dtype=jnp.float32) * (1.0 / np.sqrt(CTX_DIM))
        Wv = jax.random.normal(ks[4], (CTX_DIM, HIDDEN), dtype=jnp.float32) * (1.0 / np.sqrt(CTX_DIM))
        Wo = jax.random.normal(ks[5], (HIDDEN, DIM), dtype=jnp.float32) * (1.0 / np.sqrt(HIDDEN))
        bo = jax.random.normal(ks[6], (DIM,), dtype=jnp.float32) * 0.01
        return {'x': x, 'context': context, 'Wq': Wq, 'Wk': Wk, 'Wv': Wv, 'Wo': Wo, 'bo': bo}
    _L1_xattn_all = _L1_xattn_setup()
    _L1_xattn_in = {k: v for k, v in _L1_xattn_all.items() if k in ('Wq', 'Wk', 'Wv', 'Wo', 'bo')}
    del _L1_xattn_all

    def _L1_attn_setup():
        import jax, jax.numpy as jnp
        import numpy as np
        D_MODEL = 256
        N_HEADS = 4
        N_KV_HEADS = 2
        HEAD_DIM = D_MODEL // N_HEADS
        N_REP = N_HEADS // N_KV_HEADS
        EPS_RMS = 1e-06
        EPS_NORM = 1e-12

        def _rmsnorm(x, w):
            var = jnp.mean(jnp.square(x), axis=-1, keepdims=True)
            return x * jax.lax.rsqrt(var + EPS_RMS) * w

        def _l2norm(x):
            n = jnp.sqrt(jnp.sum(jnp.square(x), axis=-1, keepdims=True))
            return x / jnp.maximum(n, EPS_NORM)
        key = jax.random.key(seed)
        ks = jax.random.split(key, 8)
        B, L = (2, 1024)
        s = 0.02
        return {'x': jax.random.normal(ks[0], (B, L, D_MODEL), dtype=jnp.float32), 'norm_w': jnp.ones((D_MODEL,), dtype=jnp.float32), 'Wq': jax.random.normal(ks[1], (D_MODEL, N_HEADS * HEAD_DIM), dtype=jnp.float32) * s, 'Wk': jax.random.normal(ks[2], (D_MODEL, N_KV_HEADS * HEAD_DIM), dtype=jnp.float32) * s, 'Wv': jax.random.normal(ks[3], (D_MODEL, N_KV_HEADS * HEAD_DIM), dtype=jnp.float32) * s, 'Wo': jax.random.normal(ks[4], (N_HEADS * HEAD_DIM, D_MODEL), dtype=jnp.float32) * s, 'gate': jnp.asarray(0.1, dtype=jnp.float32), 'log_temperature': jnp.asarray(np.log(10.0), dtype=jnp.float32)}
    _L1_attn_all = _L1_attn_setup()
    _L1_attn_in = {k: v for k, v in _L1_attn_all.items() if k in ('norm_w', 'Wq', 'Wk', 'Wv', 'Wo', 'gate', 'log_temperature')}
    del _L1_attn_all

    def _L1_ffn_setup():
        import jax, jax.numpy as jnp
        import numpy as np
        EPS = 1e-05

        def rmsnorm(x):
            var = jnp.mean(jnp.square(x), axis=-1, keepdims=True)
            return x * jax.lax.rsqrt(var + 1e-06)

        def activation_quant(x):
            scale = 127.0 / jnp.clip(jnp.max(jnp.abs(x), axis=-1, keepdims=True), EPS, None)
            return jnp.clip(jnp.round(x * scale), -128, 127) / scale

        def weight_quant(w):
            scale = 1.0 / jnp.clip(jnp.mean(jnp.abs(w)), EPS, None)
            return jnp.clip(jnp.round(w * scale), -1, 1) / scale

        def bitlinear(x, w, b):
            xn = rmsnorm(x)
            xq = xn + jax.lax.stop_gradient(activation_quant(xn) - xn)
            wq = w + jax.lax.stop_gradient(weight_quant(w) - w)
            return jnp.einsum('bsi,oi->bso', xq, wq) + b
        key = jax.random.key(seed)
        k1, k2, k3 = jax.random.split(key, 3)
        B, S, D, H = (4, 512, 256, 1024)
        x = jax.random.normal(k1, (B, S, D), dtype=jnp.float32)
        w1 = jax.random.normal(k2, (H, D), dtype=jnp.float32) * D ** (-0.5)
        b1 = jnp.zeros((H,), dtype=jnp.float32)
        w2 = jax.random.normal(k3, (D, H), dtype=jnp.float32) * H ** (-0.5)
        b2 = jnp.zeros((D,), dtype=jnp.float32)
        return {'x': x, 'w1': w1, 'b1': b1, 'w2': w2, 'b2': b2}
    _L1_ffn_all = _L1_ffn_setup()
    _L1_ffn_in = {k: v for k, v in _L1_ffn_all.items() if k in ('w1', 'b1', 'w2', 'b2')}
    del _L1_ffn_all
    return {'x': x, 'ctx_1024': ctx_1024, 'mask_1x1xSxS2_fk1': mask_1x1xSxS2_fk1, 'L0_xattn_wq': _L0_xattn_in['wq'], 'L0_xattn_bq': _L0_xattn_in['bq'], 'L0_xattn_wk': _L0_xattn_in['wk'], 'L0_xattn_bk': _L0_xattn_in['bk'], 'L0_xattn_wv': _L0_xattn_in['wv'], 'L0_xattn_bv': _L0_xattn_in['bv'], 'L0_xattn_wo': _L0_xattn_in['wo'], 'L0_xattn_bo': _L0_xattn_in['bo'], 'L0_attn_Wqk': _L0_attn_in['Wqk'], 'L0_attn_Wv': _L0_attn_in['Wv'], 'L0_attn_Wo': _L0_attn_in['Wo'], 'L0_attn_tau': _L0_attn_in['tau'], 'L0_ffn_Wg': _L0_ffn_in['Wg'], 'L0_ffn_W_in': _L0_ffn_in['W_in'], 'L0_ffn_W_out': _L0_ffn_in['W_out'], 'L1_xattn_Wq': _L1_xattn_in['Wq'], 'L1_xattn_Wk': _L1_xattn_in['Wk'], 'L1_xattn_Wv': _L1_xattn_in['Wv'], 'L1_xattn_Wo': _L1_xattn_in['Wo'], 'L1_xattn_bo': _L1_xattn_in['bo'], 'L1_attn_norm_w': _L1_attn_in['norm_w'], 'L1_attn_Wq': _L1_attn_in['Wq'], 'L1_attn_Wk': _L1_attn_in['Wk'], 'L1_attn_Wv': _L1_attn_in['Wv'], 'L1_attn_Wo': _L1_attn_in['Wo'], 'L1_attn_gate': _L1_attn_in['gate'], 'L1_attn_log_temperature': _L1_attn_in['log_temperature'], 'L1_ffn_w1': _L1_ffn_in['w1'], 'L1_ffn_b1': _L1_ffn_in['b1'], 'L1_ffn_w2': _L1_ffn_in['w2'], 'L1_ffn_b2': _L1_ffn_in['b2']}

def reference(x, ctx_1024, mask_1x1xSxS2_fk1, L0_xattn_wq, L0_xattn_bq, L0_xattn_wk, L0_xattn_bk, L0_xattn_wv, L0_xattn_bv, L0_xattn_wo, L0_xattn_bo, L0_attn_Wqk, L0_attn_Wv, L0_attn_Wo, L0_attn_tau, L0_ffn_Wg, L0_ffn_W_in, L0_ffn_W_out, L1_xattn_Wq, L1_xattn_Wk, L1_xattn_Wv, L1_xattn_Wo, L1_xattn_bo, L1_attn_norm_w, L1_attn_Wq, L1_attn_Wk, L1_attn_Wv, L1_attn_Wo, L1_attn_gate, L1_attn_log_temperature, L1_ffn_w1, L1_ffn_b1, L1_ffn_w2, L1_ffn_b2):
    import jax
    import jax.numpy as jnp

    def _L0_xattn_ref(q, k, v, mask, wq, bq, wk, bk, wv, bv, wo, bo):
        import jax, jax.numpy as jnp
        import numpy as np
        D_MODEL = 256
        NUM_HEADS = 16
        DEPTH = D_MODEL // NUM_HEADS
        B, S = (4, 512)

        def _split_heads(x):
            b, s, _ = x.shape
            return x.reshape(b, s, NUM_HEADS, DEPTH).transpose(0, 2, 1, 3)
        qh = _split_heads(q @ wq + bq)
        kh = _split_heads(k @ wk + bk)
        vh = _split_heads(v @ wv + bv)
        inv_sqrt_dk = 1.0 / jnp.sqrt(jnp.asarray(DEPTH, jnp.float32))
        logits = jnp.einsum('bhqd,bhkd->bhqk', qh, kh) * inv_sqrt_dk
        logits = logits + mask * -1000000000.0
        attn = jax.nn.softmax(logits, axis=-1)
        out = jnp.einsum('bhqk,bhkd->bhqd', attn, vh)
        out = out.transpose(0, 2, 1, 3).reshape(q.shape[0], -1, D_MODEL)
        return out @ wo + bo

    def _L0_attn_ref(x, Wqk, Wv, Wo, tau):
        import jax, jax.numpy as jnp
        import numpy as np
        import math
        B, N, D, H = (8, 1024, 256, 16)
        DH = D // H
        Bb, Nn, Dd = x.shape
        qk = x @ Wqk
        v = x @ Wv
        qk = jnp.transpose(qk, (0, 2, 1)).reshape(Bb, H, DH, Nn)
        v = jnp.transpose(v, (0, 2, 1)).reshape(Bb, H, DH, Nn)
        dot = jnp.einsum('bhdn,bhen->bhde', qk, qk)
        q2 = jnp.sum(qk * qk, axis=-1)
        logits = 2.0 * dot - q2[..., :, None] - q2[..., None, :]
        logits = logits / jnp.sqrt(jnp.asarray(Nn, dtype=x.dtype))
        logits = logits * tau
        attn = jax.nn.softmax(logits, axis=-1)
        w = jnp.einsum('bhde,bhen->bhdn', attn, v)
        out = jnp.transpose(w.reshape(Bb, Dd, Nn), (0, 2, 1))
        return out @ Wo

    def _L0_ffn_ref(x, Wg, W_in, W_out):
        import math
        import jax, jax.numpy as jnp
        import numpy as np
        B, T, H = (4, 512, 256)
        E, K, F = (8, 2, 512)
        CAP_FACTOR = 1.25

        def _moe_forward(x, Wg, W_in, W_out):
            b, t, h = x.shape
            xf = x.reshape(-1, h)
            S = xf.shape[0]
            C = int(math.ceil(K * S / E * CAP_FACTOR))
            logits = xf @ Wg
            probs = jax.nn.softmax(logits, axis=-1)
            top_vals, top_idx = jax.lax.top_k(probs, K)
            flat_idx = top_idx.T.reshape(-1)
            onehot = jax.nn.one_hot(flat_idx, E, dtype=jnp.int32)
            cum = jnp.cumsum(onehot, axis=0) - 1
            loc = jnp.take_along_axis(cum, flat_idx[:, None], axis=1)[:, 0]
            loc = loc.reshape(K, S).T
            keep = loc < C
            gates = top_vals * keep.astype(top_vals.dtype)
            denom = jnp.maximum(gates.sum(-1, keepdims=True), 1e-09)
            gates = gates / denom
            loc_c = jnp.where(keep, loc, C)
            e_flat = top_idx.reshape(-1)
            l_flat = loc_c.reshape(-1)
            xk = jnp.broadcast_to(xf[:, None, :], (S, K, h)).reshape(-1, h)
            xk = jnp.where(keep.reshape(-1, 1), xk, 0.0)
            buf = jnp.zeros((E, C + 1, h), x.dtype).at[e_flat, l_flat].set(xk)
            inp = buf[:, :C]
            hid = jnp.einsum('ech,ehf->ecf', inp, W_in)
            a, g = jnp.split(hid, 2, axis=-1)
            hid = jax.nn.gelu(a, approximate=False) * g
            out_e = jnp.einsum('ecf,efh->ech', hid, W_out)
            out_pad = jnp.concatenate([out_e, jnp.zeros((E, 1, h), out_e.dtype)], axis=1)
            gathered = out_pad[e_flat, l_flat].reshape(S, K, h)
            y = (gathered * gates[..., None]).sum(axis=1)
            return y.reshape(b, t, h)
        return _moe_forward(x, Wg, W_in, W_out)

    def _L1_xattn_ref(x, context, Wq, Wk, Wv, Wo, bo):
        import jax, jax.numpy as jnp
        import numpy as np
        HEADS = 8
        DIM_HEAD = 64
        DIM = 256
        CTX_DIM = 256
        HIDDEN = HEADS * DIM_HEAD
        b, n, _ = x.shape
        m = context.shape[1]
        scale = DIM_HEAD ** (-0.5)
        q = (x @ Wq).reshape(b, n, HEADS, DIM_HEAD).transpose(0, 2, 1, 3)
        k = (context @ Wk).reshape(b, m, HEADS, DIM_HEAD).transpose(0, 2, 1, 3)
        v = (context @ Wv).reshape(b, m, HEADS, DIM_HEAD).transpose(0, 2, 1, 3)
        scores = jnp.einsum('bhnd,bhmd->bhnm', q, k) * scale
        attn = jax.nn.softmax(scores, axis=-1)
        out = jnp.einsum('bhnm,bhmd->bhnd', attn, v)
        out = out.transpose(0, 2, 1, 3).reshape(b, n, HIDDEN)
        return out @ Wo + bo

    def _L1_attn_ref(x, norm_w, Wq, Wk, Wv, Wo, gate, log_temperature):
        import jax, jax.numpy as jnp
        import numpy as np
        D_MODEL = 256
        N_HEADS = 4
        N_KV_HEADS = 2
        HEAD_DIM = D_MODEL // N_HEADS
        N_REP = N_HEADS // N_KV_HEADS
        EPS_RMS = 1e-06
        EPS_NORM = 1e-12

        def _rmsnorm(x, w):
            var = jnp.mean(jnp.square(x), axis=-1, keepdims=True)
            return x * jax.lax.rsqrt(var + EPS_RMS) * w

        def _l2norm(x):
            n = jnp.sqrt(jnp.sum(jnp.square(x), axis=-1, keepdims=True))
            return x / jnp.maximum(n, EPS_NORM)
        B, L, D = x.shape
        h = _rmsnorm(x, norm_w)
        q = (h @ Wq).reshape(B, L, N_HEADS, HEAD_DIM).transpose(0, 2, 1, 3)
        k = (h @ Wk).reshape(B, L, N_KV_HEADS, HEAD_DIM).transpose(0, 2, 1, 3)
        v = (h @ Wv).reshape(B, L, N_KV_HEADS, HEAD_DIM).transpose(0, 2, 1, 3)
        if N_REP > 1:
            k = jnp.repeat(k, N_REP, axis=1)
            v = jnp.repeat(v, N_REP, axis=1)
        q = _l2norm(q)
        k = _l2norm(k)
        scale = jnp.exp(log_temperature)
        attn = jnp.einsum('bhqd,bhkd->bhqk', q, k) * scale
        causal = jnp.tril(jnp.ones((L, L), dtype=bool))
        attn = jnp.where(causal, attn, -jnp.inf)
        attn = jax.nn.softmax(attn, axis=-1)
        out = jnp.einsum('bhqk,bhkd->bhqd', attn, v).transpose(0, 2, 1, 3).reshape(B, L, D)
        out = out @ Wo
        return x + gate * out

    def _L1_ffn_ref(x, w1, b1, w2, b2):
        import jax, jax.numpy as jnp
        import numpy as np
        EPS = 1e-05

        def rmsnorm(x):
            var = jnp.mean(jnp.square(x), axis=-1, keepdims=True)
            return x * jax.lax.rsqrt(var + 1e-06)

        def activation_quant(x):
            scale = 127.0 / jnp.clip(jnp.max(jnp.abs(x), axis=-1, keepdims=True), EPS, None)
            return jnp.clip(jnp.round(x * scale), -128, 127) / scale

        def weight_quant(w):
            scale = 1.0 / jnp.clip(jnp.mean(jnp.abs(w)), EPS, None)
            return jnp.clip(jnp.round(w * scale), -1, 1) / scale

        def bitlinear(x, w, b):
            xn = rmsnorm(x)
            xq = xn + jax.lax.stop_gradient(activation_quant(xn) - xn)
            wq = w + jax.lax.stop_gradient(weight_quant(w) - w)
            return jnp.einsum('bsi,oi->bso', xq, wq) + b
        h = bitlinear(x, w1, b1)
        h = jax.nn.gelu(h, approximate=False)
        return bitlinear(h, w2, b2)
    x = x + _L0_xattn_ref(_layernorm(x, axis=-1), ctx_1024, ctx_1024, mask_1x1xSxS2_fk1, L0_xattn_wq, L0_xattn_bq, L0_xattn_wk, L0_xattn_bk, L0_xattn_wv, L0_xattn_bv, L0_xattn_wo, L0_xattn_bo)
    x = x + _L0_attn_ref(_layernorm(x, axis=-1), L0_attn_Wqk, L0_attn_Wv, L0_attn_Wo, L0_attn_tau)
    x = x + _L0_ffn_ref(_layernorm(x, axis=-1), L0_ffn_Wg, L0_ffn_W_in, L0_ffn_W_out)
    x = x + _L1_xattn_ref(_layernorm(x, axis=-1), ctx_1024, L1_xattn_Wq, L1_xattn_Wk, L1_xattn_Wv, L1_xattn_Wo, L1_xattn_bo)
    x = x + _L1_attn_ref(_layernorm(x, axis=-1), L1_attn_norm_w, L1_attn_Wq, L1_attn_Wk, L1_attn_Wv, L1_attn_Wo, L1_attn_gate, L1_attn_log_temperature)
    x = x + _L1_ffn_ref(_layernorm(x, axis=-1), L1_ffn_w1, L1_ffn_b1, L1_ffn_w2, L1_ffn_b2)
    return x

_drawn_inputs = setup_inputs


def setup_inputs(seed=0):
    import zlib

    import numpy as np

    out = dict(_drawn_inputs(seed))
    spreads = {'L0_xattn_bq': (0.0, 0.1),
     'L0_xattn_bk': (0.0, 0.8),
     'L0_xattn_bv': (0.0, 0.1),
     'L0_xattn_bo': (0.0, 0.1),
     'L0_attn_tau': (1.0, 0.6),
     'L1_attn_norm_w': (1.0, 0.6),
     'L1_ffn_b1': (0.0, 0.1),
     'L1_ffn_b2': (0.0, 0.1)}
    factors = {'L0_attn_Wqk': 8.0,
     'L1_xattn_bo': 7.438,
     'L1_attn_Wq': 8.0,
     'L1_attn_Wk': 8.0,
     'L1_attn_Wv': 8.0,
     'L1_attn_Wo': 8.0}
    for name, (base, spread) in spreads.items():
        noise = np.random.default_rng([zlib.crc32(name.encode()), seed]).standard_normal(out[name].shape)
        drawn = base * np.exp(spread * noise) if base else spread * noise
        out[name] = jnp.asarray(drawn.astype(out[name].dtype))
    for name, factor in factors.items():
        out[name] = (out[name] * factor).astype(out[name].dtype)
    return out
```

```python
from contextlib import ExitStack, contextmanager

import concourse.bass as bass
from concourse import mybir

F32 = mybir.dt.float32
BF16 = mybir.dt.bfloat16
U32 = mybir.dt.uint32
ALU = mybir.AluOpType
ACT = mybir.ActivationFunctionType
AX = mybir.AxisListType

P = 128
D = 256
KT = D // P
B = 4
S = 256
QT = S // P
N = B * S
NT = N // P
S2 = 4096
CH = 512
TPC = CH // P
PAIRS = S2 // CH // 2
UNITS = 16
NEG = -1.0e30
LOWEST = -3.0e38
MAGIC = 12582912.0


class Ctx:

    def __init__(self, nc):
        self.nc = nc
        self.stack = None
        self.held = []

    def sem(self, name):
        self.held.append(self.stack.enter_context(self.nc.semaphore(name)))
        return self.held[-1]

    @contextmanager
    def stage(self):
        with ExitStack() as self.stack:
            yield
            with self.nc.Block() as block:
                @block.gpsimd
                def _(pool):
                    for held in self.held:
                        pool.sem_clear(held)
            self.held = []


def constants(c, ident, identb, ones, x_in, x_rows, tag):
    nc = c.nc
    cleared, made, copied = c.sem(tag + "cleared"), c.sem(tag + "made"), c.sem(tag + "copied")
    with nc.Block() as block:
        @block.gpsimd
        def _(pool):
            pool.memset(ident[:], 0.0).then_inc(cleared, 1)
            pool.memset(ones[:], 1.0).then_inc(cleared, 1)
            pool.wait_ge(cleared, 2)
            pool.affine_select(out=ident[:], in_=ident[:], compare_op=ALU.not_equal, fill=1.0, base=0,
                               pattern=[[-1, P]], channel_multiplier=1).then_inc(made, 1)
            pool.wait_ge(made, 1)
            pool.tensor_copy(identb[:], ident[:]).then_inc(made, 1)

        @block.sync
        def _(sp):
            sp.dma_start(x_rows.ap(), x_in.rearrange("b s d -> (b s) d")).then_inc(copied, 16)
            sp.wait_ge(copied, 16)


def layer_norm(c, x_rows, xn, xnT, ident, tag):
    nc = c.nc
    x_loaded, stats, root, normed = (c.sem(tag + n) for n in ("x_loaded", "stats", "root", "normed"))
    turned, kept = c.sem(tag + "turned"), c.sem(tag + "kept")
    with ExitStack() as s:
        x = s.enter_context(nc.sbuf_tensor(tag + "x", [P, NT, D], F32))
        st = s.enter_context(nc.sbuf_tensor(tag + "st", [P, NT, 6], F32))
        mv = s.enter_context(nc.sbuf_tensor(tag + "mv", [P, NT, 2], F32))
        var = s.enter_context(nc.sbuf_tensor(tag + "var", [P, NT], F32))
        std = s.enter_context(nc.sbuf_tensor(tag + "std", [P, NT], F32))
        r = s.enter_context(nc.sbuf_tensor(tag + "r", [P, 5, NT], F32))
        ps = [s.enter_context(nc.psum_tensor(f"{tag}ps{i}", [P, 512], F32)) for i in range(8)]
        block = s.enter_context(nc.Block())

        @block.sync
        def _(sp):
            sp.dma_start(x[:], x_rows.ap().rearrange("(t p) d -> p t d", p=P)).then_inc(x_loaded, 16)

        @block.vector
        def _(dve):
            dve.wait_ge(x_loaded, 16)
            for t in range(NT):
                dve.bn_stats(st[:, t, :], x[:, t, :]).then_inc(stats, 1)
            dve.wait_ge(stats, NT)
            for t in range(NT):
                dve.bn_aggr(mv[:, t, :], st[:, t, :]).then_inc(stats, 1)
            dve.wait_ge(stats, 2 * NT)
            dve.tensor_scalar(var[:], mv[:, :, 1], 1e-5, None, ALU.add).then_inc(stats, 1)
            dve.wait_ge(root, 1)
            dve.reciprocal(r[:, 0, :], std[:]).then_inc(stats, 1)
            dve.wait_ge(stats, 2 * NT + 2)
            dve.tensor_tensor(r[:, 1, :], r[:, 0, :], r[:, 0, :], ALU.mult).then_inc(stats, 1)
            dve.wait_ge(stats, 2 * NT + 3)
            dve.tensor_tensor(r[:, 2, :], r[:, 1, :], var[:], ALU.mult).then_inc(stats, 1)
            dve.wait_ge(stats, 2 * NT + 4)
            dve.tensor_scalar(r[:, 3, :], r[:, 2, :], -0.5, 1.5, ALU.mult, ALU.add).then_inc(stats, 1)
            dve.wait_ge(stats, 2 * NT + 5)
            dve.tensor_tensor(r[:, 4, :], r[:, 3, :], r[:, 0, :], ALU.mult).then_inc(stats, 1)
            dve.wait_ge(stats, 2 * NT + 6)
            for t in range(NT):
                dve.tensor_scalar(xn[:, t, :], x[:, t, :], mv[:, t, 0:1], r[:, 4, t:t + 1],
                                  ALU.subtract, ALU.mult).then_inc(normed, 1)

        @block.tensor
        def _(pe):
            for t in range(NT):
                pe.wait_ge(normed, t + 1)
                for k in range(KT):
                    mm = pe.transpose(ps[t][:, k * P:(k + 1) * P], xn[:, t, k * P:(k + 1) * P], ident[:])
                mm.then_inc(turned, 1)

        @block.scalar
        def _(act):
            act.wait_ge(stats, 2 * NT + 1)
            act.activation(std[:], var[:], ACT.Sqrt).then_inc(root, 1)
            for t in range(NT):
                act.wait_ge(turned, t + 1)
                act.activation(xnT[:, :, t * P:(t + 1) * P],
                               ps[t][:, 0:D].rearrange("p (k n) -> p k n", k=KT), ACT.Copy).then_inc(kept, 1)
            act.wait_ge(kept, NT)


def split_queries(c, xnT, w_q, b_q, scale, HD, qs, tag):
    nc = c.nc
    G = HD // P
    w_loaded, q_ready, q_cut, q_left, q_stored = (c.sem(tag + n) for n in
                                                  ("w_loaded", "q_ready", "q_cut", "q_left", "q_stored"))
    with ExitStack() as s:
        w = s.enter_context(nc.sbuf_tensor(tag + "w", [P, KT, HD], F32))
        bias = s.enter_context(nc.sbuf_tensor(tag + "bias", [P, G], F32))
        q = s.enter_context(nc.sbuf_tensor(tag + "q", [P, G, N], F32))
        rest = s.enter_context(nc.sbuf_tensor(tag + "rest", [P, G, N], F32))
        parts = s.enter_context(nc.sbuf_tensor(tag + "parts", [P, 3, G, N], BF16))
        ps = [s.enter_context(nc.psum_tensor(f"{tag}ps{i}", [P, 512], F32)) for i in range(8)]
        block = s.enter_context(nc.Block())
        loads = 32 if b_q is not None else 16
        halves = N // 512

        @block.sync
        def _(sp):
            sp.dma_start(w[:], w_q.rearrange("(k p) n -> p k n", p=P)).then_inc(w_loaded, 16)
            if b_q is not None:
                sp.dma_start(bias[:], b_q.rearrange("(g p) -> p g", p=P),
                             allow_slow_non_contiguous=True).then_inc(w_loaded, 16)
            for i, part_of in enumerate((1, 3, 4)):
                sp.wait_ge(q_cut, part_of * G)
                sp.dma_start(qs.ap()[i].rearrange("(g p) n -> p g n", p=P), parts[:, i]).then_inc(q_stored, 16)
            sp.wait_ge(q_stored, 48)

        @block.tensor
        def _(pe):
            pe.wait_ge(w_loaded, loads)
            for g in range(G):
                for half in range(halves):
                    for k in range(KT):
                        mm = pe.matmul(ps[(g * halves + half) % 8][:], w[:, k, g * P:(g + 1) * P],
                                       xnT[:, k, half * 512:(half + 1) * 512], start=k == 0, stop=k == KT - 1)
                    mm.then_inc(q_ready, 1)

        @block.scalar
        def _(act):
            act.wait_ge(w_loaded, loads)
            for g in range(G):
                for half in range(halves):
                    act.wait_ge(q_ready, g * halves + half + 1)
                    act.activation(q[:, g, half * 512:(half + 1) * 512], ps[(g * halves + half) % 8][:],
                                   ACT.Identity, bias=bias[:, g:g + 1] if b_q is not None else 0.0).then_inc(q_left, 1)

        @block.vector
        def _(dve):
            dve.wait_ge(q_left, G * halves)
            for g in range(G):
                dve.tensor_scalar(parts[:, 0, g, :], q[:, g, :], scale, None, ALU.mult).then_inc(q_cut, 1)
            dve.wait_ge(q_cut, G)
            for g in range(G):
                dve.scalar_tensor_tensor(rest[:, g, :], q[:, g, :], scale, parts[:, 0, g, :],
                                         ALU.mult, ALU.subtract).then_inc(q_cut, 1)
            dve.wait_ge(q_cut, 2 * G)
            for g in range(G):
                dve.tensor_copy(parts[:, 1, g, :], rest[:, g, :]).then_inc(q_cut, 1)
            dve.wait_ge(q_cut, 3 * G)
            for g in range(G):
                dve.tensor_tensor(parts[:, 2, g, :], rest[:, g, :], parts[:, 1, g, :],
                                  ALU.subtract).then_inc(q_cut, 1)


def scale_mask(c, mask, bias_qk, bias_kq, ident, tag):
    nc = c.nc
    loaded, scaled, turned, kept, stored = (c.sem(tag + n) for n in ("loaded", "scaled", "turned", "kept", "stored"))
    KEYS = S2 // P
    with ExitStack() as s:
        m = s.enter_context(nc.sbuf_tensor(tag + "m", [P, QT, S2], F32))
        mT = s.enter_context(nc.sbuf_tensor(tag + "mT", [P, KEYS, S], F32))
        ps = [s.enter_context(nc.psum_tensor(f"{tag}ps{i}", [P, 512], F32)) for i in range(8)]
        block = s.enter_context(nc.Block())

        @block.sync
        def _(sp):
            for i in range(QT):
                sp.dma_start(m[:, i], mask[0, 0].rearrange("(i p) k -> p i k", p=P)[:, i]).then_inc(loaded, 16)
            sp.wait_ge(scaled, QT)
            sp.dma_start(bias_qk.ap().rearrange("(i p) k -> p i k", p=P), m[:]).then_inc(stored, 16)
            sp.wait_ge(kept, KEYS // 2)
            sp.dma_start(bias_kq.ap().rearrange("(t p) q -> p t q", p=P), mT[:]).then_inc(stored, 16)
            sp.wait_ge(stored, 32)

        @block.vector
        def _(dve):
            dve.wait_ge(loaded, 16 * QT)
            for i in range(QT):
                dve.tensor_scalar(m[:, i], m[:, i], -1.0e9, None, ALU.mult).then_inc(scaled, 1)

        @block.tensor
        def _(pe):
            pe.wait_ge(scaled, QT)
            for t in range(KEYS):
                if t % 2 == 0 and t >= 16:
                    pe.wait_ge(kept, t // 2 - 7)
                for i in range(QT):
                    at = (t % 2) * S + i * P
                    mm = pe.transpose(ps[t // 2 % 8][:, at:at + P], m[:, i, t * P:(t + 1) * P], ident[:])
                mm.then_inc(turned, 1)

        @block.scalar
        def _(act):
            for t in range(0, KEYS, 2):
                act.wait_ge(turned, t + 2)
                act.activation(mT[:, t:t + 2, :], ps[t // 2 % 8][:].rearrange("p (t q) -> p t q", t=2),
                               ACT.Copy).then_inc(kept, 1)


def cross_attention(c, H, ctx, w_k, b_k, w_v, qs, v_rows, o_rows, sum_rows, bias_qk, bias_kq, ident, ones, tag):
    nc = c.nc
    masked = bias_qk is not None
    small = H == 16
    dh = 16 if small else 64
    HD = H * dh
    G = HD // P
    VW = dh + 1 if small else dh
    HV = H * VW
    VU = G
    TPV = TPC // VU
    UM = H * QT
    SETS = H * TPC // 4
    HS = 4 if small else 2
    TS = 4 // HS
    CHUNKS = 2 * PAIRS
    SLOT_K, SLOT_Q = (0, 0, 1, 1, 0, 2), (0, 1, 0, 1, 2, 0)
    KQ = 6 * dh if small else P
    NPARTS = 3 if small else 2
    ND = 48 if small else 4
    NDQ = 6 if small else 8
    NDO = 1 if small else 2
    ONE, M0, S0 = 16, 2 * UM, 2 * SETS

    def sem(n):
        return c.sem(tag + n)

    w_loaded, ones_set, ones_put = sem("w_loaded"), sem("ones_set"), sem("ones_put")
    ctx_in, q_in, max_in, o_out = sem("ctx_in"), sem("q_in"), sem("max_in"), sem("o_out")
    bias_in, keys_in, v_out, v_in, biasT_in = ([sem(f"{n}{u}") for u in range(2)] for n in
                                               ("bias_in", "keys_in", "v_out", "v_in", "biasT_in"))
    ctx_turned, ctxT_kept = sem("ctx_turned"), sem("ctxT_kept")
    k_made, k_kept, k_half, k_rest, k_cut2, k_cut3 = (sem(n) for n in
                                                      ("k_made", "k_kept", "k_half", "k_rest", "k_cut2", "k_cut3"))
    v_made, v_kept = sem("v_made"), sem("v_kept")
    scored, reduced, folded, best_reset = sem("scored"), sem("reduced"), sem("folded"), sem("best_reset")
    negated, max_turned, max_cut = sem("negated"), sem("max_turned"), sem("max_cut")
    out_reset, set_scored, biased, probs, used = (sem(n) for n in ("out_reset", "set_scored", "biased", "probs", "used"))
    summed, sums_made, o_kept = sem("summed"), sem("sums_made"), sem("o_kept")

    LOADS = 32 if b_k is None else 48

    settled = {n: sem("settled_" + n) for n in ("sp", "dve", "pe")}

    def settle(eng, n):
        eng.sem_inc(settled[n], 1)

    with ExitStack() as s:
        def sb(n, shape, dt=F32):
            return s.enter_context(nc.sbuf_tensor(tag + n, shape, dt))

        keys = sb("keys", [P, PAIRS, 2 * UNITS, CH], BF16)
        query = sb("query", [P, H if small else 3 * H, S], BF16)
        ctx_sb = sb("ctx_sb", [P, TPC, D])
        ctxT = sb("ctxT", [P, KT, CH])
        work = sb("work", [P, 4096])
        value = [sb(f"value{u}", [P, TPC, HV]) for u in range(2)]
        v_stage = [sb(f"v_stage{u}", [P, TPV, H, VW]) for u in range(2)]
        wk, wv = sb("wk", [P, KT, HD]), sb("wv", [P, KT, HD])
        bk = sb("bk", [P, G])
        best, best_c, neg = sb("best", [P, UM]), sb("best_c", [P, UM]), sb("neg", [P, UM])
        neg_rest, neg_parts = sb("neg_rest", [UM, P]), sb("neg_parts", [UM, 3, P], BF16)
        if masked:
            bias = [sb(f"bias{u}", [P, QT, CH]) for u in range(2)]
            biasT = [sb(f"biasT{u}", [P, TPC, S]) for u in range(2)]
            junk = [sb(f"junk{u}", [P, CH], BF16) for u in range(2)]
        if not small:
            shift, onesb = sb("shift", [P, H, S], BF16), sb("onesb", [P, P], BF16)
            acc = sb("acc", [P, H, S])
        kf = [work[:, g * CH:(g + 1) * CH] for g in range(2)]
        rest = [work[:, (2 + g) * CH:(3 + g) * CH] for g in range(2)]
        kparts = work[:, 2048:4096].bitcast(BF16)[:, 0:NPARTS * G * CH].rearrange("p (i g n) -> p i g n", i=NPARTS, g=G)
        slot = [work[:, i * 1024:(i + 1) * 1024] for i in range(4)]
        bank = [s.enter_context(nc.psum_tensor(f"{tag}bank{i}", [P, 512], F32)) for i in range(4)]
        duo = [s.enter_context(nc.psum_tensor(f"{tag}duo{i}", [P, 1024], F32)) for i in range(2)]
        quad = [duo[i // 2][:, i % 2 * 512:i % 2 * 512 + 512] for i in range(4)]
        block = s.enter_context(nc.Block())

        @block.sync
        def _(sp):
            sp.dma_start(wk[:], w_k.rearrange("(k p) n -> p k n", p=P)).then_inc(w_loaded, 16)
            sp.dma_start(wv[:], w_v.rearrange("(k p) n -> p k n", p=P)).then_inc(w_loaded, 16)
            if b_k is not None:
                sp.dma_start(bk[:], b_k.rearrange("(g p) -> p g", p=P),
                             allow_slow_non_contiguous=True).then_inc(w_loaded, 16)
            sp.sem_inc(keys_in[1], ONE)
            sp.sem_inc(v_out[0], ONE)
            sp.sem_inc(v_out[1], ONE)
            if small:
                sp.wait_ge(ones_set, 1)
                for p in range(PAIRS):
                    for u in range(4):
                        sp.dma_start(keys[KQ:KQ + 3, p, u * 8:(u + 1) * 8, :],
                                     work[KQ:KQ + 3, 0:2048].bitcast(BF16).rearrange("p (a n) -> p a n", a=8)
                                     ).then_inc(ones_put, 16)
            with sp.Fori(0, B) as b:
                sp.wait_ge(o_kept, b + ONE)
                mine = bass.ds(b * S, S)
                if small:
                    for i, part in enumerate(SLOT_Q):
                        sp.dma_start(query[i * dh:(i + 1) * dh, :, :],
                                     qs.ap()[part, :, mine].rearrange("(h d) q -> d h q", d=dh)).then_inc(q_in, 16)
                else:
                    for part in range(2):
                        for lo in (0, dh):
                            sp.dma_start(query[lo:lo + dh, part * H:(part + 1) * H, :],
                                         qs.ap()[part, :, mine].rearrange("(h d) q -> d h q", d=dh)).then_inc(q_in, 16)
                    for odd in range(2):
                        for top, part in ((0, 0 if odd else 2), (dh, 2 if odd else 0)):
                            sp.dma_start(query[top:top + dh, 2 * H + odd:3 * H:2, :],
                                         qs.ap()[part, :, mine].rearrange("(h o d) q -> o d h q", d=dh, o=2)[odd]
                                         ).then_inc(q_in, 16)
                with sp.Fori(0, PAIRS) as p:
                    n = b * CHUNKS + p * 2
                    for u in range(2):
                        sp.wait_ge(ctx_turned, n + u + ONE)
                        sp.dma_start(ctx_sb[:], ctx[bass.ds(b, 1), bass.ds(p * 2 * CH + u * CH, CH), :]
                                     .rearrange("b (t k) c -> k (b t) c", k=P)).then_inc(ctx_in, 16)
                        if masked:
                            sp.wait_ge(reduced, n * UM + (u * UM - UM + M0))
                            settle(sp, "sp")
                            sp.dma_start(bias[u][:], bias_qk.ap()[:, bass.ds(p * 2 * CH + u * CH, CH)]
                                         .rearrange("(i q) k -> q i k", q=P)).then_inc(bias_in[u], 16)
                    for u in range(2):
                        sp.wait_ge(k_cut2, n * G + (u + 1) * G)
                        sp.wait_ge(k_cut3, n * G + (u + 1) * G)
                        if small:
                            for i, part in enumerate(SLOT_K):
                                for h in range(8):
                                    sp.dma_start(keys[i * dh:(i + 1) * dh, bass.ds(p, 1), u * UNITS + h:(u + 1) * UNITS:8, :]
                                                 .rearrange("d p h n -> d (p h) n"),
                                                 kparts[h * dh:(h + 1) * dh, part]).then_inc(keys_in[u], 16)
                        else:
                            for part in range(2):
                                for odd in range(2):
                                    to, at = dh * (1 - odd), u * UNITS + 2 * odd + part
                                    sp.dma_start(keys[to:to + dh, bass.ds(p, 1), at:(u + 1) * UNITS:4, :]
                                                 .rearrange("d p h n -> d (p h) n"),
                                                 kparts[dh * odd:dh * odd + dh, part]).then_inc(keys_in[u], 16)
                        for v in range(VU):
                            sp.wait_ge(v_kept, n * VU + (u * VU + v + 1 + ONE))
                            rows = bass.ds(b * S2 + p * 2 * CH + (u * CH + v * TPV * P), TPV * P)
                            sp.dma_start(v_rows.ap()[rows, :].rearrange("(t k) c -> k t c", k=P),
                                         v_stage[v % 2][:].rearrange("p t h w -> p t (h w)")).then_inc(v_out[v % 2], 16)
                sp.wait_ge(max_cut, b * 4 + 4)
                for i in range(3):
                    row = query[KQ + i:KQ + i + 1] if small else shift[i:i + 1]
                    sp.dma_start(row.rearrange("o h (i q) -> o (h i) q", i=QT), neg_parts[:, i, :]).then_inc(max_in, 16)
                for i in range(2):
                    sp.wait_ge(v_out[i], b * (CHUNKS * VU * 8) + (CHUNKS * VU * 8 + ONE))
                settle(sp, "sp")
                with sp.Fori(0, PAIRS) as p:
                    n = b * CHUNKS + p * 2
                    for u in range(2):
                        sp.wait_ge(used, n * SETS + (u * SETS - SETS + S0))
                        rows = bass.ds(b * S2 + p * 2 * CH + u * CH, CH)
                        sp.dma_start(value[u][:], v_rows.ap()[rows, :].rearrange("(t k) c -> k t c", k=P)).then_inc(v_in[u], 16)
                        if masked:
                            sp.dma_start(biasT[u][:], bias_kq.ap()[bass.ds(p * 2 * CH + u * CH, CH), :]
                                         .rearrange("(t k) q -> k t q", k=P)).then_inc(biasT_in[u], 16)
                sp.wait_ge(o_kept, b + 1 + ONE)
                sp.dma_start(o_rows.ap()[bass.ds(b, 1)].rearrange("b p n -> (b p) n"), slot[0]).then_inc(o_out, 16)
                if not small:
                    sp.dma_start(sum_rows.ap()[bass.ds(b, 1)].rearrange("b p n -> (b p) n"), slot[1]).then_inc(o_out, 16)
            sp.wait_ge(o_out, B * NDO * 16)

        @block.gpsimd
        def _(pool):
            if small:
                pool.memset(work[96:128, 0:2048].bitcast(BF16), 1.0).then_inc(ones_set, 1)
                for u in range(2):
                    pool.wait_ge(ones_set, u + 1)
                    pool.memset(v_stage[u][:], 1.0).then_inc(ones_set, 1)
            else:
                pool.memset(onesb[:], 1.0).then_inc(ones_set, 1)
                pool.wait_ge(ones_set, 1)
                pool.memset(shift[:], 0.0).then_inc(ones_set, 1)
            pool.sem_inc(k_rest, ONE)
            with pool.Fori(0, B) as b:
                with pool.Fori(0, PAIRS) as p:
                    for u in range(2):
                        m = (b * CHUNKS + p * 2) * G + u * G

                        def third_part(g):
                            pool.wait_ge(k_cut2, m + (g + 1))
                            if not small:
                                pool.wait_ge(k_rest, m + (g + 2 + ONE if g < G - 1 else G + ONE))
                            pool.tensor_tensor(kparts[:, NPARTS - 1, g], rest[g % 2], kparts[:, NPARTS - 2, g],
                                               ALU.subtract).then_inc(k_cut3, 1)

                        for g in range(G):
                            pool.wait_ge(k_kept, m + (g + 1))
                            if small:
                                pool.tensor_tensor(rest[g % 2], kf[g % 2], kparts[:, 0, g], ALU.subtract).then_inc(k_rest, 1)
                            else:
                                even, odd = slice(0, dh), slice(dh, P)
                                if g >= 2:
                                    pool.wait_ge(k_cut3, m + (g - 1))
                                pool.tensor_tensor(rest[g % 2][even], kf[g % 2][even],
                                                   keys[even, bass.ds(p, 1), u * UNITS + 4 * g, :].rearrange("d p n -> d (p n)"),
                                                   ALU.subtract).then_inc(k_half, 1)
                                pool.wait_ge(k_half, m + (g + 1))
                                pool.tensor_tensor(rest[g % 2][odd], kf[g % 2][odd],
                                                   keys[odd, bass.ds(p, 1), u * UNITS + 4 * g + 2, :].rearrange("d p n -> d (p n)"),
                                                   ALU.subtract).then_inc(k_rest, 1)
                            if g >= 1:
                                third_part(g - 1)
                        third_part(G - 1)
                        if not small:
                            pool.wait_ge(k_cut3, m + G)

        @block.scalar
        def _(act):
            act.sem_inc(v_kept, ONE)
            act.sem_inc(o_kept, ONE)
            if not masked:
                act.sem_inc(probs, S0)
            act.wait_ge(w_loaded, LOADS)
            act.wait_ge(ones_set, 3 if small else 2)
            if small:
                act.wait_ge(ones_put, PAIRS * 4 * 16)
            with act.Fori(0, B) as b:
                with act.Fori(0, PAIRS) as p:
                    for u in range(2):
                        n = b * CHUNKS + p * 2

                        def second_part(g):
                            act.wait_ge(k_rest, n * G + (u * G + g + 1 + ONE))
                            act.activation(kparts[:, NPARTS - 2, g], rest[g % 2], ACT.Copy).then_inc(k_cut2, 1)

                        act.wait_ge(ctx_turned, n + (u + 1 + ONE))
                        for k in range(KT):
                            ins = act.activation(ctxT[:, k, :], bank[k][:], ACT.Copy)
                        ins.then_inc(ctxT_kept, 1)
                        if u == 1:
                            act.wait_ge(keys_in[0], (b * PAIRS + p) * (ND * 16) + ND * 16)
                        else:
                            act.wait_ge(keys_in[1], (b * PAIRS + p) * (ND * 16) + ONE)
                        for g in range(G):
                            act.wait_ge(k_made, n * G + (u * G + g + 1))
                            act.wait_ge(k_rest, n * G + (u * G + g - 1 + ONE))
                            shifted = bk[:, g:g + 1] if b_k is not None else 0.0
                            act.activation(kf[g % 2], bank[2 + g % 2][:], ACT.Identity, bias=shifted)
                            if small:
                                act.activation(kparts[:, 0, g], bank[2 + g % 2][:], ACT.Identity,
                                               bias=shifted).then_inc(k_kept, 1)
                            else:
                                for odd in range(2):
                                    rows = slice(odd * dh, odd * dh + dh)
                                    for slab in range(2):
                                        at = u * UNITS + 4 * g + 2 * odd + slab
                                        ins = act.activation(keys[rows, bass.ds(p, 1), at, :].rearrange("d p n -> d (p n)"),
                                                             bank[2 + g % 2][rows, :], ACT.Copy)
                                ins.then_inc(k_kept, 1)
                            if g >= 1:
                                second_part(g - 1)
                        second_part(G - 1)
                        for v in range(VU):
                            act.wait_ge(v_made, n * VU + (u * VU + v + 1))
                            act.wait_ge(v_out[v % 2], n * (VU * 8) + ((u * VU // 2 + v // 2) * 16 + ONE))
                            act.activation(v_stage[v % 2][:, :, :, 0:dh],
                                           bank[v % 2][:].rearrange("p (t h w) -> p t h w", t=TPV, h=H),
                                           ACT.Copy).then_inc(v_kept, 1)
                with act.Fori(0, PAIRS) as p:
                    for i in range(2 * SETS):
                        m = (b * CHUNKS + p * 2) * SETS
                        if masked:
                            act.wait_ge(biased, m + (i + 1 + S0))
                            act.activation(slot[i % 4], slot[i % 4], ACT.Exp).then_inc(probs, 1)
                        else:
                            act.wait_ge(set_scored, m + (i + 1))
                            act.wait_ge(used, m + (i - 3 + S0))
                            act.wait_ge(summed, m * TS + ((i - 3) * TS + S0))
                            act.activation(slot[i % 4], duo[i % 2][:], ACT.Exp).then_inc(probs, 1)
                act.wait_ge(used, b * (CHUNKS * SETS) + (CHUNKS * SETS + S0))
                if not small:
                    act.wait_ge(sums_made, b + 1)
                act.activation(slot[0][:, 0:512], bank[0][:], ACT.Copy)
                ins = act.activation(slot[0][:, 512:1024], bank[1][:], ACT.Copy)
                if not small:
                    act.activation(slot[1][:, 0:512], bank[2][:], ACT.Copy)
                    ins = act.activation(slot[1][:, 512:1024], bank[3][:], ACT.Copy)
                ins.then_inc(o_kept, 1)
                act.wait_ge(o_out, b * (NDO * 16) + NDO * 16)

        @block.vector
        def _(dve):
            dve.sem_inc(reduced, M0)
            if masked:
                dve.sem_inc(biased, S0)
            if not small:
                dve.sem_inc(summed, S0)
            with dve.Fori(0, B) as b:
                dve.memset(best[:], LOWEST).then_inc(best_reset, 1)
                dve.wait_ge(best_reset, b + 1)
                settle(dve, "dve")
                with dve.Fori(0, PAIRS) as p:
                    for u in range(2):
                        n = b * CHUNKS + p * 2
                        if masked:
                            dve.wait_ge(bias_in[u], (b * PAIRS + p) * 16 + 16)
                        for i in range(UM):
                            dve.wait_ge(scored, n * UM + (u * UM + i + 1))
                            if masked:
                                dve.wait_ge(reduced, n * UM + (u * UM + i - 1 + M0))
                                settle(dve, "dve")
                                dve.tensor_tensor_reduce(junk[i % 2][:], quad[i % 4], bias[u][:, i % QT, :], 1.0, LOWEST,
                                                         ALU.add, ALU.max, best_c[:, i:i + 1]).then_inc(reduced, 1)
                            else:
                                dve.tensor_reduce(best_c[:, i:i + 1], quad[i % 4], AX.X, ALU.max).then_inc(reduced, 1)
                        dve.wait_ge(reduced, n * UM + (u * UM + UM + M0))
                        dve.tensor_tensor(best[:], best[:], best_c[:], ALU.max).then_inc(folded, 1)
                        dve.wait_ge(folded, n + (u + 1))
                dve.tensor_scalar(neg[:], best[:], -1.0, None, ALU.mult).then_inc(negated, 1)
                dve.wait_ge(max_turned, b + 1)
                dve.tensor_copy(neg_parts[:, 0, :], quad[0][0:UM, 0:P]).then_inc(max_cut, 1)
                dve.wait_ge(max_cut, b * 4 + 1)
                dve.tensor_tensor(neg_rest[:], quad[0][0:UM, 0:P], neg_parts[:, 0, :], ALU.subtract).then_inc(max_cut, 1)
                dve.wait_ge(max_cut, b * 4 + 2)
                dve.tensor_copy(neg_parts[:, 1, :], neg_rest[:]).then_inc(max_cut, 1)
                dve.wait_ge(max_cut, b * 4 + 3)
                dve.tensor_tensor(neg_parts[:, 2, :], neg_rest[:], neg_parts[:, 1, :], ALU.subtract).then_inc(max_cut, 1)
                dve.wait_ge(v_kept, b * (CHUNKS * VU) + (CHUNKS * VU + ONE))
                dve.memset(bank[0][:], 0.0)
                ins = dve.memset(bank[1][:], 0.0)
                if not small:
                    ins = dve.memset(acc[:], 0.0)
                ins.then_inc(out_reset, 1)
                dve.wait_ge(out_reset, b + 1)
                settle(dve, "dve")
                with dve.Fori(0, PAIRS) as p:
                    m = (b * CHUNKS + p * 2) * SETS
                    for i in range(2 * SETS):
                        u, at = i // SETS, i % SETS
                        if masked:
                            if at == 0:
                                dve.wait_ge(biasT_in[u], (b * PAIRS + p) * 16 + 16)
                            dve.wait_ge(set_scored, m + (i + 1))
                            dve.wait_ge(used, m + (i - 3 + S0))
                            dve.tensor_tensor(slot[i % 4].rearrange("p (h q) -> p h q", h=HS),
                                              duo[i % 2][:].rearrange("p (h q) -> p h q", h=HS),
                                              biasT[u][:, at // 4:at // 4 + 1, :].broadcast_to([P, HS, S]),
                                              ALU.add).then_inc(biased, 1)
                        elif not small:
                            pair = at // 2
                            dve.wait_ge(probs, m + (i + 1 + S0))
                            for t in range(TS):
                                dve.wait_ge(summed, m * TS + (i * TS + t + S0))
                                both = acc[:, 2 * pair:2 * pair + 2, :].rearrange("p h q -> p (h q)")
                                dve.tensor_tensor(both, both, slot[i % 4][:, t * 512:(t + 1) * 512],
                                                  ALU.add).then_inc(summed, 1)

        @block.tensor
        def _(pe):
            pe.sem_inc(ctx_turned, ONE)
            pe.sem_inc(used, S0)
            pe.wait_ge(w_loaded, LOADS)
            if not small:
                pe.wait_ge(ones_set, 2)
            PS0 = 0 if masked else S0

            with pe.Fori(0, B) as b:
                with pe.Fori(0, PAIRS) as p:
                    n = b * CHUNKS + p * 2

                    def turn(u):
                        pe.wait_ge(ctx_in, n * 16 + (u * 16 + 16))
                        pe.wait_ge(v_kept, n * VU + (u * VU + ONE))
                        for k in range(KT):
                            for t in range(TPC):
                                mm = pe.transpose(bank[k][:, t * P:(t + 1) * P], ctx_sb[:, t, k * P:(k + 1) * P], ident[:])
                        mm.then_inc(ctx_turned, 1)

                    def make_keys(u, g):
                        pe.wait_ge(ctxT_kept, n + (u + 1))
                        if g >= 2:
                            pe.wait_ge(k_kept, n * G + (u * G + g - 1))
                        elif u == 1:
                            pe.wait_ge(k_kept, n * G + G)
                        for k in range(KT):
                            mm = pe.matmul(bank[2 + g % 2][:], wk[:, k, g * P:(g + 1) * P], ctxT[:, k, :],
                                           start=k == 0, stop=k == KT - 1)
                        mm.then_inc(k_made, 1)

                    def make_values(u, v):
                        if v >= 2:
                            pe.wait_ge(v_kept, n * VU + (u * VU + v - 1 + ONE))
                        for t in range(TPV):
                            for k in range(KT):
                                at = (v * TPV + t) * P
                                mm = pe.matmul(bank[v % 2][:, t * HD:(t + 1) * HD], ctxT[:, k, at:at + P], wv[:, k, :],
                                               start=k == 0, stop=k == KT - 1)
                        mm.then_inc(v_made, 1)

                    def score(u, i):
                        h, q = i // QT, slice(i % QT * P, i % QT * P + P)
                        if i == 0:
                            pe.wait_ge(keys_in[u], (b * PAIRS + p) * (ND * 16) + (ND * 16 + ONE * u))
                            pe.wait_ge(k_kept, n * G + (u + 1) * G)
                        pe.wait_ge(reduced, n * UM + (u * UM + i - 3 + M0))
                        if small:
                            mm = pe.matmul(quad[i % 4], query[0:KQ, h, q],
                                           keys[0:KQ, bass.ds(p, 1), u * UNITS + h, :].rearrange("k p n -> k (p n)"),
                                           start=True, stop=True)
                        else:
                            for x, (tile, slab) in enumerate(((0, 0), (1, 0), (2, 1))):
                                mm = pe.matmul(quad[i % 4], query[:, tile * H + h, q],
                                               keys[:, bass.ds(p, 1), u * UNITS + 2 * h + slab, :].rearrange("k p n -> k (p n)"),
                                               start=x == 0, stop=x == 2)
                        mm.then_inc(scored, 1)

                    turn(0)
                    for g in range(G):
                        make_keys(0, g)
                    for v in range(VU):
                        make_values(0, v)
                    turn(1)
                    for g in range(G // 2):
                        make_keys(1, g)
                    pe.wait_ge(q_in, b * (NDQ * 16) + NDQ * 16)
                    gap = 8 if small else 2
                    for i in range(UM):
                        score(0, i)
                        if i % gap == 0:
                            x = i // gap + G // 2
                            if x < G:
                                make_keys(1, x)
                            elif x < G + VU:
                                make_values(1, x - G)
                    for i in range(UM):
                        score(1, i)

                pe.wait_ge(negated, b + 1)
                pe.transpose(quad[0][0:UM, 0:P], neg[:], ident[:]).then_inc(max_turned, 1)
                pe.wait_ge(max_in, b * 48 + 48)
                pe.wait_ge(out_reset, b + 1)
                settle(pe, "pe")

                with pe.Fori(0, PAIRS) as p:
                    m = (b * CHUNKS + p * 2) * SETS

                    def score_set(i):
                        u, at = i // SETS, i % SETS
                        pe.wait_ge(biased if masked else probs, m + (i - 1 + S0))
                        for x in range(4):
                            t, h = (at // 4, at % 4 * 4 + x) if small else (at % 2 * 2 + x // 2, at // 2 * 2 + x % 2)
                            out = duo[i % 2][:, x * S:(x + 1) * S]
                            if small:
                                mm = pe.matmul(out, keys[0:KQ + 3, bass.ds(p, 1), u * UNITS + h, t * P:(t + 1) * P]
                                               .rearrange("k p n -> k (p n)"), query[0:KQ + 3, h, :], start=True, stop=True)
                            else:
                                for y, (tile, slab) in enumerate(((0, 0), (1, 0), (2, 1))):
                                    pe.matmul(out, keys[:, bass.ds(p, 1), u * UNITS + 2 * h + slab, t * P:(t + 1) * P]
                                              .rearrange("k p n -> k (p n)"), query[:, tile * H + h, :], start=y == 0, stop=False)
                                mm = pe.matmul(out, onesb[:], shift[:, h, :], start=False, stop=True)
                        mm.then_inc(set_scored, 1)

                    def use_set(i):
                        u, at = i // SETS, i % SETS
                        if at == 0:
                            pe.wait_ge(v_in[u], (b * PAIRS + p) * 16 + 16)
                        pe.wait_ge(probs, m + (i + 1 + PS0))
                        for x in range(4):
                            if small:
                                t, h, group, row = at // 4, at % 4 * 4 + x, at % 4, x * 32
                            else:
                                t, h, group, row = at % 2 * 2 + x // 2, at // 2 * 2 + x % 2, at // 2, x % 2 * 64
                            mm = pe.matmul(bank[group // 2][row:row + VW, group % 2 * S:group % 2 * S + S],
                                           value[u][:, t, h * VW:(h + 1) * VW], slot[i % 4][:, x * S:(x + 1) * S],
                                           start=False, stop=True, skip_group_check=True)
                        mm.then_inc(used, 1)

                    for i in range(2 * SETS):
                        score_set(i)
                        if i >= 2:
                            use_set(i - 2)
                    use_set(2 * SETS - 2)
                    use_set(2 * SETS - 1)

                if not small:
                    pe.wait_ge(summed, b * (CHUNKS * SETS * TS) + (CHUNKS * SETS * TS + S0))
                    for h in range(H):
                        row, group = h % 2 * 64, h // 2
                        mm = pe.matmul(bank[2 + group // 2][row:row + 64, group % 2 * S:group % 2 * S + S],
                                       ones[:, 0:64], acc[:, h, :], start=True, stop=True, skip_group_check=True)
                    mm.then_inc(sums_made, 1)
                pe.wait_ge(o_kept, b + 1 + ONE)


def project_heads(c, H, o_rows, sum_rows, b_v, w_o, b_o, x_rows, ones, tag):
    nc = c.nc
    small = H == 16
    o_in, w_in, x_in = c.sem(tag + "o_in"), c.sem(tag + "w_in"), c.sem(tag + "x_in")
    cleared, chosen, spread = c.sem(tag + "cleared"), c.sem(tag + "chosen"), c.sem(tag + "spread")
    inverted, normed, projected, added, stored = (c.sem(tag + n) for n in
                                                  ("inverted", "normed", "projected", "added", "stored"))
    W = 4 * S
    with ExitStack() as s:
        def sb(n, shape, dt=F32):
            return s.enter_context(nc.sbuf_tensor(tag + n, shape, dt))

        o = sb("o", [P, B, W])
        inv = sb("inv", [P, B, W])
        on = sb("on", [P, B, W])
        x = sb("x", [P, NT, D])
        wo = sb("wo", [P, 4, D])
        bo = sb("bo", [1, D])
        bv = sb("bv", [P, 4])
        if small:
            pick = sb("pick", [P, P])
        else:
            sums = sb("sums", [P, B, W])
        ps = [s.enter_context(nc.psum_tensor(f"{tag}ps{i}", [P, 512], F32)) for i in range(8)]
        block = s.enter_context(nc.Block())
        NW = 9 if small else 2

        @block.sync
        def _(sp):
            sp.dma_start(o[:], o_rows.ap().rearrange("b p n -> p b n")).then_inc(o_in, 16)
            if not small:
                sp.dma_start(sums[:], sum_rows.ap().rearrange("b p n -> p b n")).then_inc(o_in, 16)
            sp.dma_start(bo[:], b_o.rearrange("(a n) -> a n", a=1)).then_inc(w_in, 16)
            if small:
                sp.wait_ge(cleared, 2)
                for j in range(4):
                    sp.dma_start(wo[32 * j:32 * j + 16, :, :],
                                 w_o.rearrange("(g j d) n -> j d g n", j=4, d=16)[j]).then_inc(w_in, 16)
                    sp.dma_start(bv[32 * j:32 * j + 16, :],
                                 b_v.rearrange("(g j d) -> j d g", j=4, d=16)[j],
                                 allow_slow_non_contiguous=True).then_inc(w_in, 16)
            else:
                sp.dma_start(wo[:], w_o.rearrange("(g p) n -> p g n", p=P)).then_inc(w_in, 16)
            sp.dma_start(x[:], x_rows.ap().rearrange("(t p) d -> p t d", p=P)).then_inc(x_in, 16)
            sp.wait_ge(added, NT)
            sp.dma_start(x_rows.ap().rearrange("(t p) d -> p t d", p=P), x[:]).then_inc(stored, 16)
            sp.wait_ge(stored, 16)

        @block.gpsimd
        def _(pool):
            if small:
                pool.memset(wo[:], 0.0).then_inc(cleared, 1)
                pool.memset(bv[:], 0.0).then_inc(cleared, 1)
                pool.memset(pick[:], 0.0).then_inc(cleared, 1)
                pool.wait_ge(cleared, 3)
                view = pick[:].rearrange("k (j d) -> k j d", j=4)
                pool.affine_select(out=view, in_=view, compare_op=ALU.not_equal, fill=1.0, base=-16,
                                   pattern=[[-32, 4], [0, 32]], channel_multiplier=1).then_inc(chosen, 1)

        @block.tensor
        def _(pe):
            if small:
                pe.wait_ge(o_in, 16)
                pe.wait_ge(chosen, 1)
                for i in range(2 * B):
                    pe.matmul(ps[i][:], pick[:], o[:, i // 2, i % 2 * 512:i % 2 * 512 + 512],
                              start=True, stop=True).then_inc(spread, 1)
            pe.wait_ge(w_in, 16 * NW)
            for t in range(NT):
                pe.wait_ge(normed, 2 * (t // QT) + 2)
                if small and t == 0:
                    pe.wait_ge(inverted, 2 * B)
                for g in range(4):
                    at = g * S + t % QT * P
                    pe.matmul(ps[t][:, 0:D], on[:, t // QT, at:at + P], wo[:, g, :], start=g == 0, stop=False)
                pe.matmul(ps[t][:, 0:D], ones[0:1, :], bo[:], start=False, stop=True).then_inc(projected, 1)

        @block.vector
        def _(dve):
            dve.wait_ge(o_in, 16 if small else 32)
            dve.wait_ge(w_in, 16 * NW)
            for i in range(2 * B):
                cols = slice(i % 2 * 512, i % 2 * 512 + 512)
                if small:
                    dve.wait_ge(spread, i + 1)
                dve.reciprocal(inv[:, i // 2, cols], ps[i][:] if small else sums[:, i // 2, cols]).then_inc(inverted, 1)
            for i in range(2 * B):
                cols = slice(i % 2 * 512, i % 2 * 512 + 512)
                dve.wait_ge(inverted, i + 1)
                if small:
                    dve.tensor_tensor(inv[:, i // 2, cols], inv[:, i // 2, cols], o[:, i // 2, cols],
                                      ALU.mult).then_inc(inverted, 1)
                    dve.wait_ge(inverted, 2 * B + i + 1)
                    for g in range(i % 2 * 2, i % 2 * 2 + 2):
                        ins = dve.tensor_scalar(on[:, i // 2, g * S:(g + 1) * S], inv[:, i // 2, g * S:(g + 1) * S],
                                                bv[:, g:g + 1], None, ALU.add)
                    ins.then_inc(normed, 1)
                else:
                    dve.tensor_tensor(on[:, i // 2, cols], inv[:, i // 2, cols], o[:, i // 2, cols],
                                      ALU.mult).then_inc(normed, 1)
            dve.wait_ge(x_in, 16)
            for t in range(NT):
                dve.wait_ge(projected, t + 1)
                dve.tensor_tensor(x[:, t, :], ps[t][:, 0:D], x[:, t, :], ALU.add).then_inc(added, 1)


def channel_attention(c, xnT, w_qk, w_v, w_o, tau, x_rows, ident, ones, tag):
    nc = c.nc
    DH = 16
    w_in, picks, tau_col = c.sem(tag + "w_in"), c.sem(tag + "picks"), c.sem(tag + "tau_col")
    qk_made, qk_kept, v_made, v_kept = (c.sem(tag + n) for n in ("qk_made", "qk_kept", "v_made", "v_kept"))
    gram_made, step, norms, exped, mixed, mix_kept = (c.sem(tag + n) for n in
                                                     ("gram_made", "step", "norms", "exped", "mixed", "mix_kept"))
    x_in, projected, added, stored = (c.sem(tag + n) for n in ("x_in", "projected", "added", "stored"))
    GB = B * KT
    with ExitStack() as s:
        def sb(n, shape, dt=F32):
            return s.enter_context(nc.sbuf_tensor(tag + n, shape, dt))

        wqk, wv, wo = sb("wqk", [P, KT, D]), sb("wv", [P, KT, D]), sb("wo", [P, KT, D])
        tau_sb = sb("tau_sb", [16, 1])
        pick = sb("pick", [16, D])
        tau_c = sb("tau_c", [P, KT])
        same = sb("same", [P, P])
        off = sb("off", [P, P])
        qk = sb("qk", [P, NT, D])
        vT = sb("vT", [P, KT, N])
        gram, diag, logit = sb("gram", [P, GB, P]), sb("diag", [P, GB, P]), sb("logit", [P, GB, P])
        q2 = sb("q2", [P, GB])
        top, negtop, total, inv = (sb(n, [P, GB]) for n in ("top", "negtop", "total", "inv"))
        attn = sb("attn", [P, GB, P])
        mix = sb("mix", [P, GB, D])
        x = sb("x", [P, NT, D])
        ps = [s.enter_context(nc.psum_tensor(f"{tag}ps{i}", [P, 512], F32)) for i in range(8)]
        block = s.enter_context(nc.Block())

        @block.sync
        def _(sp):
            for w, src in ((wqk, w_qk), (wv, w_v), (wo, w_o)):
                sp.dma_start(w[:], src.rearrange("(k p) n -> p k n", p=P)).then_inc(w_in, 16)
            sp.dma_start(tau_sb[:], tau.rearrange("h a b -> h (a b)")).then_inc(w_in, 16)
            sp.dma_start(x[:], x_rows.ap().rearrange("(t p) d -> p t d", p=P)).then_inc(x_in, 16)
            sp.wait_ge(added, NT)
            sp.dma_start(x_rows.ap().rearrange("(t p) d -> p t d", p=P), x[:]).then_inc(stored, 16)
            sp.wait_ge(stored, 16)

        @block.gpsimd
        def _(pool):
            pool.memset(pick[:], 1.0).then_inc(picks, 1)
            pool.wait_ge(picks, 1)
            pool.affine_select(out=pick[:], in_=pick[:], compare_op=ALU.is_ge, fill=0.0, base=0,
                               pattern=[[1, D]], channel_multiplier=-DH).then_inc(picks, 1)
            pool.wait_ge(picks, 2)
            pool.affine_select(out=pick[:], in_=pick[:], compare_op=ALU.is_ge, fill=0.0, base=DH - 1,
                               pattern=[[-1, D]], channel_multiplier=DH).then_inc(picks, 1)

        @block.tensor
        def _(pe):
            pe.wait_ge(w_in, 64)
            pe.wait_ge(picks, 3)
            for k in range(KT):
                pe.matmul(ps[7][:, k:k + 1], pick[:, k * P:(k + 1) * P], tau_sb[:], start=True, stop=True)
            pe.matmul(ps[7][:, P:2 * P], pick[:, 0:P], pick[:, 0:P], start=True, stop=True).then_inc(tau_col, 1)
            for t in range(NT):
                if t >= 4:
                    pe.wait_ge(qk_kept, t - 3)
                for k in range(KT):
                    mm = pe.matmul(ps[t % 4][:, 0:D], xnT[:, k, t * P:(t + 1) * P], wqk[:, k, :],
                                   start=k == 0, stop=k == KT - 1)
                mm.then_inc(qk_made, 1)
            for i in range(KT * 2):
                if i >= 2:
                    pe.wait_ge(v_kept, i - 1)
                for k in range(KT):
                    mm = pe.matmul(ps[4 + i % 2][:], wv[:, k, i // 2 * P:(i // 2 + 1) * P],
                                   xnT[:, k, i % 2 * 512:i % 2 * 512 + 512], start=k == 0, stop=k == KT - 1)
                mm.then_inc(v_made, 1)
            pe.wait_ge(qk_kept, NT)
            for i in range(GB):
                b, m = i // KT, i % KT
                for t in range(QT):
                    rows = qk[:, b * QT + t, m * P:(m + 1) * P]
                    mm = pe.matmul(ps[i // 4][:, i % 4 * P:(i % 4 + 1) * P], rows, rows, start=t == 0, stop=t == QT - 1)
                mm.then_inc(gram_made, 1)
            pe.wait_ge(step, 3)
            for i in range(2):
                mm = pe.matmul(ps[2 + i][:], ones[:], diag[:, 4 * i:4 * i + 4, :].rearrange("p i n -> p (i n)"),
                               start=True, stop=True)
            mm.then_inc(norms, 1)
            pe.wait_ge(v_kept, 2 * KT)
            for i in range(GB):
                if i >= 4:
                    pe.wait_ge(mix_kept, i - 3)
                pe.wait_ge(step, 13 + i)
                pe.matmul(ps[4 + i % 4][:, 0:D], attn[:, i, :], wo[:, i % KT, :], start=True, stop=True).then_inc(mixed, 1)
            pe.wait_ge(mix_kept, GB)
            for t in range(NT):
                if t >= 4:
                    pe.wait_ge(added, t - 3)
                for k in range(KT):
                    mm = pe.matmul(ps[t % 4][:, 0:D], vT[:, k, t * P:(t + 1) * P], mix[:, t // QT * KT + k, :],
                                   start=k == 0, stop=k == KT - 1)
                mm.then_inc(projected, 1)

        @block.scalar
        def _(act):
            for t in range(NT):
                act.wait_ge(qk_made, t + 1)
                act.activation(qk[:, t, :], ps[t % 4][:, 0:D], ACT.Copy).then_inc(qk_kept, 1)
            for i in range(KT * 2):
                act.wait_ge(v_made, i + 1)
                act.activation(vT[:, i // 2, i % 2 * 512:i % 2 * 512 + 512], ps[4 + i % 2][:], ACT.Copy).then_inc(v_kept, 1)
            act.wait_ge(step, 11)
            for i in range(GB):
                act.activation(attn[:, i, :], logit[:, i, :], ACT.Exp, bias=negtop[:, i:i + 1],
                               accum_out=total[:, i:i + 1]).then_inc(exped, 1)
            for i in range(GB):
                act.wait_ge(mixed, i + 1)
                act.activation(mix[:, i, :], ps[4 + i % 4][:, 0:D], ACT.Copy).then_inc(mix_kept, 1)

        @block.vector
        def _(dve):
            dve.wait_ge(tau_col, 1)
            dve.tensor_copy(tau_c[:], ps[7][:, 0:KT])
            dve.tensor_copy(same[:], ps[7][:, P:2 * P]).then_inc(step, 1)
            dve.wait_ge(step, 1)
            dve.tensor_scalar(off[:], same[:], -LOWEST, LOWEST, ALU.mult, ALU.add)
            dve.wait_ge(gram_made, GB)
            for i in range(2):
                ins = dve.tensor_copy(gram[:, 4 * i:4 * i + 4, :].rearrange("p i n -> p (i n)"), ps[i][:])
            ins.then_inc(step, 1)
            dve.wait_ge(step, 2)
            dve.tensor_tensor(diag[:], gram[:], ident[:].unsqueeze(1).broadcast_to([P, GB, P]), ALU.mult).then_inc(step, 1)
            dve.wait_ge(step, 3)
            dve.tensor_reduce(q2[:], diag[:], AX.X, ALU.add).then_inc(step, 1)
            dve.wait_ge(step, 4)
            for i in range(GB):
                ins = dve.tensor_scalar(logit[:, i, :], gram[:, i, :], 2.0, q2[:, i:i + 1], ALU.mult, ALU.subtract)
            ins.then_inc(step, 1)
            dve.wait_ge(step, 5)
            dve.wait_ge(norms, 1)
            for i in range(2):
                half = logit[:, 4 * i:4 * i + 4, :].rearrange("p i n -> p (i n)")
                ins = dve.tensor_tensor(half, half, ps[2 + i][:], ALU.subtract)
            ins.then_inc(step, 1)
            dve.wait_ge(step, 6)
            for m in range(KT):
                ins = dve.tensor_scalar(logit[:, m:GB:KT, :], logit[:, m:GB:KT, :], 1.0 / 16.0, tau_c[:, m:m + 1],
                                        ALU.mult, ALU.mult)
            ins.then_inc(step, 1)
            dve.wait_ge(step, 7)
            dve.tensor_tensor(logit[:], logit[:], same[:].unsqueeze(1).broadcast_to([P, GB, P]), ALU.mult).then_inc(step, 1)
            dve.wait_ge(step, 8)
            dve.tensor_tensor(logit[:], logit[:], off[:].unsqueeze(1).broadcast_to([P, GB, P]), ALU.add).then_inc(step, 1)
            dve.wait_ge(step, 9)
            dve.tensor_reduce(top[:], logit[:], AX.X, ALU.max).then_inc(step, 1)
            dve.wait_ge(step, 10)
            dve.tensor_scalar(negtop[:], top[:], -1.0, None, ALU.mult).then_inc(step, 1)
            dve.wait_ge(exped, GB)
            dve.reciprocal(inv[:], total[:]).then_inc(step, 1)
            dve.wait_ge(step, 12)
            for i in range(GB):
                dve.tensor_scalar(attn[:, i, :], attn[:, i, :], inv[:, i:i + 1], None, ALU.mult).then_inc(step, 1)
            dve.wait_ge(x_in, 16)
            for t in range(NT):
                dve.wait_ge(projected, t + 1)
                dve.tensor_tensor(x[:, t, :], ps[t % 4][:, 0:D], x[:, t, :], ALU.add).then_inc(added, 1)


def route(c, xnT, w_g, gate, ones, onesb, tag):
    nc = c.nc
    E = 8
    CAP = 320
    w_in, built, logits, step, exped, counted = (c.sem(tag + n) for n in
                                                 ("w_in", "built", "logits", "step", "exped", "counted"))
    with ExitStack() as s:
        def sb(n, shape, dt=F32):
            return s.enter_context(nc.sbuf_tensor(tag + n, shape, dt))

        wg = sb("wg", [P, KT, E])
        lg, pr = sb("lg", [P, NT, E]), sb("pr", [P, NT, E])
        top, total, inv = sb("top", [P, NT]), sb("total", [P, NT]), sb("inv", [P, NT])
        best8, at8, at8f = sb("best8", [P, NT, E]), sb("at8", [P, NT, E], U32), sb("at8f", [P, NT, E])
        iota = sb("iota", [P, E])
        one = sb("one", [P, 2, NT, E])
        oneb = sb("oneb", [P, 2 * NT, E], BF16)
        upto = sb("upto", [P, P], BF16)
        seat = sb("seat", [P, 2, NT, E])
        place = sb("place", [P, 2 * NT])
        kept = sb("kept", [P, 2, NT])
        g2, den, rden, part = sb("g2", [P, 2, NT]), sb("den", [P, NT]), sb("rden", [P, NT]), sb("part", [P, 2, NT, E])
        ps = [s.enter_context(nc.psum_tensor(f"{tag}ps{i}", [P, 512], F32)) for i in range(2)]
        block = s.enter_context(nc.Block())

        @block.sync
        def _(sp):
            sp.dma_start(wg[:], w_g.rearrange("(k p) n -> p k n", p=P)).then_inc(w_in, 16)

        @block.gpsimd
        def _(pool):
            pool.memset(upto[:], 1.0).then_inc(built, 1)
            pool.memset(onesb[:], 1.0).then_inc(built, 1)
            for e in range(E):
                pool.memset(iota[:, e:e + 1], float(e)).then_inc(built, 1)
            pool.wait_ge(built, 2 + E)
            pool.affine_select(out=upto[:], in_=upto[:], compare_op=ALU.is_ge, fill=0.0, base=0,
                               pattern=[[1, P]], channel_multiplier=-1).then_inc(built, 1)

        @block.tensor
        def _(pe):
            pe.wait_ge(w_in, 16)
            for t in range(NT):
                for k in range(KT):
                    mm = pe.matmul(ps[0][:, t * E:(t + 1) * E], xnT[:, k, t * P:(t + 1) * P], wg[:, k, :],
                                   start=k == 0, stop=k == KT - 1)
            mm.then_inc(logits, 1)
            pe.wait_ge(built, 3 + E)
            pe.wait_ge(step, 11)
            for j in range(2 * NT):
                for i in range(j):
                    pe.matmul(ps[1][:, j * E:(j + 1) * E], onesb[:], oneb[:, i, :], start=i == 0, stop=False)
                mm = pe.matmul(ps[1][:, j * E:(j + 1) * E], upto[:], oneb[:, j, :], start=j == 0, stop=True)
            mm.then_inc(counted, 1)

        @block.scalar
        def _(act):
            act.wait_ge(step, 3)
            act.activation(pr[:], lg[:], ACT.Exp).then_inc(exped, 1)

        @block.vector
        def _(dve):
            def wide(a, n=NT):
                return a.unsqueeze(2).broadcast_to([P, n, E])

            dve.wait_ge(logits, 1)
            dve.tensor_copy(lg[:].rearrange("p t e -> p (t e)"), ps[0][:, 0:NT * E]).then_inc(step, 1)
            dve.wait_ge(step, 1)
            dve.tensor_reduce(top[:], lg[:], AX.X, ALU.max).then_inc(step, 1)
            dve.wait_ge(step, 2)
            dve.tensor_tensor(lg[:], lg[:], wide(top[:]), ALU.subtract).then_inc(step, 1)
            dve.wait_ge(exped, 1)
            dve.tensor_reduce(total[:], pr[:], AX.X, ALU.add).then_inc(step, 1)
            dve.wait_ge(step, 4)
            dve.reciprocal(inv[:], total[:]).then_inc(step, 1)
            dve.wait_ge(step, 5)
            dve.tensor_tensor(pr[:], pr[:], wide(inv[:]), ALU.mult).then_inc(step, 1)
            dve.wait_ge(step, 6)
            for t in range(NT):
                ins = dve.max(best8[:, t, :], pr[:, t, :])
            ins.then_inc(step, 1)
            dve.wait_ge(step, 7)
            for t in range(NT):
                ins = dve.max_index(at8[:, t, :], best8[:, t, :], pr[:, t, :])
            ins.then_inc(step, 1)
            dve.wait_ge(step, 8)
            dve.tensor_copy(at8f[:], at8[:]).then_inc(step, 1)
            dve.wait_ge(step, 9)
            dve.wait_ge(built, 2 + E)
            for j in range(2):
                ins = dve.tensor_tensor(one[:, j], wide(at8f[:, :, j]), iota[:].unsqueeze(1).broadcast_to([P, NT, E]),
                                        ALU.is_equal)
            ins.then_inc(step, 1)
            dve.wait_ge(step, 10)
            dve.tensor_copy(oneb[:].rearrange("p (j t) e -> p j t e", j=2), one[:]).then_inc(step, 1)
            dve.wait_ge(counted, 1)
            dve.tensor_tensor(seat[:].rearrange("p j t e -> p (j t e)"), one[:].rearrange("p j t e -> p (j t e)"),
                              ps[1][:, 0:2 * NT * E], ALU.mult).then_inc(step, 1)
            dve.wait_ge(step, 12)
            dve.tensor_reduce(place[:], seat[:].rearrange("p j t e -> p (j t) e"), AX.X, ALU.add).then_inc(step, 1)
            dve.wait_ge(step, 13)
            dve.tensor_scalar(kept[:].rearrange("p j t -> p (j t)"), place[:], float(CAP), None, ALU.is_le).then_inc(step, 1)
            dve.wait_ge(step, 14)
            for j in range(2):
                ins = dve.tensor_tensor(g2[:, j], best8[:, :, j], kept[:, j], ALU.mult)
            ins.then_inc(step, 1)
            dve.wait_ge(step, 15)
            dve.tensor_tensor(den[:], g2[:, 0], g2[:, 1], ALU.add).then_inc(step, 1)
            dve.wait_ge(step, 16)
            dve.tensor_scalar(den[:], den[:], 1e-9, None, ALU.max).then_inc(step, 1)
            dve.wait_ge(step, 17)
            dve.reciprocal(rden[:], den[:]).then_inc(step, 1)
            dve.wait_ge(step, 18)
            dve.tensor_tensor(g2[:], g2[:], rden[:].unsqueeze(1).broadcast_to([P, 2, NT]), ALU.mult).then_inc(step, 1)
            dve.wait_ge(step, 19)
            for j in range(2):
                ins = dve.tensor_tensor(part[:, j], one[:, j], wide(g2[:, j]), ALU.mult)
            ins.then_inc(step, 1)
            dve.wait_ge(step, 20)
            dve.tensor_tensor(gate[:], part[:, 0], part[:, 1], ALU.add).then_inc(step, 1)


def experts(c, xnT, gate, w_in_all, w_out_all, x_rows, tag):
    nc = c.nc
    E, F = 8, 512
    FT = F // P
    HALVES = N // 512
    ONE = 16
    x_in, w_loaded, hidden, gelued, gated, out_made, added, stored = (
        c.sem(tag + n) for n in ("x_in", "w_loaded", "hidden", "gelued", "gated", "out_made", "added", "stored"))
    win_in, wout_in = ([c.sem(f"{tag}{n}{u}") for u in range(2)] for n in ("win_in", "wout_in"))
    with ExitStack() as s:
        def sb(n, shape, dt=F32):
            return s.enter_context(nc.sbuf_tensor(tag + n, shape, dt))

        win = [sb(f"win{u}", [P, KT, 2 * F]) for u in range(2)]
        wout = [sb(f"wout{u}", [P, FT, D]) for u in range(2)]
        ga = [sb(f"ga{i}", [P, 512]) for i in range(2)]
        hid = [sb(f"hid{i}", [P, FT, 512]) for i in range(2)]
        x = sb("x", [P, NT, D])
        ps = [s.enter_context(nc.psum_tensor(f"{tag}ps{i}", [P, 512], F32)) for i in range(8)]
        block = s.enter_context(nc.Block())
        TH = 512 // P
        OUTS = HALVES * TH
        HIDS = HALVES * FT

        @block.sync
        def _(sp):
            sp.dma_start(x[:], x_rows.ap().rearrange("(t p) d -> p t d", p=P)).then_inc(x_in, 16)
            with sp.Fori(0, E // 2) as e:
                for u in range(2):
                    sp.wait_ge(out_made, e * (2 * OUTS) + (u * OUTS - OUTS + 2 * OUTS))
                    sp.dma_start(win[u][:], w_in_all[bass.ds(e * 2 + u, 1)].rearrange("e (k p) n -> p (e k) n", p=P)).then_inc(win_in[u], 16)
                    sp.dma_start(wout[u][:], w_out_all[bass.ds(e * 2 + u, 1)].rearrange("e (k p) n -> p (e k) n", p=P)).then_inc(wout_in[u], 16)
            sp.wait_ge(added, E * OUTS + ONE)
            sp.dma_start(x_rows.ap().rearrange("(t p) d -> p t d", p=P), x[:]).then_inc(stored, 16)
            sp.wait_ge(stored, 16)

        @block.tensor
        def _(pe):
            pe.sem_inc(out_made, 2 * OUTS)
            with pe.Fori(0, E // 2) as e:
                for u in range(2):
                    pe.wait_ge(win_in[u], e * 16 + 16)
                    for half in range(HALVES):
                        cols = slice(half * 512, half * 512 + 512)
                        for f in range(FT):
                            i = (u * HALVES + half) * FT + f
                            pe.wait_ge(gated, e * (2 * HIDS) + (i - 1 + ONE))
                            for part in range(2):
                                at = part * F + f * P
                                for k in range(KT):
                                    mm = pe.matmul(ps[2 * (f % 2) + part][:], win[u][:, k, at:at + P], xnT[:, k, cols],
                                                   start=k == 0, stop=k == KT - 1)
                            mm.then_inc(hidden, 1)
                        if half == 0:
                            pe.wait_ge(wout_in[u], e * 16 + 16)
                        pe.wait_ge(gated, e * (2 * HIDS) + ((u * HALVES + half + 1) * FT + ONE))
                        for t in range(TH):
                            j = (u * HALVES + half) * TH + t
                            pe.wait_ge(added, e * (2 * OUTS) + (j - 3 + ONE))
                            for f in range(FT):
                                mm = pe.matmul(ps[4 + t][:, 0:D], hid[half][:, f, t * P:(t + 1) * P], wout[u][:, f, :],
                                               start=f == 0, stop=f == FT - 1)
                            mm.then_inc(out_made, 1)

        @block.scalar
        def _(act):
            with act.Fori(0, E // 2) as e:
                for i in range(2 * HIDS):
                    act.wait_ge(hidden, e * (2 * HIDS) + (i + 1))
                    act.wait_ge(gated, e * (2 * HIDS) + (i - 1 + ONE))
                    act.activation(ga[i % 2][:], ps[2 * (i % 2)][:], ACT.Gelu).then_inc(gelued, 1)

        @block.vector
        def _(dve):
            dve.sem_inc(gated, ONE)
            dve.sem_inc(added, ONE)
            dve.wait_ge(x_in, 16)
            with dve.Fori(0, E // 2) as e:
                for u in range(2):
                    for half in range(HALVES):
                        for f in range(FT):
                            i = (u * HALVES + half) * FT + f
                            dve.wait_ge(gelued, e * (2 * HIDS) + (i + 1))
                            if f == 0:
                                dve.wait_ge(out_made, e * (2 * OUTS) + ((u * HALVES + half - 1) * TH + 2 * OUTS))
                            dve.tensor_tensor(hid[half][:, f, :], ps[2 * (f % 2) + 1][:], ga[i % 2][:], ALU.mult).then_inc(gated, 1)
                        for t in range(TH):
                            j = (u * HALVES + half) * TH + t
                            row = half * TH + t
                            dve.wait_ge(out_made, e * (2 * OUTS) + (j + 1 + 2 * OUTS))
                            dve.wait_ge(added, e * (2 * OUTS) + (j - 7 + ONE))
                            dve.scalar_tensor_tensor(x[:, row, :], ps[4 + t][:, 0:D],
                                                     gate[:, row, bass.ds(e * 2 + u, 1)],
                                                     x[:, row, :], ALU.mult, ALU.add).then_inc(added, 1)


def refine_root(dve, step, at, var, root, tmp):
    dve.reciprocal(tmp[:, 0], root).then_inc(step, 1)
    dve.wait_ge(step, at + 1)
    dve.tensor_tensor(tmp[:, 1], tmp[:, 0], tmp[:, 0], ALU.mult).then_inc(step, 1)
    dve.wait_ge(step, at + 2)
    dve.tensor_tensor(tmp[:, 2], tmp[:, 1], var, ALU.mult).then_inc(step, 1)
    dve.wait_ge(step, at + 3)
    dve.tensor_scalar(tmp[:, 1], tmp[:, 2], -0.5, 1.5, ALU.mult, ALU.add).then_inc(step, 1)
    dve.wait_ge(step, at + 4)
    dve.tensor_tensor(tmp[:, 3], tmp[:, 1], tmp[:, 0], ALU.mult).then_inc(step, 1)


def self_attention(c, xn, xnT, norm_w, w_q, w_k, w_v, w_o, gate, log_t, x_rows, ident, ones, tag):
    nc = c.nc
    H, KV, DH = 4, 2, 64
    NQK = (H + KV) * DH
    w_in, x_in, step, rooted, spread, scaled = (c.sem(tag + n) for n in
                                               ("w_in", "x_in", "step", "rooted", "spread", "scaled"))
    masks, qkv_made, qkv_kept, turned, kept = (c.sem(tag + n) for n in ("masks", "qkv_made", "qkv_kept", "turned", "kept"))
    scored, masked, maxed, exped, p_turned, p_kept = (c.sem(tag + n) for n in
                                                     ("scored", "masked", "maxed", "exped", "p_turned", "p_kept"))
    mixed, o_normed, o_turned, o_kept, projected, blended, added, stored = (
        c.sem(tag + n) for n in ("mixed", "o_normed", "o_turned", "o_kept", "projected", "blended", "added", "stored"))
    with ExitStack() as s:
        def sb(n, shape, dt=F32):
            return s.enter_context(nc.sbuf_tensor(tag + n, shape, dt))

        w = sb("w", [P, KT, NQK + KV * DH])
        wo, nw = sb("wo", [P, KT, D]), sb("nw", [P, KT])
        two, two_c = sb("two", [1, 2]), sb("two_c", [P, 2])
        scale = sb("scale", [P, 1])
        cmask = sb("cmask", [P, QT, S])
        sq, ms, var, root, tmp = sb("sq", [P, NT, D]), sb("ms", [P, NT]), sb("var", [P, NT]), sb("root", [P, NT]), sb("tmp", [P, 4, NT])
        qkv = sb("qkv", [P, NT, NQK + KV * DH])
        qsq, qn = sb("qsq", [P, NT, NQK]), sb("qn", [P, NT, NQK])
        n2, n1, n0, ninv = (sb(n, [P, NT * 6]) for n in ("n2", "n1", "n0", "ninv"))
        qkT = sb("qkT", [P, 3, N])
        lg = [sb(f"lg{i}", [P, H, S]) for i in range(2)]
        pb = [sb(f"pb{i}", [P, H, S]) for i in range(2)]
        top, bias, total, inv = (sb(n, [P, NT, H]) for n in ("top", "bias", "total", "inv"))
        pT = [sb(f"pT{i}", [P, 2 * H, P]) for i in range(2)]
        o = [sb(f"o{i}", [P, D]) for i in range(2)]
        oT = [sb(f"oT{i}", [P, KT, P]) for i in range(2)]
        x, y = sb("x", [P, NT, D]), sb("y", [P, NT, D])
        duo = [s.enter_context(nc.psum_tensor(f"{tag}duo{i}", [P, 1024], F32)) for i in range(3)]
        mixp = s.enter_context(nc.psum_tensor(tag + "mixp", [P, 512], F32))
        outp = s.enter_context(nc.psum_tensor(tag + "outp", [P, 512], F32))
        block = s.enter_context(nc.Block())

        @block.sync
        def _(sp):
            for j in range(2):
                for kv in range(KV):
                    h = 2 * kv + j
                    sp.dma_start(w[:, :, (j * KV + kv) * DH:(j * KV + kv + 1) * DH],
                                 w_q.rearrange("(k p) n -> p k n", p=P)[:, :, h * DH:(h + 1) * DH]).then_inc(w_in, 16)
            sp.dma_start(w[:, :, H * DH:NQK], w_k.rearrange("(k p) n -> p k n", p=P)).then_inc(w_in, 16)
            sp.dma_start(w[:, :, NQK:], w_v.rearrange("(k p) n -> p k n", p=P)).then_inc(w_in, 16)
            sp.dma_start(wo[:], w_o.rearrange("(k p) n -> p k n", p=P)).then_inc(w_in, 16)
            sp.dma_start(nw[:], norm_w.rearrange("(k p) -> p k", p=P), allow_slow_non_contiguous=True).then_inc(w_in, 16)
            sp.dma_start(two[:, 0:1], gate).then_inc(w_in, 16)
            sp.dma_start(two[:, 1:2], log_t).then_inc(w_in, 16)
            sp.dma_start(x[:], x_rows.ap().rearrange("(t p) d -> p t d", p=P)).then_inc(x_in, 16)
            sp.wait_ge(added, NT)
            sp.dma_start(x_rows.ap().rearrange("(t p) d -> p t d", p=P), x[:]).then_inc(stored, 16)
            sp.wait_ge(stored, 16)

        @block.gpsimd
        def _(pool):
            pool.memset(cmask[:], 0.0).then_inc(masks, 1)
            pool.wait_ge(masks, 1)
            for i in range(QT):
                pool.affine_select(out=cmask[:, i, :], in_=cmask[:, i, :], compare_op=ALU.is_ge, fill=NEG, base=i * P,
                                   pattern=[[-1, S]], channel_multiplier=1).then_inc(masks, 1)

        @block.tensor
        def _(pe):
            pe.wait_ge(w_in, 160)
            pe.matmul(outp[:, 0:2], ones[0:1, :], two[:], start=True, stop=True).then_inc(spread, 1)
            pe.wait_ge(step, 2)
            for t in range(NT):
                if t >= 4:
                    pe.wait_ge(qkv_kept, t - 3)
                for k in range(KT):
                    mm = pe.matmul(duo[t % 4 // 2][:, t % 2 * 512:t % 2 * 512 + 512], xnT[:, k, t * P:(t + 1) * P], w[:, k, :],
                                   start=k == 0, stop=k == KT - 1)
                mm.then_inc(qkv_made, 1)
            for t in range(NT):
                pe.wait_ge(step, 18)
                if t >= 2:
                    pe.wait_ge(kept, t - 1)
                for i in range(3):
                    mm = pe.transpose(duo[2][:, t % 2 * 512 + i * P:t % 2 * 512 + (i + 1) * P],
                                      qn[:, t, i * P:(i + 1) * P], ident[:])
                mm.then_inc(turned, 1)
            pe.wait_ge(kept, NT)
            for i in range(NT + 2):
                if i < NT:
                    if i >= 2:
                        pe.wait_ge(masked, i - 1)
                    for kv in range(KV):
                        rows = slice(kv * DH, kv * DH + DH)
                        for j in range(2):
                            mm = pe.matmul(duo[i % 2][:, (2 * kv + j) * S:(2 * kv + j + 1) * S],
                                           qkT[rows, j, i * P:(i + 1) * P], qkT[rows, 2, i // QT * S:i // QT * S + S],
                                           start=True, stop=True)
                    mm.then_inc(scored, 1)
                if 1 <= i <= NT:
                    g = i - 1
                    pe.wait_ge(exped, H * (g + 1))
                    if g >= 1:
                        pe.wait_ge(p_kept, g)
                    for h in range(H):
                        for k in range(2):
                            mm = pe.transpose(duo[2][:, (2 * h + k) * P:(2 * h + k + 1) * P],
                                              pb[g % 2][:, h, k * P:(k + 1) * P], ident[:])
                    mm.then_inc(p_turned, 1)
                    pe.wait_ge(p_kept, g + 1)
                    if g >= 1:
                        pe.wait_ge(o_kept, g)
                    for h in range(H):
                        for k in range(2):
                            at = NQK + h // 2 * DH
                            mm = pe.matmul(mixp[:, h * DH:(h + 1) * DH], pT[g % 2][:, 2 * h + k, :],
                                           qkv[:, g // QT * QT + k, at:at + DH], start=k == 0, stop=k == 1)
                    mm.then_inc(mixed, 1)
                    pe.wait_ge(o_normed, g + 1)
                    for k in range(KT):
                        mm = pe.transpose(mixp[:, D + k * P:D + (k + 1) * P], o[g % 2][:, k * P:(k + 1) * P], ident[:])
                    mm.then_inc(o_turned, 1)
                if i >= 2:
                    g = i - 2
                    pe.wait_ge(o_kept, g + 1)
                    if g >= 1:
                        pe.wait_ge(blended, g)
                    for k in range(KT):
                        mm = pe.matmul(outp[:, 0:D], oT[g % 2][:, k, :], wo[:, k, :], start=k == 0, stop=k == KT - 1)
                    mm.then_inc(projected, 1)

        @block.scalar
        def _(act):
            act.wait_ge(step, 4)
            act.activation(root[:], var[:], ACT.Sqrt).then_inc(rooted, 1)
            act.wait_ge(step, 9)
            for t in range(NT):
                act.wait_ge(qkv_made, t + 1)
                act.activation(qkv[:, t, :], duo[t % 4 // 2][:, t % 2 * 512:t % 2 * 512 + 512], ACT.Copy,
                               scale=tmp[:, 3, t:t + 1]).then_inc(qkv_kept, 1)
            act.wait_ge(step, 11)
            act.activation(n1[:], n2[:], ACT.Sqrt).then_inc(rooted, 1)
            for t in range(NT):
                act.wait_ge(turned, t + 1)
                act.activation(qkT[:, :, t * P:(t + 1) * P],
                               duo[2][:, t % 2 * 512:t % 2 * 512 + 3 * P].rearrange("p (i n) -> p i n", i=3),
                               ACT.Copy).then_inc(kept, 1)
            act.wait_ge(step, 1)
            act.activation(scale[:], two_c[:, 1:2], ACT.Exp).then_inc(scaled, 1)
            for g in range(NT):
                act.wait_ge(maxed, g + 1)
                if g >= 2:
                    act.wait_ge(p_turned, g - 1)
                for h in range(H):
                    act.activation(pb[g % 2][:, h, :], lg[g % 2][:, h, :], ACT.Exp, bias=bias[:, g, h:h + 1],
                                   scale=scale[:], accum_out=total[:, g, h:h + 1]).then_inc(exped, 1)
                act.wait_ge(p_turned, g + 1)
                if g >= 2:
                    act.wait_ge(mixed, g - 1)
                act.activation(pT[g % 2][:].rearrange("p i n -> p (i n)"), duo[2][:], ACT.Copy).then_inc(p_kept, 1)
                act.wait_ge(o_turned, g + 1)
                if g >= 2:
                    act.wait_ge(projected, g - 1)
                act.activation(oT[g % 2][:], mixp[:, D:2 * D].rearrange("p (k n) -> p k n", k=KT), ACT.Copy).then_inc(o_kept, 1)

        @block.vector
        def _(dve):
            dve.wait_ge(spread, 1)
            dve.tensor_copy(two_c[:], outp[:, 0:2]).then_inc(step, 1)
            dve.wait_ge(w_in, 160)
            for k in range(KT):
                ins = dve.tensor_scalar(w[:, k, :], w[:, k, :], nw[:, k:k + 1], None, ALU.mult)
            ins.then_inc(step, 1)
            for t in range(NT):
                ins = dve.tensor_tensor_reduce(sq[:, t, :], xn[:, t, :], xn[:, t, :], 1.0 / D, 0.0, ALU.mult, ALU.add,
                                               ms[:, t:t + 1])
            ins.then_inc(step, 1)
            dve.wait_ge(step, 3)
            dve.tensor_scalar(var[:], ms[:], 1e-6, None, ALU.add).then_inc(step, 1)
            dve.wait_ge(rooted, 1)
            refine_root(dve, step, 4, var[:], root[:], tmp)
            dve.wait_ge(qkv_kept, NT)
            dve.tensor_tensor(qsq[:], qkv[:, :, 0:NQK], qkv[:, :, 0:NQK], ALU.mult).then_inc(step, 1)
            dve.wait_ge(step, 10)
            dve.tensor_reduce(n2[:], qsq[:].rearrange("p t (h d) -> p (t h) d", d=DH), AX.X, ALU.add).then_inc(step, 1)
            dve.wait_ge(rooted, 2)
            dve.tensor_scalar(n0[:], n1[:], 1e-12, None, ALU.max).then_inc(step, 1)
            dve.wait_ge(step, 12)
            dve.reciprocal(ninv[:], n0[:]).then_inc(step, 1)
            dve.wait_ge(step, 13)
            dve.tensor_tensor(ninv[:], ninv[:], n2[:], ALU.mult).then_inc(step, 1)
            dve.wait_ge(step, 14)
            dve.tensor_tensor(ninv[:], ninv[:], n1[:], ALU.add).then_inc(step, 1)
            dve.wait_ge(step, 15)
            dve.tensor_scalar(n0[:], ninv[:], 0.5, 1e-12, ALU.mult, ALU.max).then_inc(step, 1)
            dve.wait_ge(step, 16)
            dve.reciprocal(n1[:], n0[:]).then_inc(step, 1)
            dve.wait_ge(step, 17)
            dve.tensor_tensor(qn[:].rearrange("p t (h d) -> p (t h) d", d=DH),
                              qkv[:, :, 0:NQK].rearrange("p t (h d) -> p t h d", d=DH),
                              n1[:].unsqueeze(2).broadcast_to([P, NT * 6, DH]), ALU.mult).then_inc(step, 1)
            dve.wait_ge(masks, 1 + QT)
            dve.wait_ge(scaled, 1)
            dve.wait_ge(x_in, 16)
            for g in range(NT + 1):
                if g < NT:
                    dve.wait_ge(scored, g + 1)
                    if g >= 2:
                        dve.wait_ge(exped, H * (g - 1))
                    dve.tensor_tensor(lg[g % 2][:], duo[g % 2][:].rearrange("p (h n) -> p h n", h=H),
                                      cmask[:, g % QT, :].unsqueeze(1).broadcast_to([P, H, S]), ALU.add).then_inc(masked, 1)
                    dve.wait_ge(masked, g + 1)
                    dve.tensor_reduce(top[:, g, :], lg[g % 2][:], AX.X, ALU.max).then_inc(step, 1)
                    dve.wait_ge(step, 19 + 2 * g)
                    dve.tensor_scalar(bias[:, g, :], top[:, g, :], scale[:], -1.0, ALU.mult, ALU.mult).then_inc(maxed, 1)
                    dve.wait_ge(exped, H * (g + 1))
                    dve.reciprocal(inv[:, g, :], total[:, g, :]).then_inc(step, 1)
                    dve.wait_ge(step, 20 + 2 * g)
                    dve.wait_ge(mixed, g + 1)
                    if g >= 2:
                        dve.wait_ge(o_turned, g - 1)
                    dve.tensor_tensor(o[g % 2][:].rearrange("p (h d) -> p h d", d=DH),
                                      mixp[:, 0:D].rearrange("p (h d) -> p h d", d=DH),
                                      inv[:, g, :].unsqueeze(2).broadcast_to([P, H, DH]), ALU.mult).then_inc(o_normed, 1)
                if g >= 1:
                    t = g - 1
                    dve.wait_ge(projected, t + 1)
                    dve.scalar_tensor_tensor(y[:, t, :], outp[:, 0:D], two_c[:, 0:1], xn[:, t, :],
                                             ALU.mult, ALU.add).then_inc(blended, 1)
                    dve.wait_ge(blended, t + 1)
                    dve.tensor_tensor(x[:, t, :], x[:, t, :], y[:, t, :], ALU.add).then_inc(added, 1)


def feed_forward(c, xn, w1, b1, w2, b2, x_rows, out, identb, ones, tag):
    nc = c.nc
    F = 1024
    FT = F // P
    w_in, x_in, wstep, summed, step, rooted = (c.sem(tag + n) for n in ("w_in", "x_in", "wstep", "summed", "step", "rooted"))
    w_turned, w_kept, b_spread, b_kept = (c.sem(tag + n) for n in ("w_turned", "w_kept", "b_spread", "b_kept"))
    x_turned, x_kept, up_made, scaled, gelued, squared = (c.sem(tag + n) for n in
                                                          ("x_turned", "x_kept", "up_made", "scaled", "gelued", "squared"))
    h_turned, h_kept, down_made, added, stored, hstep, biased = (
        c.sem(tag + n) for n in ("h_turned", "h_kept", "down_made", "added", "stored", "hstep", "biased"))
    with ExitStack() as s:
        def sb(n, shape, dt=F32):
            return s.enter_context(nc.sbuf_tensor(tag + n, shape, dt))

        w1_sb, w2_sb = sb("w1", [P, FT, D]), sb("w2", [P, KT, F])
        q1, q2 = sb("q1", [P, FT, D], BF16), sb("q2", [P, KT, F], BF16)
        w1T, w2T = sb("w1T", [P, KT, F], BF16), sb("w2T", [P, FT, D], BF16)
        wsum, mean, wscale = sb("wsum", [P, 2]), sb("mean", [P, 2]), sb("wscale", [P, 2])
        brow, b_all = sb("brow", [1, F + D]), sb("b_all", [P, F + D])
        sq, ms, var, root, tmp = sb("sq", [P, NT, D]), sb("ms", [P, NT]), sb("var", [P, NT]), sb("root", [P, NT]), sb("tmp", [P, 4, NT])
        big, cut, back = sb("big", [P, NT]), sb("cut", [P, NT]), sb("back", [P, NT])
        xs, xq, xqT = sb("xs", [P, NT, D]), sb("xq", [P, NT, D], BF16), sb("xqT", [P, KT, N], BF16)
        h = sb("h", [P, NT, F])
        hq = sb("hq", [P, NT, F], BF16)
        junk = [sb(f"junk{i}", [P, F]) for i in range(2)]
        hqT = [sb(f"hqT{i}", [P, FT, P], BF16) for i in range(2)]
        ms2, var2, root2, tmp2 = sb("ms2", [P, NT]), sb("var2", [P, NT]), sb("root2", [P, NT]), sb("tmp2", [P, 4, NT])
        big2, cut2, back2 = sb("big2", [P, NT]), sb("cut2", [P, NT]), sb("back2", [P, NT])
        x = sb("x", [P, NT, D])
        y = sb("y", [P, NT, D])
        tp = [s.enter_context(nc.psum_tensor(f"{tag}tp{i}", [P, 1024], BF16)) for i in range(2)]
        up = [s.enter_context(nc.psum_tensor(f"{tag}up{i}", [P, 1024], F32)) for i in range(2)]
        down = [s.enter_context(nc.psum_tensor(f"{tag}down{i}", [P, 512], F32)) for i in range(2)]
        block = s.enter_context(nc.Block())

        @block.sync
        def _(sp):
            sp.dma_start(w1_sb[:], w1.rearrange("(k p) n -> p k n", p=P)).then_inc(w_in, 16)
            sp.dma_start(w2_sb[:], w2.rearrange("(k p) n -> p k n", p=P)).then_inc(w_in, 16)
            sp.dma_start(brow[:, 0:F], b1.rearrange("(a n) -> a n", a=1)).then_inc(w_in, 16)
            sp.dma_start(brow[:, F:], b2.rearrange("(a n) -> a n", a=1)).then_inc(w_in, 16)
            sp.dma_start(x[:], x_rows.ap().rearrange("(t p) d -> p t d", p=P)).then_inc(x_in, 16)
            rows = out.rearrange("b s d -> (b s) d").rearrange("(t p) d -> p t d", p=P)
            for t in range(0, NT, 2):
                sp.wait_ge(added, t + 2)
                sp.dma_start(rows[:, t:t + 2, :], y[:, t:t + 2, :]).then_inc(stored, 16)
            sp.wait_ge(stored, 8 * NT)

        @block.tensor
        def _(pe):
            pe.wait_ge(w_in, 64)
            for i, (lo, hi) in enumerate(((0, 512), (512, 1024))):
                pe.matmul(up[0][:, lo:hi], ones[0:1, :], brow[:, lo:hi], start=True, stop=True)
            pe.matmul(up[1][:, 0:D], ones[0:1, :], brow[:, F:], start=True, stop=True).then_inc(b_spread, 1)
            pe.wait_ge(wstep, 2)
            pe.matmul(down[0][:, 0:2], ones[:], wsum[:], start=True, stop=True).then_inc(summed, 1)
            pe.wait_ge(wstep, 10)
            for i in range(4):
                if i >= 2:
                    pe.wait_ge(w_kept, i - 1)
                for j in range(8):
                    if i < 2:
                        mm = pe.transpose(tp[i % 2][:, j * P:(j + 1) * P], q1[:, j, i * P:(i + 1) * P], identb[:])
                    else:
                        f = 4 * (i - 2) + j // 2
                        mm = pe.transpose(tp[i % 2][:, j * P:(j + 1) * P], q2[:, j % 2, f * P:(f + 1) * P], identb[:])
                mm.then_inc(w_turned, 1)
            pe.wait_ge(w_kept, 4)
            pe.wait_ge(step, 16)
            for i in range(KT):
                for t in range(NT):
                    mm = pe.transpose(tp[i][:, t * P:(t + 1) * P], xq[:, t, i * P:(i + 1) * P], identb[:])
                mm.then_inc(x_turned, 1)
            pe.wait_ge(x_kept, KT)
            pe.wait_ge(b_kept, 1)
            for t in range(NT):
                if t >= 2:
                    pe.wait_ge(scaled, t - 1)
                for half in range(2):
                    for k in range(KT):
                        mm = pe.matmul(up[t % 2][:, half * 512:half * 512 + 512], xqT[:, k, t * P:(t + 1) * P],
                                       w1T[:, k, half * 512:half * 512 + 512], start=k == 0, stop=k == KT - 1)
                mm.then_inc(up_made, 1)
            for t in range(NT):
                pe.wait_ge(hstep, 12 + NT + t + 1)
                if t >= 2:
                    pe.wait_ge(h_kept, t - 1)
                for f in range(FT):
                    mm = pe.transpose(tp[t % 2][:, f * P:(f + 1) * P], hq[:, t, f * P:(f + 1) * P], identb[:])
                mm.then_inc(h_turned, 1)
                pe.wait_ge(h_kept, t + 1)
                if t >= 2:
                    pe.wait_ge(added, t - 1)
                for f in range(FT):
                    mm = pe.matmul(down[t % 2][:, 0:D], hqT[t % 2][:, f, :], w2T[:, f, :], start=f == 0, stop=f == FT - 1)
                mm.then_inc(down_made, 1)

        @block.scalar
        def _(act):
            act.wait_ge(b_spread, 1)
            act.activation(b_all[:, 0:F], up[0][:], ACT.Copy)
            act.activation(b_all[:, F:], up[1][:, 0:D], ACT.Copy).then_inc(b_kept, 1)
            act.wait_ge(step, 2)
            act.activation(root[:], var[:], ACT.Sqrt).then_inc(rooted, 1)
            for i in range(4):
                act.wait_ge(w_turned, i + 1)
                if i < 2:
                    act.activation(w1T[:, i, :], tp[i % 2][:], ACT.Copy).then_inc(w_kept, 1)
                else:
                    act.activation(w2T[:, 4 * (i - 2):4 * (i - 1), :].rearrange("p f n -> p (f n)"), tp[i % 2][:],
                                   ACT.Copy).then_inc(w_kept, 1)
            for i in range(KT):
                act.wait_ge(x_turned, i + 1)
                act.activation(xqT[:, i, :], tp[i][:], ACT.Copy).then_inc(x_kept, 1)
            for t in range(NT):
                act.wait_ge(scaled, t + 1)
                act.activation(h[:, t, :], h[:, t, :], ACT.Gelu).then_inc(gelued, 1)
                act.wait_ge(gelued, t + 1)
                if t >= 2:
                    act.wait_ge(squared, t - 1)
                act.activation(junk[t % 2][:], h[:, t, :], ACT.Square, accum_out=ms2[:, t:t + 1]).then_inc(squared, 1)
            act.wait_ge(hstep, NT + 1)
            act.activation(root2[:], var2[:], ACT.Sqrt).then_inc(rooted, 1)
            for t in range(NT):
                act.wait_ge(h_turned, t + 1)
                if t >= 2:
                    act.wait_ge(down_made, t - 1)
                act.activation(hqT[t % 2][:].rearrange("p f n -> p (f n)"), tp[t % 2][:], ACT.Copy).then_inc(h_kept, 1)

        @block.vector
        def _(dve):
            dve.wait_ge(w_in, 64)
            dve.tensor_reduce(wsum[:, 0:1], w1_sb[:].rearrange("p k n -> p (k n)"), AX.X, ALU.add,
                              apply_absolute_value=True).then_inc(wstep, 1)
            dve.tensor_reduce(wsum[:, 1:2], w2_sb[:].rearrange("p k n -> p (k n)"), AX.X, ALU.add,
                              apply_absolute_value=True).then_inc(wstep, 1)
            for t in range(NT):
                ins = dve.tensor_tensor_reduce(sq[:, t, :], xn[:, t, :], xn[:, t, :], 1.0 / D, 0.0, ALU.mult, ALU.add,
                                               ms[:, t:t + 1])
            ins.then_inc(step, 1)
            dve.wait_ge(step, 1)
            dve.tensor_scalar(var[:], ms[:], 1e-6, None, ALU.add).then_inc(step, 1)
            dve.tensor_reduce(big[:], xn[:], AX.X, ALU.max, apply_absolute_value=True).then_inc(step, 1)
            dve.wait_ge(summed, 1)
            dve.tensor_scalar(mean[:], down[0][:, 0:2], 1.0 / (F * D), 1e-5, ALU.mult, ALU.max).then_inc(wstep, 1)
            dve.wait_ge(wstep, 3)
            dve.reciprocal(wscale[:], mean[:]).then_inc(wstep, 1)
            dve.wait_ge(wstep, 4)
            f1, f2 = w1_sb[:].rearrange("p k n -> p (k n)"), w2_sb[:].rearrange("p k n -> p (k n)")
            for i, f in enumerate((f1, f2)):
                dve.tensor_scalar(f, f, wscale[:, i:i + 1], MAGIC, ALU.mult, ALU.add).then_inc(wstep, 1)
            dve.wait_ge(wstep, 6)
            for f in (f1, f2):
                dve.tensor_scalar(f, f, MAGIC, 1.0, ALU.subtract, ALU.min).then_inc(wstep, 1)
            dve.wait_ge(wstep, 8)
            for f, q in ((f1, q1), (f2, q2)):
                dve.tensor_scalar(q[:].rearrange("p k n -> p (k n)"), f, -1.0, None, ALU.max).then_inc(wstep, 1)
            dve.wait_ge(wstep, 10)
            dve.wait_ge(rooted, 1)
            refine_root(dve, step, 3, var[:], root[:], tmp)
            dve.wait_ge(step, 8)
            dve.tensor_tensor(big[:], big[:], tmp[:, 3], ALU.mult).then_inc(step, 1)
            dve.wait_ge(step, 9)
            dve.tensor_scalar(big[:], big[:], 1e-5, None, ALU.max).then_inc(step, 1)
            dve.wait_ge(step, 10)
            dve.reciprocal(cut[:], big[:]).then_inc(step, 1)
            dve.wait_ge(step, 11)
            dve.tensor_scalar(cut[:], cut[:], 127.0, None, ALU.mult).then_inc(step, 1)
            dve.tensor_scalar(back[:], big[:], 1.0 / 127.0, mean[:, 0:1], ALU.mult, ALU.mult).then_inc(step, 1)
            dve.wait_ge(step, 13)
            for t in range(NT):
                ins = dve.tensor_scalar(xs[:, t, :], xn[:, t, :], tmp[:, 3, t:t + 1], cut[:, t:t + 1], ALU.mult, ALU.mult)
            ins.then_inc(step, 1)
            dve.wait_ge(step, 14)
            dve.tensor_scalar(xs[:], xs[:], MAGIC, MAGIC, ALU.add, ALU.subtract).then_inc(step, 1)
            dve.wait_ge(step, 15)
            dve.tensor_scalar(xq[:], xs[:], 127.0, -128.0, ALU.min, ALU.max).then_inc(step, 1)
            dve.wait_ge(b_kept, 1)
            for t in range(NT):
                dve.wait_ge(up_made, t + 1)
                dve.scalar_tensor_tensor(h[:, t, :], up[t % 2][:], back[:, t:t + 1], b_all[:, 0:F],
                                         ALU.mult, ALU.add).then_inc(scaled, 1)
                if t >= 1:
                    dve.wait_ge(gelued, t)
                    dve.tensor_reduce(big2[:, t - 1:t], h[:, t - 1, :], AX.X, ALU.max,
                                      apply_absolute_value=True).then_inc(hstep, 1)
            dve.wait_ge(gelued, NT)
            dve.tensor_reduce(big2[:, NT - 1:NT], h[:, NT - 1, :], AX.X, ALU.max,
                              apply_absolute_value=True).then_inc(hstep, 1)
            dve.wait_ge(squared, NT)
            dve.tensor_scalar(var2[:], ms2[:], 1.0 / F, 1e-6, ALU.mult, ALU.add).then_inc(hstep, 1)
            dve.wait_ge(rooted, 2)
            refine_root(dve, hstep, NT + 1, var2[:], root2[:], tmp2)
            dve.wait_ge(hstep, NT + 6)
            dve.tensor_tensor(big2[:], big2[:], tmp2[:, 3], ALU.mult).then_inc(hstep, 1)
            dve.wait_ge(hstep, NT + 7)
            dve.tensor_scalar(big2[:], big2[:], 1e-5, None, ALU.max).then_inc(hstep, 1)
            dve.wait_ge(hstep, NT + 8)
            dve.reciprocal(cut2[:], big2[:]).then_inc(hstep, 1)
            dve.wait_ge(hstep, NT + 9)
            dve.tensor_scalar(cut2[:], cut2[:], 127.0, None, ALU.mult).then_inc(hstep, 1)
            dve.tensor_scalar(back2[:], big2[:], 1.0 / 127.0, mean[:, 1:2], ALU.mult, ALU.mult).then_inc(hstep, 1)
            dve.wait_ge(hstep, NT + 11)
            dve.wait_ge(x_in, 16)
            dve.tensor_tensor(x[:], x[:], b_all[:, F:].unsqueeze(1).broadcast_to([P, NT, D]), ALU.add).then_inc(hstep, 1)

            def add_out(t):
                dve.wait_ge(down_made, t + 1)
                dve.scalar_tensor_tensor(y[:, t, :], down[t % 2][:, 0:D], back2[:, t:t + 1], x[:, t, :],
                                         ALU.mult, ALU.add).then_inc(added, 1)

            for t in range(NT):
                dve.tensor_scalar(h[:, t, :], h[:, t, :], tmp2[:, 3, t:t + 1], cut2[:, t:t + 1], ALU.mult, ALU.mult).then_inc(biased, 1)
                dve.wait_ge(biased, 2 * t + 1)
                dve.tensor_scalar(h[:, t, :], h[:, t, :], MAGIC, MAGIC, ALU.add, ALU.subtract).then_inc(biased, 1)
                dve.wait_ge(biased, 2 * t + 2)
                dve.tensor_scalar(hq[:, t, :], h[:, t, :], 127.0, -128.0, ALU.min, ALU.max).then_inc(hstep, 1)
                if t >= 2:
                    add_out(t - 2)
            add_out(NT - 2)
            add_out(NT - 1)


def perceiver(nc, a, out, stages=range(1, 7)):
    with ExitStack() as stack:
        c = Ctx(nc)
        x_rows = nc.dram_tensor("x_rows", [N, D], F32, kind="Internal")
        o_rows = nc.dram_tensor("o_rows", [B, P, 1024], F32, kind="Internal")
        sum_rows = nc.dram_tensor("sum_rows", [B, P, 1024], F32, kind="Internal")
        q0 = nc.dram_tensor("q0", [3, 256, N], BF16, kind="Internal")
        q1 = nc.dram_tensor("q1", [3, 512, N], BF16, kind="Internal")
        v0 = nc.dram_tensor("v0", [B * S2, 16 * 17], F32, kind="Internal")
        v1 = nc.dram_tensor("v1", [B * S2, 8 * 64], F32, kind="Internal")
        bias_qk = nc.dram_tensor("bias_qk", [S, S2], F32, kind="Internal")
        bias_kq = nc.dram_tensor("bias_kq", [S2, S], F32, kind="Internal")
        ident = stack.enter_context(nc.sbuf_tensor("ident", [P, P], F32))
        identb = stack.enter_context(nc.sbuf_tensor("identb", [P, P], BF16))
        ones = stack.enter_context(nc.sbuf_tensor("ones", [P, P], F32))
        with c.stage():
            constants(c, ident, identb, ones, a["x"], x_rows, "c_")

        def normed(s, tag):
            xn = s.enter_context(nc.sbuf_tensor(tag + "xn", [P, NT, D], F32))
            xnT = s.enter_context(nc.sbuf_tensor(tag + "xnT", [P, KT, N], F32))
            layer_norm(c, x_rows, xn, xnT, ident, tag)
            return xn, xnT

        if 1 in stages:
            with c.stage():
                with ExitStack() as s:
                    _, xnT = normed(s, "n0_")
                    split_queries(c, xnT, a["L0_xattn_wq"], a["L0_xattn_bq"], 0.25, 256, q0, "q0_")
                scale_mask(c, a["mask_1x1xSxS2_fk1"], bias_qk, bias_kq, ident, "m_")
                cross_attention(c, 16, a["ctx_1024"], a["L0_xattn_wk"], a["L0_xattn_bk"], a["L0_xattn_wv"], q0, v0, o_rows,
                                None, bias_qk, bias_kq, ident, ones, "a0_")
                project_heads(c, 16, o_rows, None, a["L0_xattn_bv"], a["L0_xattn_wo"], a["L0_xattn_bo"], x_rows, ones, "p0_")
        if 2 in stages:
            with c.stage(), ExitStack() as s:
                _, xnT = normed(s, "n1_")
                channel_attention(c, xnT, a["L0_attn_Wqk"], a["L0_attn_Wv"], a["L0_attn_Wo"], a["L0_attn_tau"], x_rows,
                                  ident, ones, "ch_")
        if 3 in stages:
            with c.stage(), ExitStack() as s:
                _, xnT = normed(s, "n2_")
                gate = s.enter_context(nc.sbuf_tensor("gate", [P, NT, 8], F32))
                onesb = s.enter_context(nc.sbuf_tensor("onesb", [P, P], BF16))
                route(c, xnT, a["L0_ffn_Wg"], gate, ones, onesb, "r_")
                experts(c, xnT, gate, a["L0_ffn_W_in"], a["L0_ffn_W_out"], x_rows, "e_")
        if 4 in stages:
            with c.stage():
                with ExitStack() as s:
                    _, xnT = normed(s, "n3_")
                    split_queries(c, xnT, a["L1_xattn_Wq"], None, 0.125, 512, q1, "q1_")
                cross_attention(c, 8, a["ctx_1024"], a["L1_xattn_Wk"], None, a["L1_xattn_Wv"], q1, v1, o_rows, sum_rows,
                                None, None, ident, ones, "a1_")
                project_heads(c, 8, o_rows, sum_rows, None, a["L1_xattn_Wo"], a["L1_xattn_bo"], x_rows, ones, "p1_")
        if 5 in stages:
            with c.stage(), ExitStack() as s:
                xn, xnT = normed(s, "n4_")
                self_attention(c, xn, xnT, a["L1_attn_norm_w"], a["L1_attn_Wq"], a["L1_attn_Wk"], a["L1_attn_Wv"],
                               a["L1_attn_Wo"], a["L1_attn_gate"], a["L1_attn_log_temperature"], x_rows, ident, ones, "s_")
        if 6 in stages:
            with c.stage(), ExitStack() as s:
                xn, _ = normed(s, "n5_")
                feed_forward(c, xn, a["L1_ffn_w1"], a["L1_ffn_b1"], a["L1_ffn_w2"], a["L1_ffn_b2"], x_rows, out,
                             identb, ones, "f_")


_INS = ["x", "ctx_1024", "mask_1x1xSxS2_fk1", "L0_xattn_wq", "L0_xattn_bq", "L0_xattn_wk", "L0_xattn_bk",
        "L0_xattn_wv", "L0_xattn_bv", "L0_xattn_wo", "L0_xattn_bo", "L0_attn_Wqk", "L0_attn_Wv", "L0_attn_Wo",
        "L0_attn_tau", "L0_ffn_Wg", "L0_ffn_W_in", "L0_ffn_W_out", "L1_xattn_Wq", "L1_xattn_Wk", "L1_xattn_Wv",
        "L1_xattn_Wo", "L1_xattn_bo", "L1_attn_norm_w", "L1_attn_Wq", "L1_attn_Wk", "L1_attn_Wv", "L1_attn_Wo",
        "L1_attn_gate", "L1_attn_log_temperature", "L1_ffn_w1", "L1_ffn_b1", "L1_ffn_w2", "L1_ffn_b2"]


def kernel(**inputs):
    import numpy as np
    from concourse import bacc
    from concourse.bass_utils import run_bass_kernel_spmd

    nc = bacc.Bacc("TRN2", target_bir_lowering=False, num_devices=1)
    arrays, args = {}, {}
    for name in _INS:
        v = np.ascontiguousarray(inputs[name])
        if v.ndim == 0:
            v = v.reshape(1, 1)
        arrays[name + "_in"] = v
        args[name] = nc.dram_tensor(name + "_in", v.shape, mybir.dt.from_np(v.dtype), kind="ExternalInput").ap()
    out = nc.dram_tensor("out", (B, S, D), F32, kind="ExternalOutput").ap()
    perceiver(nc, args, out)
    r = run_bass_kernel_spmd(nc, [arrays], core_ids=[0])
    return r.results[0]["out"]
```

```python
from contextlib import ExitStack, contextmanager

import concourse.bass as bass
from concourse import mybir

F32 = mybir.dt.float32
BF16 = mybir.dt.bfloat16
U32 = mybir.dt.uint32
ALU = mybir.AluOpType
ACT = mybir.ActivationFunctionType
AX = mybir.AxisListType

P = 128
D = 256
KT = D // P
B = 4
S = 256
QT = S // P
N = B * S
NT = N // P
S2 = 4096
CH = 512
TPC = CH // P
PAIRS = S2 // CH // 2
UNITS = 16
NEG = -1.0e30
LOWEST = -3.0e38
MAGIC = 12582912.0


class Ctx:

    def __init__(self, nc):
        self.nc = nc
        self.stack = None
        self.held = []

    def sem(self, name):
        self.held.append(self.stack.enter_context(self.nc.semaphore(name)))
        return self.held[-1]

    @contextmanager
    def stage(self):
        with ExitStack() as self.stack:
            yield
            with self.nc.Block() as block:
                @block.gpsimd
                def _(pool):
                    for held in self.held:
                        pool.sem_clear(held)
            self.held = []


def constants(c, ident, identb, ones, x_in, x_rows, tag):
    nc = c.nc
    cleared, made, copied = c.sem(tag + "cleared"), c.sem(tag + "made"), c.sem(tag + "copied")
    with nc.Block() as block:
        @block.gpsimd
        def _(pool):
            pool.memset(ident[:], 0.0).then_inc(cleared, 1)
            pool.memset(ones[:], 1.0).then_inc(cleared, 1)
            pool.wait_ge(cleared, 2)
            pool.affine_select(out=ident[:], in_=ident[:], compare_op=ALU.not_equal, fill=1.0, base=0,
                               pattern=[[-1, P]], channel_multiplier=1).then_inc(made, 1)
            pool.wait_ge(made, 1)
            pool.tensor_copy(identb[:], ident[:]).then_inc(made, 1)

        @block.sync
        def _(sp):
            sp.dma_start(x_rows.ap(), x_in.rearrange("b s d -> (b s) d")).then_inc(copied, 16)
            sp.wait_ge(copied, 16)


def layer_norm(c, x_rows, xn, xnT, ident, tag):
    nc = c.nc
    x_loaded, stats, root, normed = (c.sem(tag + n) for n in ("x_loaded", "stats", "root", "normed"))
    turned, kept = c.sem(tag + "turned"), c.sem(tag + "kept")
    with ExitStack() as s:
        x = s.enter_context(nc.sbuf_tensor(tag + "x", [P, NT, D], F32))
        st = s.enter_context(nc.sbuf_tensor(tag + "st", [P, NT, 6], F32))
        mv = s.enter_context(nc.sbuf_tensor(tag + "mv", [P, NT, 2], F32))
        var = s.enter_context(nc.sbuf_tensor(tag + "var", [P, NT], F32))
        std = s.enter_context(nc.sbuf_tensor(tag + "std", [P, NT], F32))
        r = s.enter_context(nc.sbuf_tensor(tag + "r", [P, 5, NT], F32))
        ps = [s.enter_context(nc.psum_tensor(f"{tag}ps{i}", [P, 512], F32)) for i in range(8)]
        block = s.enter_context(nc.Block())

        @block.sync
        def _(sp):
            sp.dma_start(x[:], x_rows.ap().rearrange("(t p) d -> p t d", p=P)).then_inc(x_loaded, 16)

        @block.vector
        def _(dve):
            dve.wait_ge(x_loaded, 16)
            for t in range(NT):
                dve.bn_stats(st[:, t, :], x[:, t, :]).then_inc(stats, 1)
            dve.wait_ge(stats, NT)
            for t in range(NT):
                dve.bn_aggr(mv[:, t, :], st[:, t, :]).then_inc(stats, 1)
            dve.wait_ge(stats, 2 * NT)
            dve.tensor_scalar(var[:], mv[:, :, 1], 1e-5, None, ALU.add).then_inc(stats, 1)
            dve.wait_ge(root, 1)
            dve.reciprocal(r[:, 0, :], std[:]).then_inc(stats, 1)
            dve.wait_ge(stats, 2 * NT + 2)
            dve.tensor_tensor(r[:, 1, :], r[:, 0, :], r[:, 0, :], ALU.mult).then_inc(stats, 1)
            dve.wait_ge(stats, 2 * NT + 3)
            dve.tensor_tensor(r[:, 2, :], r[:, 1, :], var[:], ALU.mult).then_inc(stats, 1)
            dve.wait_ge(stats, 2 * NT + 4)
            dve.tensor_scalar(r[:, 3, :], r[:, 2, :], -0.5, 1.5, ALU.mult, ALU.add).then_inc(stats, 1)
            dve.wait_ge(stats, 2 * NT + 5)
            dve.tensor_tensor(r[:, 4, :], r[:, 3, :], r[:, 0, :], ALU.mult).then_inc(stats, 1)
            dve.wait_ge(stats, 2 * NT + 6)
            for t in range(NT):
                dve.tensor_scalar(xn[:, t, :], x[:, t, :], mv[:, t, 0:1], r[:, 4, t:t + 1],
                                  ALU.subtract, ALU.mult).then_inc(normed, 1)

        @block.tensor
        def _(pe):
            for t in range(NT):
                pe.wait_ge(normed, t + 1)
                for k in range(KT):
                    mm = pe.transpose(ps[t][:, k * P:(k + 1) * P], xn[:, t, k * P:(k + 1) * P], ident[:])
                mm.then_inc(turned, 1)

        @block.scalar
        def _(act):
            act.wait_ge(stats, 2 * NT + 1)
            act.activation(std[:], var[:], ACT.Sqrt).then_inc(root, 1)
            for t in range(NT):
                act.wait_ge(turned, t + 1)
                act.activation(xnT[:, :, t * P:(t + 1) * P],
                               ps[t][:, 0:D].rearrange("p (k n) -> p k n", k=KT), ACT.Copy).then_inc(kept, 1)
            act.wait_ge(kept, NT)


def split_queries(c, xnT, w_q, b_q, scale, HD, qs, tag, prefetch=None, q_max=None):
    nc = c.nc
    G = HD // P
    w_loaded, q_ready, q_cut, q_left, q_stored = (c.sem(tag + n) for n in
                                                  ("w_loaded", "q_ready", "q_cut", "q_left", "q_stored"))
    with ExitStack() as s:
        w = s.enter_context(nc.sbuf_tensor(tag + "w", [P, KT, HD], F32))
        bias = s.enter_context(nc.sbuf_tensor(tag + "bias", [P, G], F32))
        q = s.enter_context(nc.sbuf_tensor(tag + "q", [P, G, N], F32))
        rest = s.enter_context(nc.sbuf_tensor(tag + "rest", [P, G, N], F32))
        parts = s.enter_context(nc.sbuf_tensor(tag + "parts", [P, 3, G, N], BF16))
        ps = [s.enter_context(nc.psum_tensor(f"{tag}ps{i}", [P, 512], F32)) for i in range(8)]
        block = s.enter_context(nc.Block())
        loads = 32 if b_q is not None else 16
        halves = N // 512

        @block.sync
        def _(sp):
            sp.dma_start(w[:], w_q.rearrange("(k p) n -> p k n", p=P)).then_inc(w_loaded, 16)
            if b_q is not None:
                sp.dma_start(bias[:], b_q.rearrange("(g p) -> p g", p=P),
                             allow_slow_non_contiguous=True).then_inc(w_loaded, 16)
            for i, part_of in enumerate((1, 3, 4)):
                sp.wait_ge(q_cut, part_of * G)
                sp.dma_start(qs.ap()[i].rearrange("(g p) n -> p g n", p=P), parts[:, i]).then_inc(q_stored, 16)
            sp.wait_ge(q_stored, 48)

        @block.tensor
        def _(pe):
            pe.wait_ge(w_loaded, loads)
            for g in range(G):
                for half in range(halves):
                    for k in range(KT):
                        mm = pe.matmul(ps[(g * halves + half) % 8][:], w[:, k, g * P:(g + 1) * P],
                                       xnT[:, k, half * 512:(half + 1) * 512], start=k == 0, stop=k == KT - 1)
                    mm.then_inc(q_ready, 1)

        @block.scalar
        def _(act):
            if prefetch is not None:
                prefetch(act)
            act.wait_ge(w_loaded, loads)
            for g in range(G):
                for half in range(halves):
                    act.wait_ge(q_ready, g * halves + half + 1)
                    act.activation(q[:, g, half * 512:(half + 1) * 512], ps[(g * halves + half) % 8][:],
                                   ACT.Identity, bias=bias[:, g:g + 1] if b_q is not None else 0.0).then_inc(q_left, 1)

        @block.vector
        def _(dve):
            dve.wait_ge(q_left, G * halves)
            for g in range(G):
                dve.tensor_scalar(parts[:, 0, g, :], q[:, g, :], scale, None, ALU.mult).then_inc(q_cut, 1)
            dve.wait_ge(q_cut, G)
            for g in range(G):
                dve.scalar_tensor_tensor(rest[:, g, :], q[:, g, :], scale, parts[:, 0, g, :],
                                         ALU.mult, ALU.subtract).then_inc(q_cut, 1)
            dve.wait_ge(q_cut, 2 * G)
            for g in range(G):
                dve.tensor_copy(parts[:, 1, g, :], rest[:, g, :]).then_inc(q_cut, 1)
            dve.wait_ge(q_cut, 3 * G)
            for g in range(G):
                dve.tensor_tensor(parts[:, 2, g, :], rest[:, g, :], parts[:, 1, g, :],
                                  ALU.subtract).then_inc(q_cut, 1)
            if q_max is not None:
                dve.tensor_reduce(q_max, q[:].rearrange("p g n -> p (g n)"), AX.X, ALU.max,
                                  apply_absolute_value=True).then_inc(q_cut, 1)


LAST = S2 - 2 * CH


def scale_mask(c, m, mask_in, lo, hi, short, bias_qk, bias_kq, ident, tag):
    nc = c.nc
    scaled, turned, kept, stored = (c.sem(tag + n) for n in ("scaled", "turned", "kept", "stored"))
    KEYS = (hi - lo) // P
    with ExitStack() as s:
        mT = s.enter_context(nc.sbuf_tensor(tag + "mT", [P, KEYS, S], F32))
        ps = [s.enter_context(nc.psum_tensor(f"{tag}ps{i}", [P, 512], F32)) for i in range(8)]
        block = s.enter_context(nc.Block())

        def where_needed(eng, run):
            if short is None:
                run()
            else:
                last_only = eng.value_load(short[0:1, 0:1], min_val=0, max_val=1)
                with eng.If(last_only == 0):
                    run()

        @block.sync
        def _(sp):
            def run():
                sp.wait_ge(scaled, QT)
                sp.dma_start(bias_qk.ap()[:, lo:hi].rearrange("(i p) k -> p i k", p=P), m[:, :, lo:hi]).then_inc(stored, 16)
                sp.wait_ge(kept, KEYS // 2)
                sp.dma_start(bias_kq.ap()[lo:hi].rearrange("(t p) q -> p t q", p=P), mT[:]).then_inc(stored, 16)
                sp.wait_ge(stored, 32)

            where_needed(sp, run)

        @block.vector
        def _(dve):
            def run():
                dve.wait_ge(mask_in, 16)
                for i in range(QT):
                    dve.tensor_scalar(m[:, i, lo:hi], m[:, i, lo:hi], -1.0e9, None, ALU.mult).then_inc(scaled, 1)

            where_needed(dve, run)

        @block.tensor
        def _(pe):
            def run():
                pe.wait_ge(scaled, QT)
                for t in range(KEYS):
                    if t % 2 == 0 and t >= 16:
                        pe.wait_ge(kept, t // 2 - 7)
                    for i in range(QT):
                        at = (t % 2) * S + i * P
                        mm = pe.transpose(ps[t // 2 % 8][:, at:at + P], m[:, i, lo + t * P:lo + (t + 1) * P], ident[:])
                    mm.then_inc(turned, 1)

            where_needed(pe, run)

        @block.scalar
        def _(act):
            def run():
                for t in range(0, KEYS, 2):
                    act.wait_ge(turned, t + 2)
                    act.activation(mT[:, t:t + 2, :], ps[t // 2 % 8][:].rearrange("p (t q) -> p t q", t=2),
                                   ACT.Copy).then_inc(kept, 1)

            where_needed(act, run)


def survey(c, m, mask_in, lead, lead_in, w_k, b_k, q_max, dh, short, ident, tag):
    nc = c.nc
    w_in, step, turned = c.sem(tag + "w_in"), c.sem(tag + "step"), c.sem(tag + "turned")
    with ExitStack() as s:
        def sb(n, shape, dt=F32):
            return s.enter_context(nc.sbuf_tensor(tag + n, shape, dt))

        wk, bk = sb("wk", [P, KT * D]), sb("bk", [1, D])
        low, part, pack, most, row, term = (sb("low", [P, 2 * QT]), sb("part", [P, B]), sb("pack", [P, 8]),
                                            sb("most", [8, 1]), sb("row", [1, 8]), sb("term", [1, 8]))
        ps = [s.enter_context(nc.psum_tensor(f"{tag}ps{i}", [P, 512], F32)) for i in range(2)]
        block = s.enter_context(nc.Block())

        @block.sync
        def _(sp):
            sp.dma_start(wk[:].rearrange("p (k n) -> p k n", k=KT), w_k.rearrange("(k p) n -> p k n", p=P)).then_inc(w_in, 16)
            sp.dma_start(bk[:], b_k.rearrange("(a n) -> a n", a=1)).then_inc(w_in, 16)

        @block.tensor
        def _(pe):
            pe.wait_ge(step, 4)
            pe.transpose(ps[0][0:8, 0:P], pack[:], ident[:]).then_inc(turned, 1)
            pe.wait_ge(step, 5)
            pe.transpose(ps[1][0:1, 0:8], most[:], ident[0:8, 0:8]).then_inc(turned, 1)

        @block.vector
        def _(dve):
            dve.memset(pack[:], 0.0).then_inc(step, 1)
            dve.wait_ge(step, 1)
            dve.wait_ge(w_in, 32)
            dve.wait_ge(mask_in, 16)
            dve.tensor_copy(pack[:, 3:4], q_max)
            dve.tensor_reduce(pack[:, 4:5], wk[:], AX.X, ALU.max, apply_absolute_value=True)
            dve.tensor_reduce(pack[0:1, 5:6], bk[:], AX.X, ALU.max, apply_absolute_value=True)
            dve.tensor_reduce(low[:, 0:QT], m[:, :, 0:LAST], AX.X, ALU.min)
            dve.tensor_reduce(low[:, QT:2 * QT], m[:, :, LAST:S2], AX.X, ALU.max)
            for b in range(B):
                dve.wait_ge(lead_in[b], 16)
                ins = dve.tensor_reduce(part[:, b:b + 1], lead[b][:], AX.X, ALU.max, apply_absolute_value=True)
            ins.then_inc(step, 1)
            dve.wait_ge(step, 2)
            dve.tensor_reduce(pack[:, 0:1], low[:, 0:QT], AX.X, ALU.min)
            dve.tensor_reduce(pack[:, 1:2], low[:, QT:2 * QT], AX.X, ALU.min)
            dve.tensor_reduce(pack[:, 2:3], part[:], AX.X, ALU.max).then_inc(step, 1)
            dve.wait_ge(step, 3)
            dve.tensor_scalar(pack[:, 0:2], pack[:, 0:2], -1.0, None, ALU.mult).then_inc(step, 1)
            dve.wait_ge(turned, 1)
            dve.tensor_reduce(most[:], ps[0][0:8, 0:P], AX.X, ALU.max).then_inc(step, 1)
            dve.wait_ge(turned, 2)
            dve.tensor_copy(row[:], ps[1][0:1, 0:8]).then_inc(step, 1)
            dve.wait_ge(step, 6)
            dve.scalar_tensor_tensor(term[:, 0:1], row[:, 2:3], float(D), row[:, 4:5], ALU.mult, ALU.mult).then_inc(step, 1)
            dve.wait_ge(step, 7)
            dve.tensor_tensor(term[:, 1:2], term[:, 0:1], row[:, 5:6], ALU.add).then_inc(step, 1)
            dve.wait_ge(step, 8)
            dve.scalar_tensor_tensor(term[:, 2:3], term[:, 1:2], float(dh), row[:, 3:4], ALU.mult, ALU.mult).then_inc(step, 1)
            dve.wait_ge(step, 9)
            dve.tensor_scalar(term[:, 3:4], row[:, 0:1], -1.0, None, ALU.is_le)
            dve.tensor_scalar(term[:, 4:5], row[:, 1:2], 0.0, None, ALU.is_le)
            dve.tensor_scalar(term[:, 5:6], term[:, 2:3], 1.0e8, None, ALU.is_le).then_inc(step, 1)
            dve.wait_ge(step, 10)
            dve.tensor_tensor(term[:, 6:7], term[:, 3:4], term[:, 4:5], ALU.mult).then_inc(step, 1)
            dve.wait_ge(step, 11)
            dve.tensor_tensor(short[:], term[:, 6:7], term[:, 5:6], ALU.mult).then_inc(step, 1)
            dve.wait_ge(step, 12)


def cross_attention(c, H, ctx, w_k, b_k, w_v, qs, k_rows, v_rows, o_rows, sum_rows, bias_qk, bias_kq, short,
                    first_in, ident, ones, tag):
    nc = c.nc
    masked = bias_qk is not None
    small = H == 16
    dh = 16 if small else 64
    HD = H * dh
    G = HD // P
    VW = dh + 1 if small else dh
    HV = H * VW
    VU = G
    TPV = TPC // VU
    UM = H * QT
    SETS = H * TPC // 4
    HS = 4 if small else 2
    TS = 4 // HS
    SLOT_K, SLOT_Q = (0, 0, 1, 1, 0, 2), (0, 1, 0, 1, 2, 0)
    KQ = 6 * dh if small else P
    STEPS = "tkkvv" if small else "tkkvkvkvv"
    ACT_STEPS = "kksvsv" if small else "kksvskvskvsv"
    POOL_STEPS = "rrtt" if small else "rrttrtrt"
    NPARTS = 3 if small else 2
    ND = 6 if small else 4
    NDQ = 6 if small else 8
    NDO = 1 if small else 2
    ONE, M0, S0 = 16, 2 * UM, 2 * SETS

    def sem(n):
        return c.sem(tag + n)

    w_loaded, ones_set, ones_put = sem("w_loaded"), sem("ones_set"), sem("ones_put")
    ctx_in, q_in, max_in, o_out, k_out = sem("ctx_in"), sem("q_in"), sem("max_in"), sem("o_out"), sem("k_out")
    bias_in, v_out, v_in, biasT_in = ([sem(f"{n}{u}") for u in range(2)] for n in
                                      ("bias_in", "v_out", "v_in", "biasT_in"))
    keys_in = [[sem(f"keys_in{u}{half}") for half in range(2)] for u in range(2)]
    ctx_turned, ctxT_kept = sem("ctx_turned"), sem("ctxT_kept")
    k_made, k_kept, k_half, k_rest, k_cut2, k_cut3 = (sem(n) for n in
                                                      ("k_made", "k_kept", "k_half", "k_rest", "k_cut2", "k_cut3"))
    v_made, v_kept = sem("v_made"), sem("v_kept")
    scored, reduced, folded, best_reset = sem("scored"), sem("reduced"), sem("folded"), sem("best_reset")
    negated, max_turned, max_cut, acc_reset = sem("negated"), sem("max_turned"), sem("max_cut"), sem("acc_reset")
    out_reset, set_scored, biased, probs, used = (sem(n) for n in ("out_reset", "set_scored", "biased", "probs", "used"))
    summed, sums_made, o_kept = sem("summed"), sem("sums_made"), sem("o_kept")

    LOADS = 32 if b_k is None else 48

    def choose(eng, run):
        if short is None:
            run(0)
        else:
            last_only = eng.value_load(short[0:1, 0:1], min_val=0, max_val=1)
            with eng.If(last_only == 1):
                run(PAIRS - 1)
            with eng.Else():
                run(0)

    settled = {n: sem("settled_" + n) for n in ("sp", "dve", "pe", "pool")}

    def settle(eng, n):
        eng.sem_inc(settled[n], 1)

    with ExitStack() as s:
        def sb(n, shape, dt=F32):
            return s.enter_context(nc.sbuf_tensor(tag + n, shape, dt))

        keys = sb("keys", [P, PAIRS, 2 * UNITS, CH], BF16)
        query = sb("query", [P, H if small else 3 * H, S], BF16)
        ctx_sb = sb("ctx_sb", [P, TPC, D])
        ctxT = sb("ctxT", [P, KT, CH])
        work = sb("work", [P, 4096])
        value = [sb(f"value{u}", [P, TPC, HV]) for u in range(2)]
        v_stage = [sb(f"v_stage{u}", [P, TPV, H, VW]) for u in range(2)]
        wk, wv = sb("wk", [P, KT, HD]), sb("wv", [P, KT, HD])
        bk = sb("bk", [P, G])
        best, best_c, neg = sb("best", [P, UM]), sb("best_c", [P, UM]), sb("neg", [P, UM])
        neg_rest, neg_parts = sb("neg_rest", [UM, P]), sb("neg_parts", [UM, 3, P], BF16)
        if masked:
            bias = [sb(f"bias{u}", [P, QT, CH]) for u in range(2)]
            biasT = [sb(f"biasT{u}", [P, TPC, S]) for u in range(2)]
            junk = [sb(f"junk{u}", [P, CH], BF16) for u in range(2)]
        if not small:
            shift, onesb = sb("shift", [P, H, S], BF16), sb("onesb", [P, P], BF16)
            acc = sb("acc", [P, H, S])
        kf = [work[:, g * CH:(g + 1) * CH] for g in range(2)]
        rest = [work[:, (2 + g) * CH:(3 + g) * CH] for g in range(2)]
        kparts = work[:, 2048:4096].bitcast(BF16)[:, 0:NPARTS * G * CH].rearrange("p (i g n) -> p i g n", i=NPARTS, g=G)
        out_sb = value[0][:].rearrange("p t c -> p (t c)")[:, 0:1024]
        sum_sb = None if small else value[0][:].rearrange("p t c -> p (t c)")[:, 1024:2048]
        slot = [work[:, i * 1024:(i + 1) * 1024] for i in range(4)]
        bank = [s.enter_context(nc.psum_tensor(f"{tag}bank{i}", [P, 512], F32)) for i in range(4)]
        duo = [s.enter_context(nc.psum_tensor(f"{tag}duo{i}", [P, 1024], F32)) for i in range(2)]
        quad = [duo[i // 2][:, i % 2 * 512:i % 2 * 512 + 512] for i in range(4)]
        block = s.enter_context(nc.Block())

        @block.sync
        def _(sp):
            sp.dma_start(wk[:], w_k.rearrange("(k p) n -> p k n", p=P)).then_inc(w_loaded, 16)
            sp.dma_start(wv[:], w_v.rearrange("(k p) n -> p k n", p=P)).then_inc(w_loaded, 16)
            if b_k is not None:
                sp.dma_start(bk[:], b_k.rearrange("(g p) -> p g", p=P),
                             allow_slow_non_contiguous=True).then_inc(w_loaded, 16)
            for half in range(2):
                sp.sem_inc(keys_in[1][half], ONE)
            sp.sem_inc(o_out, ONE)
            sp.sem_inc(v_out[0], ONE)
            sp.sem_inc(v_out[1], ONE)
            def run(lo):
                PAIRS_RUN = PAIRS - lo
                CHUNKS = 2 * PAIRS_RUN
                if small:
                    sp.wait_ge(ones_set, 1)
                    for p in range(lo, PAIRS):
                        for u in range(4):
                            sp.dma_start(keys[KQ:KQ + 3, p, u * 8:(u + 1) * 8, :],
                                         work[KQ:KQ + 3, 0:2048].bitcast(BF16).rearrange("p (a n) -> p a n", a=8)
                                         ).then_inc(ones_put, 16)
                with sp.Fori(0, B) as b:
                    sp.wait_ge(o_kept, b + ONE)
                    mine = bass.ds(b * S, S)
                    if small:
                        for i, part in enumerate(SLOT_Q):
                            sp.dma_start(query[i * dh:(i + 1) * dh, :, :],
                                         qs.ap()[part, :, mine].rearrange("(h d) q -> d h q", d=dh)).then_inc(q_in, 16)
                    else:
                        for part in range(2):
                            for row in (0, dh):
                                sp.dma_start(query[row:row + dh, part * H:(part + 1) * H, :],
                                             qs.ap()[part, :, mine].rearrange("(h d) q -> d h q", d=dh)).then_inc(q_in, 16)
                        for odd in range(2):
                            for top, part in ((0, 0 if odd else 2), (dh, 2 if odd else 0)):
                                sp.dma_start(query[top:top + dh, 2 * H + odd:3 * H:2, :],
                                             qs.ap()[part, :, mine].rearrange("(h o d) q -> o d h q", d=dh, o=2)[odd]
                                             ).then_inc(q_in, 16)

                    def load_bias(p, u):
                        if masked:
                            sp.wait_ge(reduced, (b * CHUNKS + (p - lo) * 2) * UM + (u * UM - UM + M0))
                            settle(sp, "sp")
                            sp.dma_start(bias[u][:], bias_qk.ap()[:, bass.ds(p * 2 * CH + u * CH, CH)]
                                         .rearrange("(i q) k -> q i k", q=P)).then_inc(bias_in[u], 16)

                    def store_chunk(p, u):
                        n = b * CHUNKS + (p - lo) * 2

                        def store_values(v):
                            sp.wait_ge(v_kept, n * VU + (u * VU + v + 1 + ONE))
                            rows = bass.ds(b * S2 + p * 2 * CH + (u * CH + v * TPV * P), TPV * P)
                            sp.dma_start(v_rows.ap()[rows, :].rearrange("(t k) c -> k t c", k=P),
                                         v_stage[v % 2][:].rearrange("p t h w -> p t (h w)")).then_inc(v_out[v % 2], 16)

                        def store_keys(half):
                            gs = slice(half * G // 2, (half + 1) * G // 2)
                            sp.wait_ge(k_cut2, n * G + u * G + gs.stop)
                            sp.wait_ge(k_cut3, n * G + u * G + gs.stop)
                            if small:
                                rows = k_rows.ap()[u, :, half * P:(half + 1) * P, :]
                                sp.dma_start(rows.rearrange("i k n -> k i n"), kparts[:, :, half]).then_inc(k_out, 16)
                                sp.wait_ge(k_out, n * 32 + (u * 32 + half * 16 + 16))
                                at = u * UNITS + half * 8
                                for i, part in enumerate(SLOT_K):
                                    sp.dma_start(keys[i * dh:(i + 1) * dh, bass.ds(p, 1), at:at + 8, :]
                                                 .rearrange("d p h n -> d (p h) n"),
                                                 rows[part].rearrange("(h d) n -> d h n", d=dh)).then_inc(keys_in[u][half], 16)
                            else:
                                for part in range(2):
                                    for odd in range(2):
                                        to, at = dh * (1 - odd), u * UNITS + half * 8 + 2 * odd + part
                                        sp.dma_start(keys[to:to + dh, bass.ds(p, 1), at:u * UNITS + half * 8 + 8:4, :]
                                                     .rearrange("d p h n -> d (p h) n"),
                                                     kparts[dh * odd:dh * odd + dh, part, gs]).then_inc(keys_in[u][half], 16)

                        store_keys(0)
                        for v in range(VU - 2):
                            store_values(v)
                        store_keys(1)
                        for v in range(VU - 2, VU):
                            store_values(v)

                    load_bias(lo, 0)
                    if lo < PAIRS - 1:
                        with sp.Fori(lo, PAIRS - 1) as p:
                            store_chunk(p, 0)
                            load_bias(p, 1)
                            store_chunk(p, 1)
                            load_bias(p + 1, 0)
                    store_chunk(PAIRS - 1, 0)
                    load_bias(PAIRS - 1, 1)
                    store_chunk(PAIRS - 1, 1)
                    sp.wait_ge(max_cut, b * 4 + 4)
                    for i in range(3):
                        row = query[KQ + i:KQ + i + 1] if small else shift[i:i + 1]
                        sp.dma_start(row.rearrange("o h (i q) -> o (h i) q", i=QT), neg_parts[:, i, :]).then_inc(max_in, 16)
                    for i in range(2):
                        sp.wait_ge(v_out[i], b * (CHUNKS * VU * 8) + (CHUNKS * VU * 8 + ONE))
                    sp.wait_ge(o_out, b * (NDO * 16) + ONE)
                    settle(sp, "sp")
                    with sp.Fori(lo, PAIRS) as p:
                        n = b * CHUNKS + (p - lo) * 2
                        for u in range(2):
                            sp.wait_ge(used, n * SETS + (u * SETS - SETS + S0))
                            rows = bass.ds(b * S2 + p * 2 * CH + u * CH, CH)
                            sp.dma_start(value[u][:], v_rows.ap()[rows, :].rearrange("(t k) c -> k t c", k=P)).then_inc(v_in[u], 16)
                            if masked:
                                sp.dma_start(biasT[u][:], bias_kq.ap()[bass.ds(p * 2 * CH + u * CH, CH), :]
                                             .rearrange("(t k) q -> k t q", k=P)).then_inc(biasT_in[u], 16)
                    sp.wait_ge(o_kept, b + 1 + ONE)
                    sp.dma_start(o_rows.ap()[bass.ds(b, 1)].rearrange("b p n -> (b p) n"), out_sb).then_inc(o_out, 16)
                    if not small:
                        sp.dma_start(sum_rows.ap()[bass.ds(b, 1)].rearrange("b p n -> (b p) n"), sum_sb).then_inc(o_out, 16)

            choose(sp, run)
            sp.wait_ge(o_out, B * NDO * 16 + ONE)

        @block.gpsimd
        def _(pool):
            if small:
                pool.memset(work[96:128, 0:2048].bitcast(BF16), 1.0).then_inc(ones_set, 1)
                for u in range(2):
                    pool.wait_ge(ones_set, u + 1)
                    pool.memset(v_stage[u][:], 1.0).then_inc(ones_set, 1)
            else:
                pool.memset(onesb[:], 1.0).then_inc(ones_set, 1)
                pool.wait_ge(ones_set, 1)
                pool.memset(shift[:], 0.0).then_inc(ones_set, 1)
            pool.sem_inc(k_rest, ONE)
            def run(lo):
                PAIRS_RUN = PAIRS - lo
                CHUNKS = 2 * PAIRS_RUN
                with pool.Fori(0, B) as b:
                    pool.wait_ge(ctx_turned, b * CHUNKS + ONE)
                    pool.dma_start(ctx_sb[:], ctx[bass.ds(b, 1), lo * 2 * CH:lo * 2 * CH + CH, :]
                                   .rearrange("b (t k) c -> k (b t) c", k=P)).then_inc(first_in, 16)
                    if not small:
                        pool.wait_ge(o_kept, b + ONE)
                        settle(pool, "pool")
                        pool.memset(acc[:], 0.0).then_inc(acc_reset, 1)
                        pool.wait_ge(acc_reset, b + 1)
                        settle(pool, "pool")
                    with pool.Fori(lo, PAIRS) as p:
                        for u in range(2):
                            m = (b * CHUNKS + (p - lo) * 2) * G + u * G

                            def finished(before):
                                step, g = before
                                if not small and step == "r":
                                    pool.wait_ge(k_rest, m + (g + 1 + ONE))
                                elif not small:
                                    pool.wait_ge(k_cut3, m + (g + 1))

                            def first_rest(g):
                                pool.wait_ge(k_kept, m + (g + 1 + ONE))
                                if small:
                                    pool.tensor_tensor(rest[g % 2], kf[g % 2], kparts[:, 0, g], ALU.subtract).then_inc(k_rest, 1)
                                else:
                                    even, odd = slice(0, dh), slice(dh, P)
                                    pool.tensor_tensor(rest[g % 2][even], kf[g % 2][even],
                                                       keys[even, bass.ds(p, 1), u * UNITS + 4 * g, :].rearrange("d p n -> d (p n)"),
                                                       ALU.subtract).then_inc(k_half, 1)
                                    pool.wait_ge(k_half, m + (g + 1))
                                    pool.tensor_tensor(rest[g % 2][odd], kf[g % 2][odd],
                                                       keys[odd, bass.ds(p, 1), u * UNITS + 4 * g + 2, :].rearrange("d p n -> d (p n)"),
                                                       ALU.subtract).then_inc(k_rest, 1)

                            def third_part(g):
                                pool.wait_ge(k_cut2, m + (g + 1))
                                pool.tensor_tensor(kparts[:, NPARTS - 1, g], rest[g % 2], kparts[:, NPARTS - 2, g],
                                                   ALU.subtract).then_inc(k_cut3, 1)

                            for x, step in enumerate(POOL_STEPS):
                                if x > 0:
                                    finished((POOL_STEPS[x - 1], POOL_STEPS[:x - 1].count(POOL_STEPS[x - 1])))
                                if step == "r":
                                    first_rest(POOL_STEPS[:x].count(step))
                                else:
                                    third_part(POOL_STEPS[:x].count(step))
                            finished(("t", G - 1))

            choose(pool, run)

        @block.scalar
        def _(act):
            act.sem_inc(k_kept, ONE)
            act.sem_inc(v_kept, ONE)
            act.sem_inc(o_kept, ONE)
            if not masked:
                act.sem_inc(probs, S0)
            act.wait_ge(w_loaded, LOADS)
            act.wait_ge(ones_set, 3 if small else 2)
            def run(lo):
                PAIRS_RUN = PAIRS - lo
                CHUNKS = 2 * PAIRS_RUN
                if small:
                    act.wait_ge(ones_put, PAIRS_RUN * 4 * 16)
                with act.Fori(0, B) as b:
                    def make_pair(p, last):
                        for u in range(2):
                            n = b * CHUNKS + (p - lo) * 2

                            def kparts_free(g):
                                done = b * PAIRS_RUN + (p - lo)
                                if g % (G // 2) == 0:
                                    before = keys_in[1 - u][g // (G // 2)]
                                    act.wait_ge(before, done * (ND * 16) + (ND * 16 if u == 1 else ONE))

                            def second_part(g):
                                if not small:
                                    kparts_free(g)
                                act.wait_ge(k_rest, n * G + (u * G + g + 1 + ONE))
                                act.activation(kparts[:, NPARTS - 2, g], rest[g % 2], ACT.Copy).then_inc(k_cut2, 1)

                            act.wait_ge(ctx_turned, n + (u + 1 + ONE))
                            if u == 0 or not last:
                                nxt = (p * 2 + u + 1) * CH
                                act.dma_start(ctx_sb[:], ctx[bass.ds(b, 1), bass.ds(nxt, CH), :]
                                              .rearrange("b (t k) c -> k (b t) c", k=P)).then_inc(ctx_in, 16)

                            for k in range(KT):
                                ins = act.activation(ctxT[:, k, :], bank[k][:], ACT.Copy)
                            ins.then_inc(ctxT_kept, 1)

                            def keep_keys(g):
                                act.wait_ge(k_made, n * G + (u * G + g + 1))
                                act.wait_ge(k_rest, n * G + (u * G + g - 1 + ONE))
                                shifted = bk[:, g:g + 1] if b_k is not None else 0.0
                                act.activation(kf[g % 2], bank[2 + g % 2][:], ACT.Identity, bias=shifted)
                                if small:
                                    kparts_free(g)
                                    act.activation(kparts[:, 0, g], bank[2 + g % 2][:], ACT.Identity,
                                                   bias=shifted).then_inc(k_kept, 1)
                                else:
                                    for odd in range(2):
                                        rows = slice(odd * dh, odd * dh + dh)
                                        for slab in range(2):
                                            at = u * UNITS + 4 * g + 2 * odd + slab
                                            ins = act.activation(keys[rows, bass.ds(p, 1), at, :].rearrange("d p n -> d (p n)"),
                                                                 bank[2 + g % 2][rows, :], ACT.Copy)
                                    ins.then_inc(k_kept, 1)

                            def keep_values(v):
                                act.wait_ge(v_made, n * VU + (u * VU + v + 1))
                                act.wait_ge(v_out[v % 2], n * (VU * 8) + ((u * VU // 2 + v // 2) * 16 + ONE))
                                act.activation(v_stage[v % 2][:, :, :, 0:dh],
                                               bank[v % 2][:].rearrange("p (t h w) -> p t h w", t=TPV, h=H),
                                               ACT.Copy).then_inc(v_kept, 1)

                            for x, step in enumerate(ACT_STEPS):
                                g = ACT_STEPS[:x].count(step)
                                if step == "k":
                                    keep_keys(g)
                                elif step == "v":
                                    keep_values(g)
                                else:
                                    second_part(g)

                    if lo < PAIRS - 1:
                        with act.Fori(lo, PAIRS - 1) as p:
                            make_pair(p, False)
                    make_pair(PAIRS - 1, True)
                    with act.Fori(lo, PAIRS) as p:
                        for i in range(2 * SETS):
                            m = (b * CHUNKS + (p - lo) * 2) * SETS
                            if masked:
                                act.wait_ge(biased, m + (i + 1 + S0))
                                act.activation(slot[i % 4], slot[i % 4], ACT.Exp).then_inc(probs, 1)
                            else:
                                act.wait_ge(set_scored, m + (i + 1))
                                act.wait_ge(used, m + (i - 3 + S0))
                                act.wait_ge(summed, m * TS + ((i - 3) * TS + S0))
                                act.activation(slot[i % 4], duo[i % 2][:], ACT.Exp).then_inc(probs, 1)
                    act.wait_ge(used, b * (CHUNKS * SETS) + (CHUNKS * SETS + S0))
                    if not small:
                        act.wait_ge(sums_made, b + 1)
                    act.activation(out_sb[:, 0:512], bank[0][:], ACT.Copy)
                    ins = act.activation(out_sb[:, 512:1024], bank[1][:], ACT.Copy)
                    if not small:
                        act.activation(sum_sb[:, 0:512], bank[2][:], ACT.Copy)
                        ins = act.activation(sum_sb[:, 512:1024], bank[3][:], ACT.Copy)
                    ins.then_inc(o_kept, 1)

            choose(act, run)

        @block.vector
        def _(dve):
            dve.sem_inc(reduced, M0)
            if masked:
                dve.sem_inc(biased, S0)
            if not small:
                dve.sem_inc(summed, S0)
            def run(lo):
                PAIRS_RUN = PAIRS - lo
                CHUNKS = 2 * PAIRS_RUN
                with dve.Fori(0, B) as b:
                    dve.memset(best[:], LOWEST).then_inc(best_reset, 1)
                    dve.wait_ge(best_reset, b + 1)
                    settle(dve, "dve")
                    with dve.Fori(lo, PAIRS) as p:
                        for u in range(2):
                            n = b * CHUNKS + (p - lo) * 2
                            if masked:
                                dve.wait_ge(bias_in[u], (b * PAIRS_RUN + (p - lo)) * 16 + 16)
                            for i in range(UM):
                                dve.wait_ge(scored, n * UM + (u * UM + i + 1))
                                if masked:
                                    dve.wait_ge(reduced, n * UM + (u * UM + i - 1 + M0))
                                    settle(dve, "dve")
                                    dve.tensor_tensor_reduce(junk[i % 2][:], quad[i % 4], bias[u][:, i % QT, :], 1.0, LOWEST,
                                                             ALU.add, ALU.max, best_c[:, i:i + 1]).then_inc(reduced, 1)
                                else:
                                    dve.tensor_reduce(best_c[:, i:i + 1], quad[i % 4], AX.X, ALU.max).then_inc(reduced, 1)
                            dve.wait_ge(reduced, n * UM + (u * UM + UM + M0))
                            dve.tensor_tensor(best[:], best[:], best_c[:], ALU.max).then_inc(folded, 1)
                            dve.wait_ge(folded, n + (u + 1))
                    dve.tensor_scalar(neg[:], best[:], -1.0, None, ALU.mult).then_inc(negated, 1)
                    dve.wait_ge(v_kept, b * (CHUNKS * VU) + (CHUNKS * VU + ONE))
                    dve.memset(bank[0][:], 0.0)
                    dve.memset(bank[1][:], 0.0).then_inc(out_reset, 1)
                    dve.wait_ge(max_turned, b + 1)
                    dve.tensor_copy(neg_parts[:, 0, :], quad[0][0:UM, 0:P]).then_inc(max_cut, 1)
                    dve.wait_ge(max_cut, b * 4 + 1)
                    dve.tensor_tensor(neg_rest[:], quad[0][0:UM, 0:P], neg_parts[:, 0, :], ALU.subtract).then_inc(max_cut, 1)
                    dve.wait_ge(max_cut, b * 4 + 2)
                    dve.tensor_copy(neg_parts[:, 1, :], neg_rest[:]).then_inc(max_cut, 1)
                    dve.wait_ge(max_cut, b * 4 + 3)
                    dve.tensor_tensor(neg_parts[:, 2, :], neg_rest[:], neg_parts[:, 1, :], ALU.subtract).then_inc(max_cut, 1)
                    dve.wait_ge(out_reset, b + 1)
                    if not small:
                        dve.wait_ge(acc_reset, b + 1)
                    settle(dve, "dve")
                    with dve.Fori(lo, PAIRS) as p:
                        m = (b * CHUNKS + (p - lo) * 2) * SETS
                        for i in range(2 * SETS):
                            u, at = i // SETS, i % SETS
                            if masked:
                                if at == 0:
                                    dve.wait_ge(biasT_in[u], (b * PAIRS_RUN + (p - lo)) * 16 + 16)
                                dve.wait_ge(set_scored, m + (i + 1))
                                dve.wait_ge(used, m + (i - 3 + S0))
                                dve.tensor_tensor(slot[i % 4].rearrange("p (h q) -> p h q", h=HS),
                                                  duo[i % 2][:].rearrange("p (h q) -> p h q", h=HS),
                                                  biasT[u][:, at // 4:at // 4 + 1, :].broadcast_to([P, HS, S]),
                                                  ALU.add).then_inc(biased, 1)
                            elif not small:
                                pair = at // 2
                                dve.wait_ge(probs, m + (i + 1 + S0))
                                for t in range(TS):
                                    dve.wait_ge(summed, m * TS + (i * TS + t + S0))
                                    both = acc[:, 2 * pair:2 * pair + 2, :].rearrange("p h q -> p (h q)")
                                    dve.tensor_tensor(both, both, slot[i % 4][:, t * 512:(t + 1) * 512],
                                                      ALU.add).then_inc(summed, 1)

            choose(dve, run)

        @block.tensor
        def _(pe):
            pe.sem_inc(ctx_turned, ONE)
            pe.sem_inc(used, S0)
            pe.wait_ge(w_loaded, LOADS)
            if not small:
                pe.wait_ge(ones_set, 2)
            PS0 = 0 if masked else S0

            def run(lo):
                PAIRS_RUN = PAIRS - lo
                CHUNKS = 2 * PAIRS_RUN
                with pe.Fori(0, B) as b:
                    def counted(p):
                        return b * CHUNKS + (p - lo) * 2

                    def turn(p, u):
                        n = counted(p)
                        if u == 0 and isinstance(p, int) and p == lo:
                            pe.wait_ge(first_in, b * 16 + 16)
                        else:
                            pe.wait_ge(ctx_in, b * ((CHUNKS - 1) * 16) + ((p - lo) * 32 + u * 16))
                        pe.wait_ge(v_kept, n * VU + (u * VU + ONE))
                        for k in range(KT):
                            for t in range(TPC):
                                mm = pe.transpose(bank[k][:, t * P:(t + 1) * P], ctx_sb[:, t, k * P:(k + 1) * P], ident[:])
                        mm.then_inc(ctx_turned, 1)

                    def make_keys(p, u, g):
                        n = counted(p)
                        pe.wait_ge(ctxT_kept, n + (u + 1))
                        pe.wait_ge(k_kept, n * G + (u * G + g - 1 + ONE))
                        for k in range(KT):
                            mm = pe.matmul(bank[2 + g % 2][:], wk[:, k, g * P:(g + 1) * P], ctxT[:, k, :],
                                           start=k == 0, stop=k == KT - 1)
                        mm.then_inc(k_made, 1)

                    def make_values(p, u, v):
                        n = counted(p)
                        if v >= 2:
                            pe.wait_ge(v_kept, n * VU + (u * VU + v - 1 + ONE))
                        for t in range(TPV):
                            for k in range(KT):
                                at = (v * TPV + t) * P
                                mm = pe.matmul(bank[v % 2][:, t * HD:(t + 1) * HD], ctxT[:, k, at:at + P], wv[:, k, :],
                                               start=k == 0, stop=k == KT - 1)
                        mm.then_inc(v_made, 1)

                    def score(p, u, i):
                        n = counted(p)
                        h, q = i // QT, slice(i % QT * P, i % QT * P + P)
                        if i % (UM // 2) == 0:
                            half = i // (UM // 2)
                            pe.wait_ge(keys_in[u][half], (b * PAIRS_RUN + (p - lo)) * (ND * 16) + (ND * 16 + ONE * u))
                            pe.wait_ge(k_kept, n * G + (u * G + (half + 1) * G // 2 + ONE))
                        pe.wait_ge(reduced, n * UM + (u * UM + i - 3 + M0))
                        if small:
                            mm = pe.matmul(quad[i % 4], query[0:KQ, h, q],
                                           keys[0:KQ, bass.ds(p, 1), u * UNITS + h, :].rearrange("k p n -> k (p n)"),
                                           start=True, stop=True)
                        else:
                            for x, (tile, slab) in enumerate(((0, 0), (1, 0), (2, 1))):
                                mm = pe.matmul(quad[i % 4], query[:, tile * H + h, q],
                                               keys[:, bass.ds(p, 1), u * UNITS + 2 * h + slab, :].rearrange("k p n -> k (p n)"),
                                               start=x == 0, stop=x == 2)
                        mm.then_inc(scored, 1)

                    GAP = 2 if small else 1
                    EARLY = 3

                    def make(p, u, first, last):
                        for x in range(first, min(last, len(STEPS))):
                            g = STEPS[:x].count(STEPS[x])
                            if STEPS[x] == "t":
                                turn(p, u)
                            elif STEPS[x] == "k":
                                make_keys(p, u, g)
                            else:
                                make_values(p, u, g)

                    def score_chunk(p, u, after, later):
                        for i in range(UM):
                            score(p, u, i)
                            if after is not None and i % GAP == 0 and i < 10 * GAP:
                                x = EARLY + i // GAP
                                make(*after, x, x + 1)
                            if later is not None and i >= 10 * GAP and i % (2 * GAP) == 0:
                                x = i // (2 * GAP) - 5
                                make(*later, x, x + 1)

                    make(lo, 0, 0, len(STEPS))
                    make(lo, 1, 0, EARLY)
                    pe.wait_ge(q_in, b * (NDQ * 16) + NDQ * 16)
                    settle(pe, "pe")
                    if lo < PAIRS - 1:
                        with pe.Fori(lo, PAIRS - 1) as p:
                            score_chunk(p, 0, (p, 1), (p + 1, 0))
                            score_chunk(p, 1, (p + 1, 0), (p + 1, 1))
                    score_chunk(PAIRS - 1, 0, (PAIRS - 1, 1), None)
                    score_chunk(PAIRS - 1, 1, None, None)

                    pe.wait_ge(negated, b + 1)
                    pe.transpose(quad[0][0:UM, 0:P], neg[:], ident[:]).then_inc(max_turned, 1)
                    pe.wait_ge(max_in, b * 48 + 48)
                    pe.wait_ge(out_reset, b + 1)
                    settle(pe, "pe")

                    with pe.Fori(lo, PAIRS) as p:
                        m = (b * CHUNKS + (p - lo) * 2) * SETS

                        def score_set(i):
                            u, at = i // SETS, i % SETS
                            pe.wait_ge(biased if masked else probs, m + (i - 1 + S0))
                            for x in range(4):
                                t, h = (at // 4, at % 4 * 4 + x) if small else (at % 2 * 2 + x // 2, at // 2 * 2 + x % 2)
                                out = duo[i % 2][:, x * S:(x + 1) * S]
                                if small:
                                    mm = pe.matmul(out, keys[0:KQ + 3, bass.ds(p, 1), u * UNITS + h, t * P:(t + 1) * P]
                                                   .rearrange("k p n -> k (p n)"), query[0:KQ + 3, h, :], start=True, stop=True)
                                else:
                                    for y, (tile, slab) in enumerate(((0, 0), (1, 0), (2, 1))):
                                        pe.matmul(out, keys[:, bass.ds(p, 1), u * UNITS + 2 * h + slab, t * P:(t + 1) * P]
                                                  .rearrange("k p n -> k (p n)"), query[:, tile * H + h, :], start=y == 0, stop=False)
                                    mm = pe.matmul(out, onesb[:], shift[:, h, :], start=False, stop=True)
                            mm.then_inc(set_scored, 1)

                        def use_set(i):
                            u, at = i // SETS, i % SETS
                            if at == 0:
                                pe.wait_ge(v_in[u], (b * PAIRS_RUN + (p - lo)) * 16 + 16)
                            pe.wait_ge(probs, m + (i + 1 + PS0))
                            for x in range(4):
                                if small:
                                    t, h, group, row = at // 4, at % 4 * 4 + x, at % 4, x * 32
                                else:
                                    t, h, group, row = at % 2 * 2 + x // 2, at // 2 * 2 + x % 2, at // 2, x % 2 * 64
                                mm = pe.matmul(bank[group // 2][row:row + VW, group % 2 * S:group % 2 * S + S],
                                               value[u][:, t, h * VW:(h + 1) * VW], slot[i % 4][:, x * S:(x + 1) * S],
                                               start=False, stop=True, skip_group_check=True)
                            mm.then_inc(used, 1)

                        for i in range(2 * SETS):
                            score_set(i)
                            if i >= 2:
                                use_set(i - 2)
                        use_set(2 * SETS - 2)
                        use_set(2 * SETS - 1)

                    if not small:
                        pe.wait_ge(summed, b * (CHUNKS * SETS * TS) + (CHUNKS * SETS * TS + S0))
                        for h in range(H):
                            row, group = h % 2 * 64, h // 2
                            mm = pe.matmul(bank[2 + group // 2][row:row + 64, group % 2 * S:group % 2 * S + S],
                                           ones[:, 0:64], acc[:, h, :], start=True, stop=True, skip_group_check=True)
                        mm.then_inc(sums_made, 1)
                    pe.wait_ge(o_kept, b + 1 + ONE)

            choose(pe, run)


def project_heads(c, H, o_rows, sum_rows, b_v, w_o, b_o, x_rows, ones, tag):
    nc = c.nc
    small = H == 16
    o_in, w_in, x_in = c.sem(tag + "o_in"), c.sem(tag + "w_in"), c.sem(tag + "x_in")
    cleared, chosen, spread = c.sem(tag + "cleared"), c.sem(tag + "chosen"), c.sem(tag + "spread")
    inverted, normed, projected, added, stored = (c.sem(tag + n) for n in
                                                  ("inverted", "normed", "projected", "added", "stored"))
    W = 4 * S
    with ExitStack() as s:
        def sb(n, shape, dt=F32):
            return s.enter_context(nc.sbuf_tensor(tag + n, shape, dt))

        o = sb("o", [P, B, W])
        inv = sb("inv", [P, B, W])
        on = sb("on", [P, B, W])
        x = sb("x", [P, NT, D])
        wo = sb("wo", [P, 4, D])
        bo = sb("bo", [1, D])
        bv = sb("bv", [P, 4])
        if small:
            pick = sb("pick", [P, P])
        else:
            sums = sb("sums", [P, B, W])
        ps = [s.enter_context(nc.psum_tensor(f"{tag}ps{i}", [P, 512], F32)) for i in range(8)]
        block = s.enter_context(nc.Block())
        NW = 9 if small else 2

        @block.sync
        def _(sp):
            sp.dma_start(o[:], o_rows.ap().rearrange("b p n -> p b n")).then_inc(o_in, 16)
            if not small:
                sp.dma_start(sums[:], sum_rows.ap().rearrange("b p n -> p b n")).then_inc(o_in, 16)
            sp.dma_start(bo[:], b_o.rearrange("(a n) -> a n", a=1)).then_inc(w_in, 16)
            if small:
                sp.wait_ge(cleared, 2)
                for j in range(4):
                    sp.dma_start(wo[32 * j:32 * j + 16, :, :],
                                 w_o.rearrange("(g j d) n -> j d g n", j=4, d=16)[j]).then_inc(w_in, 16)
                    sp.dma_start(bv[32 * j:32 * j + 16, :],
                                 b_v.rearrange("(g j d) -> j d g", j=4, d=16)[j],
                                 allow_slow_non_contiguous=True).then_inc(w_in, 16)
            else:
                sp.dma_start(wo[:], w_o.rearrange("(g p) n -> p g n", p=P)).then_inc(w_in, 16)
            sp.dma_start(x[:], x_rows.ap().rearrange("(t p) d -> p t d", p=P)).then_inc(x_in, 16)
            sp.wait_ge(added, NT)
            sp.dma_start(x_rows.ap().rearrange("(t p) d -> p t d", p=P), x[:]).then_inc(stored, 16)
            sp.wait_ge(stored, 16)

        @block.gpsimd
        def _(pool):
            if small:
                pool.memset(wo[:], 0.0).then_inc(cleared, 1)
                pool.memset(bv[:], 0.0).then_inc(cleared, 1)
                pool.memset(pick[:], 0.0).then_inc(cleared, 1)
                pool.wait_ge(cleared, 3)
                view = pick[:].rearrange("k (j d) -> k j d", j=4)
                pool.affine_select(out=view, in_=view, compare_op=ALU.not_equal, fill=1.0, base=-16,
                                   pattern=[[-32, 4], [0, 32]], channel_multiplier=1).then_inc(chosen, 1)

        @block.tensor
        def _(pe):
            if small:
                pe.wait_ge(o_in, 16)
                pe.wait_ge(chosen, 1)
                for i in range(2 * B):
                    pe.matmul(ps[i][:], pick[:], o[:, i // 2, i % 2 * 512:i % 2 * 512 + 512],
                              start=True, stop=True).then_inc(spread, 1)
            pe.wait_ge(w_in, 16 * NW)
            for t in range(NT):
                pe.wait_ge(normed, 2 * (t // QT) + 2)
                if small and t == 0:
                    pe.wait_ge(inverted, 2 * B)
                for g in range(4):
                    at = g * S + t % QT * P
                    pe.matmul(ps[t][:, 0:D], on[:, t // QT, at:at + P], wo[:, g, :], start=g == 0, stop=False)
                pe.matmul(ps[t][:, 0:D], ones[0:1, :], bo[:], start=False, stop=True).then_inc(projected, 1)

        @block.vector
        def _(dve):
            dve.wait_ge(o_in, 16 if small else 32)
            dve.wait_ge(w_in, 16 * NW)
            for i in range(2 * B):
                cols = slice(i % 2 * 512, i % 2 * 512 + 512)
                if small:
                    dve.wait_ge(spread, i + 1)
                dve.reciprocal(inv[:, i // 2, cols], ps[i][:] if small else sums[:, i // 2, cols]).then_inc(inverted, 1)
            for i in range(2 * B):
                cols = slice(i % 2 * 512, i % 2 * 512 + 512)
                dve.wait_ge(inverted, i + 1)
                if small:
                    dve.tensor_tensor(inv[:, i // 2, cols], inv[:, i // 2, cols], o[:, i // 2, cols],
                                      ALU.mult).then_inc(inverted, 1)
                    dve.wait_ge(inverted, 2 * B + i + 1)
                    for g in range(i % 2 * 2, i % 2 * 2 + 2):
                        ins = dve.tensor_scalar(on[:, i // 2, g * S:(g + 1) * S], inv[:, i // 2, g * S:(g + 1) * S],
                                                bv[:, g:g + 1], None, ALU.add)
                    ins.then_inc(normed, 1)
                else:
                    dve.tensor_tensor(on[:, i // 2, cols], inv[:, i // 2, cols], o[:, i // 2, cols],
                                      ALU.mult).then_inc(normed, 1)
            dve.wait_ge(x_in, 16)
            for t in range(NT):
                dve.wait_ge(projected, t + 1)
                dve.tensor_tensor(x[:, t, :], ps[t][:, 0:D], x[:, t, :], ALU.add).then_inc(added, 1)


def channel_attention(c, xnT, w_qk, w_v, w_o, tau, x_rows, ident, ones, tag):
    nc = c.nc
    DH = 16
    w_in, picks, tau_col = c.sem(tag + "w_in"), c.sem(tag + "picks"), c.sem(tag + "tau_col")
    qk_made, qk_kept, v_made, v_kept = (c.sem(tag + n) for n in ("qk_made", "qk_kept", "v_made", "v_kept"))
    gram_made, step, norms, exped, mixed, mix_kept = (c.sem(tag + n) for n in
                                                     ("gram_made", "step", "norms", "exped", "mixed", "mix_kept"))
    x_in, projected, added, stored = (c.sem(tag + n) for n in ("x_in", "projected", "added", "stored"))
    GB = B * KT
    with ExitStack() as s:
        def sb(n, shape, dt=F32):
            return s.enter_context(nc.sbuf_tensor(tag + n, shape, dt))

        wqk, wv, wo = sb("wqk", [P, KT, D]), sb("wv", [P, KT, D]), sb("wo", [P, KT, D])
        tau_sb = sb("tau_sb", [16, 1])
        pick = sb("pick", [16, D])
        tau_c = sb("tau_c", [P, KT])
        same = sb("same", [P, P])
        off = sb("off", [P, P])
        qk = sb("qk", [P, NT, D])
        vT = sb("vT", [P, KT, N])
        gram, diag, logit = sb("gram", [P, GB, P]), sb("diag", [P, GB, P]), sb("logit", [P, GB, P])
        q2 = sb("q2", [P, GB])
        top, negtop, total, inv = (sb(n, [P, GB]) for n in ("top", "negtop", "total", "inv"))
        attn = sb("attn", [P, GB, P])
        mix = sb("mix", [P, GB, D])
        x = sb("x", [P, NT, D])
        ps = [s.enter_context(nc.psum_tensor(f"{tag}ps{i}", [P, 512], F32)) for i in range(8)]
        block = s.enter_context(nc.Block())

        @block.sync
        def _(sp):
            for w, src in ((wqk, w_qk), (wv, w_v), (wo, w_o)):
                sp.dma_start(w[:], src.rearrange("(k p) n -> p k n", p=P)).then_inc(w_in, 16)
            sp.dma_start(tau_sb[:], tau.rearrange("h a b -> h (a b)")).then_inc(w_in, 16)
            sp.dma_start(x[:], x_rows.ap().rearrange("(t p) d -> p t d", p=P)).then_inc(x_in, 16)
            sp.wait_ge(added, NT)
            sp.dma_start(x_rows.ap().rearrange("(t p) d -> p t d", p=P), x[:]).then_inc(stored, 16)
            sp.wait_ge(stored, 16)

        @block.gpsimd
        def _(pool):
            pool.memset(pick[:], 1.0).then_inc(picks, 1)
            pool.wait_ge(picks, 1)
            pool.affine_select(out=pick[:], in_=pick[:], compare_op=ALU.is_ge, fill=0.0, base=0,
                               pattern=[[1, D]], channel_multiplier=-DH).then_inc(picks, 1)
            pool.wait_ge(picks, 2)
            pool.affine_select(out=pick[:], in_=pick[:], compare_op=ALU.is_ge, fill=0.0, base=DH - 1,
                               pattern=[[-1, D]], channel_multiplier=DH).then_inc(picks, 1)

        @block.tensor
        def _(pe):
            pe.wait_ge(w_in, 64)
            pe.wait_ge(picks, 3)
            for k in range(KT):
                pe.matmul(ps[7][:, k:k + 1], pick[:, k * P:(k + 1) * P], tau_sb[:], start=True, stop=True)
            pe.matmul(ps[7][:, P:2 * P], pick[:, 0:P], pick[:, 0:P], start=True, stop=True).then_inc(tau_col, 1)
            for t in range(NT):
                if t >= 4:
                    pe.wait_ge(qk_kept, t - 3)
                for k in range(KT):
                    mm = pe.matmul(ps[t % 4][:, 0:D], xnT[:, k, t * P:(t + 1) * P], wqk[:, k, :],
                                   start=k == 0, stop=k == KT - 1)
                mm.then_inc(qk_made, 1)
            for i in range(KT * 2):
                if i >= 2:
                    pe.wait_ge(v_kept, i - 1)
                for k in range(KT):
                    mm = pe.matmul(ps[4 + i % 2][:], wv[:, k, i // 2 * P:(i // 2 + 1) * P],
                                   xnT[:, k, i % 2 * 512:i % 2 * 512 + 512], start=k == 0, stop=k == KT - 1)
                mm.then_inc(v_made, 1)
            pe.wait_ge(qk_kept, NT)
            for i in range(GB):
                b, m = i // KT, i % KT
                for t in range(QT):
                    rows = qk[:, b * QT + t, m * P:(m + 1) * P]
                    mm = pe.matmul(ps[i // 4][:, i % 4 * P:(i % 4 + 1) * P], rows, rows, start=t == 0, stop=t == QT - 1)
                mm.then_inc(gram_made, 1)
            pe.wait_ge(step, 3)
            for i in range(2):
                mm = pe.matmul(ps[2 + i][:], ones[:], diag[:, 4 * i:4 * i + 4, :].rearrange("p i n -> p (i n)"),
                               start=True, stop=True)
            mm.then_inc(norms, 1)
            pe.wait_ge(v_kept, 2 * KT)
            for i in range(GB):
                if i >= 4:
                    pe.wait_ge(mix_kept, i - 3)
                pe.wait_ge(step, 13 + i)
                pe.matmul(ps[4 + i % 4][:, 0:D], attn[:, i, :], wo[:, i % KT, :], start=True, stop=True).then_inc(mixed, 1)
            pe.wait_ge(mix_kept, GB)
            for t in range(NT):
                if t >= 4:
                    pe.wait_ge(added, t - 3)
                for k in range(KT):
                    mm = pe.matmul(ps[t % 4][:, 0:D], vT[:, k, t * P:(t + 1) * P], mix[:, t // QT * KT + k, :],
                                   start=k == 0, stop=k == KT - 1)
                mm.then_inc(projected, 1)

        @block.scalar
        def _(act):
            for t in range(NT):
                act.wait_ge(qk_made, t + 1)
                act.activation(qk[:, t, :], ps[t % 4][:, 0:D], ACT.Copy).then_inc(qk_kept, 1)
            for i in range(KT * 2):
                act.wait_ge(v_made, i + 1)
                act.activation(vT[:, i // 2, i % 2 * 512:i % 2 * 512 + 512], ps[4 + i % 2][:], ACT.Copy).then_inc(v_kept, 1)
            act.wait_ge(step, 11)
            for i in range(GB):
                act.activation(attn[:, i, :], logit[:, i, :], ACT.Exp, bias=negtop[:, i:i + 1],
                               accum_out=total[:, i:i + 1]).then_inc(exped, 1)
            for i in range(GB):
                act.wait_ge(mixed, i + 1)
                act.activation(mix[:, i, :], ps[4 + i % 4][:, 0:D], ACT.Copy).then_inc(mix_kept, 1)

        @block.vector
        def _(dve):
            dve.wait_ge(tau_col, 1)
            dve.tensor_copy(tau_c[:], ps[7][:, 0:KT])
            dve.tensor_copy(same[:], ps[7][:, P:2 * P]).then_inc(step, 1)
            dve.wait_ge(step, 1)
            dve.tensor_scalar(off[:], same[:], -LOWEST, LOWEST, ALU.mult, ALU.add)
            dve.wait_ge(gram_made, GB)
            for i in range(2):
                ins = dve.tensor_copy(gram[:, 4 * i:4 * i + 4, :].rearrange("p i n -> p (i n)"), ps[i][:])
            ins.then_inc(step, 1)
            dve.wait_ge(step, 2)
            dve.tensor_tensor(diag[:], gram[:], ident[:].unsqueeze(1).broadcast_to([P, GB, P]), ALU.mult).then_inc(step, 1)
            dve.wait_ge(step, 3)
            dve.tensor_reduce(q2[:], diag[:], AX.X, ALU.add).then_inc(step, 1)
            dve.wait_ge(step, 4)
            for i in range(GB):
                ins = dve.tensor_scalar(logit[:, i, :], gram[:, i, :], 2.0, q2[:, i:i + 1], ALU.mult, ALU.subtract)
            ins.then_inc(step, 1)
            dve.wait_ge(step, 5)
            dve.wait_ge(norms, 1)
            for i in range(2):
                half = logit[:, 4 * i:4 * i + 4, :].rearrange("p i n -> p (i n)")
                ins = dve.tensor_tensor(half, half, ps[2 + i][:], ALU.subtract)
            ins.then_inc(step, 1)
            dve.wait_ge(step, 6)
            for m in range(KT):
                ins = dve.tensor_scalar(logit[:, m:GB:KT, :], logit[:, m:GB:KT, :], 1.0 / 16.0, tau_c[:, m:m + 1],
                                        ALU.mult, ALU.mult)
            ins.then_inc(step, 1)
            dve.wait_ge(step, 7)
            dve.tensor_tensor(logit[:], logit[:], same[:].unsqueeze(1).broadcast_to([P, GB, P]), ALU.mult).then_inc(step, 1)
            dve.wait_ge(step, 8)
            dve.tensor_tensor(logit[:], logit[:], off[:].unsqueeze(1).broadcast_to([P, GB, P]), ALU.add).then_inc(step, 1)
            dve.wait_ge(step, 9)
            dve.tensor_reduce(top[:], logit[:], AX.X, ALU.max).then_inc(step, 1)
            dve.wait_ge(step, 10)
            dve.tensor_scalar(negtop[:], top[:], -1.0, None, ALU.mult).then_inc(step, 1)
            dve.wait_ge(exped, GB)
            dve.reciprocal(inv[:], total[:]).then_inc(step, 1)
            dve.wait_ge(step, 12)
            for i in range(GB):
                dve.tensor_scalar(attn[:, i, :], attn[:, i, :], inv[:, i:i + 1], None, ALU.mult).then_inc(step, 1)
            dve.wait_ge(x_in, 16)
            for t in range(NT):
                dve.wait_ge(projected, t + 1)
                dve.tensor_tensor(x[:, t, :], ps[t % 4][:, 0:D], x[:, t, :], ALU.add).then_inc(added, 1)


def route(c, xnT, w_g, gate, ones, onesb, tag):
    nc = c.nc
    E = 8
    CAP = 320
    w_in, built, logits, step, exped, counted = (c.sem(tag + n) for n in
                                                 ("w_in", "built", "logits", "step", "exped", "counted"))
    with ExitStack() as s:
        def sb(n, shape, dt=F32):
            return s.enter_context(nc.sbuf_tensor(tag + n, shape, dt))

        wg = sb("wg", [P, KT, E])
        lg, pr = sb("lg", [P, NT, E]), sb("pr", [P, NT, E])
        top, total, inv = sb("top", [P, NT]), sb("total", [P, NT]), sb("inv", [P, NT])
        best8, at8, at8f = sb("best8", [P, NT, E]), sb("at8", [P, NT, E], U32), sb("at8f", [P, NT, E])
        iota = sb("iota", [P, E])
        one = sb("one", [P, 2, NT, E])
        oneb = sb("oneb", [P, 2 * NT, E], BF16)
        upto = sb("upto", [P, P], BF16)
        seat = sb("seat", [P, 2, NT, E])
        place = sb("place", [P, 2 * NT])
        kept = sb("kept", [P, 2, NT])
        g2, den, rden, part = sb("g2", [P, 2, NT]), sb("den", [P, NT]), sb("rden", [P, NT]), sb("part", [P, 2, NT, E])
        ps = [s.enter_context(nc.psum_tensor(f"{tag}ps{i}", [P, 512], F32)) for i in range(2)]
        block = s.enter_context(nc.Block())

        @block.sync
        def _(sp):
            sp.dma_start(wg[:], w_g.rearrange("(k p) n -> p k n", p=P)).then_inc(w_in, 16)

        @block.gpsimd
        def _(pool):
            pool.memset(upto[:], 1.0).then_inc(built, 1)
            pool.memset(onesb[:], 1.0).then_inc(built, 1)
            for e in range(E):
                pool.memset(iota[:, e:e + 1], float(e)).then_inc(built, 1)
            pool.wait_ge(built, 2 + E)
            pool.affine_select(out=upto[:], in_=upto[:], compare_op=ALU.is_ge, fill=0.0, base=0,
                               pattern=[[1, P]], channel_multiplier=-1).then_inc(built, 1)

        @block.tensor
        def _(pe):
            pe.wait_ge(w_in, 16)
            for t in range(NT):
                for k in range(KT):
                    mm = pe.matmul(ps[0][:, t * E:(t + 1) * E], xnT[:, k, t * P:(t + 1) * P], wg[:, k, :],
                                   start=k == 0, stop=k == KT - 1)
            mm.then_inc(logits, 1)
            pe.wait_ge(built, 3 + E)
            pe.wait_ge(step, 11)
            for j in range(2 * NT):
                for i in range(j):
                    pe.matmul(ps[1][:, j * E:(j + 1) * E], onesb[:], oneb[:, i, :], start=i == 0, stop=False)
                mm = pe.matmul(ps[1][:, j * E:(j + 1) * E], upto[:], oneb[:, j, :], start=j == 0, stop=True)
            mm.then_inc(counted, 1)

        @block.scalar
        def _(act):
            act.wait_ge(step, 3)
            act.activation(pr[:], lg[:], ACT.Exp).then_inc(exped, 1)

        @block.vector
        def _(dve):
            def wide(a, n=NT):
                return a.unsqueeze(2).broadcast_to([P, n, E])

            dve.wait_ge(logits, 1)
            dve.tensor_copy(lg[:].rearrange("p t e -> p (t e)"), ps[0][:, 0:NT * E]).then_inc(step, 1)
            dve.wait_ge(step, 1)
            dve.tensor_reduce(top[:], lg[:], AX.X, ALU.max).then_inc(step, 1)
            dve.wait_ge(step, 2)
            dve.tensor_tensor(lg[:], lg[:], wide(top[:]), ALU.subtract).then_inc(step, 1)
            dve.wait_ge(exped, 1)
            dve.tensor_reduce(total[:], pr[:], AX.X, ALU.add).then_inc(step, 1)
            dve.wait_ge(step, 4)
            dve.reciprocal(inv[:], total[:]).then_inc(step, 1)
            dve.wait_ge(step, 5)
            dve.tensor_tensor(pr[:], pr[:], wide(inv[:]), ALU.mult).then_inc(step, 1)
            dve.wait_ge(step, 6)
            for t in range(NT):
                ins = dve.max(best8[:, t, :], pr[:, t, :])
            ins.then_inc(step, 1)
            dve.wait_ge(step, 7)
            for t in range(NT):
                ins = dve.max_index(at8[:, t, :], best8[:, t, :], pr[:, t, :])
            ins.then_inc(step, 1)
            dve.wait_ge(step, 8)
            dve.tensor_copy(at8f[:], at8[:]).then_inc(step, 1)
            dve.wait_ge(step, 9)
            dve.wait_ge(built, 2 + E)
            for j in range(2):
                ins = dve.tensor_tensor(one[:, j], wide(at8f[:, :, j]), iota[:].unsqueeze(1).broadcast_to([P, NT, E]),
                                        ALU.is_equal)
            ins.then_inc(step, 1)
            dve.wait_ge(step, 10)
            dve.tensor_copy(oneb[:].rearrange("p (j t) e -> p j t e", j=2), one[:]).then_inc(step, 1)
            dve.wait_ge(counted, 1)
            dve.tensor_tensor(seat[:].rearrange("p j t e -> p (j t e)"), one[:].rearrange("p j t e -> p (j t e)"),
                              ps[1][:, 0:2 * NT * E], ALU.mult).then_inc(step, 1)
            dve.wait_ge(step, 12)
            dve.tensor_reduce(place[:], seat[:].rearrange("p j t e -> p (j t) e"), AX.X, ALU.add).then_inc(step, 1)
            dve.wait_ge(step, 13)
            dve.tensor_scalar(kept[:].rearrange("p j t -> p (j t)"), place[:], float(CAP), None, ALU.is_le).then_inc(step, 1)
            dve.wait_ge(step, 14)
            for j in range(2):
                ins = dve.tensor_tensor(g2[:, j], best8[:, :, j], kept[:, j], ALU.mult)
            ins.then_inc(step, 1)
            dve.wait_ge(step, 15)
            dve.tensor_tensor(den[:], g2[:, 0], g2[:, 1], ALU.add).then_inc(step, 1)
            dve.wait_ge(step, 16)
            dve.tensor_scalar(den[:], den[:], 1e-9, None, ALU.max).then_inc(step, 1)
            dve.wait_ge(step, 17)
            dve.reciprocal(rden[:], den[:]).then_inc(step, 1)
            dve.wait_ge(step, 18)
            dve.tensor_tensor(g2[:], g2[:], rden[:].unsqueeze(1).broadcast_to([P, 2, NT]), ALU.mult).then_inc(step, 1)
            dve.wait_ge(step, 19)
            for j in range(2):
                ins = dve.tensor_tensor(part[:, j], one[:, j], wide(g2[:, j]), ALU.mult)
            ins.then_inc(step, 1)
            dve.wait_ge(step, 20)
            dve.tensor_tensor(gate[:], part[:, 0], part[:, 1], ALU.add).then_inc(step, 1)


def experts(c, xnT, gate, w_in_all, w_out_all, x_rows, tag):
    nc = c.nc
    E, F = 8, 512
    FT = F // P
    HALVES = N // 512
    ONE = 16
    x_in, w_loaded, hidden, gelued, gated, out_made, added, stored = (
        c.sem(tag + n) for n in ("x_in", "w_loaded", "hidden", "gelued", "gated", "out_made", "added", "stored"))
    win_in, wout_in = ([c.sem(f"{tag}{n}{u}") for u in range(2)] for n in ("win_in", "wout_in"))
    with ExitStack() as s:
        def sb(n, shape, dt=F32):
            return s.enter_context(nc.sbuf_tensor(tag + n, shape, dt))

        win = [sb(f"win{u}", [P, KT, 2 * F]) for u in range(2)]
        wout = [sb(f"wout{u}", [P, FT, D]) for u in range(2)]
        ga = [sb(f"ga{i}", [P, 512]) for i in range(2)]
        hid = [sb(f"hid{i}", [P, FT, 512]) for i in range(2)]
        x = sb("x", [P, NT, D])
        ps = [s.enter_context(nc.psum_tensor(f"{tag}ps{i}", [P, 512], F32)) for i in range(8)]
        block = s.enter_context(nc.Block())
        TH = 512 // P
        OUTS = HALVES * TH
        HIDS = HALVES * FT

        @block.sync
        def _(sp):
            sp.dma_start(x[:], x_rows.ap().rearrange("(t p) d -> p t d", p=P)).then_inc(x_in, 16)
            with sp.Fori(0, E // 2) as e:
                for u in range(2):
                    sp.wait_ge(out_made, e * (2 * OUTS) + (u * OUTS - OUTS + 2 * OUTS))
                    sp.dma_start(win[u][:], w_in_all[bass.ds(e * 2 + u, 1)].rearrange("e (k p) n -> p (e k) n", p=P)).then_inc(win_in[u], 16)
                    sp.dma_start(wout[u][:], w_out_all[bass.ds(e * 2 + u, 1)].rearrange("e (k p) n -> p (e k) n", p=P)).then_inc(wout_in[u], 16)
            sp.wait_ge(added, E * OUTS + ONE)
            sp.dma_start(x_rows.ap().rearrange("(t p) d -> p t d", p=P), x[:]).then_inc(stored, 16)
            sp.wait_ge(stored, 16)

        @block.tensor
        def _(pe):
            pe.sem_inc(out_made, 2 * OUTS)
            with pe.Fori(0, E // 2) as e:
                for u in range(2):
                    pe.wait_ge(win_in[u], e * 16 + 16)
                    for half in range(HALVES):
                        cols = slice(half * 512, half * 512 + 512)
                        for f in range(FT):
                            i = (u * HALVES + half) * FT + f
                            pe.wait_ge(gated, e * (2 * HIDS) + (i - 1 + ONE))
                            for part in range(2):
                                at = part * F + f * P
                                for k in range(KT):
                                    mm = pe.matmul(ps[2 * (f % 2) + part][:], win[u][:, k, at:at + P], xnT[:, k, cols],
                                                   start=k == 0, stop=k == KT - 1)
                            mm.then_inc(hidden, 1)
                        if half == 0:
                            pe.wait_ge(wout_in[u], e * 16 + 16)
                        pe.wait_ge(gated, e * (2 * HIDS) + ((u * HALVES + half + 1) * FT + ONE))
                        for t in range(TH):
                            j = (u * HALVES + half) * TH + t
                            pe.wait_ge(added, e * (2 * OUTS) + (j - 3 + ONE))
                            for f in range(FT):
                                mm = pe.matmul(ps[4 + t][:, 0:D], hid[half][:, f, t * P:(t + 1) * P], wout[u][:, f, :],
                                               start=f == 0, stop=f == FT - 1)
                            mm.then_inc(out_made, 1)

        @block.scalar
        def _(act):
            with act.Fori(0, E // 2) as e:
                for i in range(2 * HIDS):
                    act.wait_ge(hidden, e * (2 * HIDS) + (i + 1))
                    act.wait_ge(gated, e * (2 * HIDS) + (i - 1 + ONE))
                    act.activation(ga[i % 2][:], ps[2 * (i % 2)][:], ACT.Gelu).then_inc(gelued, 1)

        @block.vector
        def _(dve):
            dve.sem_inc(gated, ONE)
            dve.sem_inc(added, ONE)
            dve.wait_ge(x_in, 16)
            with dve.Fori(0, E // 2) as e:
                for u in range(2):
                    for half in range(HALVES):
                        for f in range(FT):
                            i = (u * HALVES + half) * FT + f
                            dve.wait_ge(gelued, e * (2 * HIDS) + (i + 1))
                            if f == 0:
                                dve.wait_ge(out_made, e * (2 * OUTS) + ((u * HALVES + half - 1) * TH + 2 * OUTS))
                            dve.tensor_tensor(hid[half][:, f, :], ps[2 * (f % 2) + 1][:], ga[i % 2][:], ALU.mult).then_inc(gated, 1)
                        for t in range(TH):
                            j = (u * HALVES + half) * TH + t
                            row = half * TH + t
                            dve.wait_ge(out_made, e * (2 * OUTS) + (j + 1 + 2 * OUTS))
                            dve.wait_ge(added, e * (2 * OUTS) + (j - 7 + ONE))
                            dve.scalar_tensor_tensor(x[:, row, :], ps[4 + t][:, 0:D],
                                                     gate[:, row, bass.ds(e * 2 + u, 1)],
                                                     x[:, row, :], ALU.mult, ALU.add).then_inc(added, 1)


def refine_root(dve, step, at, var, root, tmp):
    dve.reciprocal(tmp[:, 0], root).then_inc(step, 1)
    dve.wait_ge(step, at + 1)
    dve.tensor_tensor(tmp[:, 1], tmp[:, 0], tmp[:, 0], ALU.mult).then_inc(step, 1)
    dve.wait_ge(step, at + 2)
    dve.tensor_tensor(tmp[:, 2], tmp[:, 1], var, ALU.mult).then_inc(step, 1)
    dve.wait_ge(step, at + 3)
    dve.tensor_scalar(tmp[:, 1], tmp[:, 2], -0.5, 1.5, ALU.mult, ALU.add).then_inc(step, 1)
    dve.wait_ge(step, at + 4)
    dve.tensor_tensor(tmp[:, 3], tmp[:, 1], tmp[:, 0], ALU.mult).then_inc(step, 1)


def self_attention(c, xn, xnT, norm_w, w_q, w_k, w_v, w_o, gate, log_t, x_rows, ident, ones, tag):
    nc = c.nc
    H, KV, DH = 4, 2, 64
    NQK = (H + KV) * DH
    w_in, x_in, step, rooted, spread, scaled = (c.sem(tag + n) for n in
                                               ("w_in", "x_in", "step", "rooted", "spread", "scaled"))
    masks, qkv_made, qkv_kept, turned, kept = (c.sem(tag + n) for n in ("masks", "qkv_made", "qkv_kept", "turned", "kept"))
    scored, masked, maxed, exped, p_turned, p_kept = (c.sem(tag + n) for n in
                                                     ("scored", "masked", "maxed", "exped", "p_turned", "p_kept"))
    mixed, o_normed, o_turned, o_kept, projected, blended, added, stored = (
        c.sem(tag + n) for n in ("mixed", "o_normed", "o_turned", "o_kept", "projected", "blended", "added", "stored"))
    with ExitStack() as s:
        def sb(n, shape, dt=F32):
            return s.enter_context(nc.sbuf_tensor(tag + n, shape, dt))

        w = sb("w", [P, KT, NQK + KV * DH])
        wo, nw = sb("wo", [P, KT, D]), sb("nw", [P, KT])
        two, two_c = sb("two", [1, 2]), sb("two_c", [P, 2])
        scale = sb("scale", [P, 1])
        cmask = sb("cmask", [P, QT, S])
        sq, ms, var, root, tmp = sb("sq", [P, NT, D]), sb("ms", [P, NT]), sb("var", [P, NT]), sb("root", [P, NT]), sb("tmp", [P, 4, NT])
        qkv = sb("qkv", [P, NT, NQK + KV * DH])
        qsq, qn = sb("qsq", [P, NT, NQK]), sb("qn", [P, NT, NQK])
        n2, n1, n0, ninv = (sb(n, [P, NT * 6]) for n in ("n2", "n1", "n0", "ninv"))
        qkT = sb("qkT", [P, 3, N])
        lg = [sb(f"lg{i}", [P, H, S]) for i in range(2)]
        pb = [sb(f"pb{i}", [P, H, S]) for i in range(2)]
        top, bias, total, inv = (sb(n, [P, NT, H]) for n in ("top", "bias", "total", "inv"))
        pT = [sb(f"pT{i}", [P, 2 * H, P]) for i in range(2)]
        o = [sb(f"o{i}", [P, D]) for i in range(2)]
        oT = [sb(f"oT{i}", [P, KT, P]) for i in range(2)]
        x, y = sb("x", [P, NT, D]), sb("y", [P, NT, D])
        duo = [s.enter_context(nc.psum_tensor(f"{tag}duo{i}", [P, 1024], F32)) for i in range(3)]
        mixp = s.enter_context(nc.psum_tensor(tag + "mixp", [P, 512], F32))
        outp = s.enter_context(nc.psum_tensor(tag + "outp", [P, 512], F32))
        block = s.enter_context(nc.Block())

        @block.sync
        def _(sp):
            for j in range(2):
                for kv in range(KV):
                    h = 2 * kv + j
                    sp.dma_start(w[:, :, (j * KV + kv) * DH:(j * KV + kv + 1) * DH],
                                 w_q.rearrange("(k p) n -> p k n", p=P)[:, :, h * DH:(h + 1) * DH]).then_inc(w_in, 16)
            sp.dma_start(w[:, :, H * DH:NQK], w_k.rearrange("(k p) n -> p k n", p=P)).then_inc(w_in, 16)
            sp.dma_start(w[:, :, NQK:], w_v.rearrange("(k p) n -> p k n", p=P)).then_inc(w_in, 16)
            sp.dma_start(wo[:], w_o.rearrange("(k p) n -> p k n", p=P)).then_inc(w_in, 16)
            sp.dma_start(nw[:], norm_w.rearrange("(k p) -> p k", p=P), allow_slow_non_contiguous=True).then_inc(w_in, 16)
            sp.dma_start(two[:, 0:1], gate).then_inc(w_in, 16)
            sp.dma_start(two[:, 1:2], log_t).then_inc(w_in, 16)
            sp.dma_start(x[:], x_rows.ap().rearrange("(t p) d -> p t d", p=P)).then_inc(x_in, 16)
            sp.wait_ge(added, NT)
            sp.dma_start(x_rows.ap().rearrange("(t p) d -> p t d", p=P), x[:]).then_inc(stored, 16)
            sp.wait_ge(stored, 16)

        @block.gpsimd
        def _(pool):
            pool.memset(cmask[:], 0.0).then_inc(masks, 1)
            pool.wait_ge(masks, 1)
            for i in range(QT):
                pool.affine_select(out=cmask[:, i, :], in_=cmask[:, i, :], compare_op=ALU.is_ge, fill=NEG, base=i * P,
                                   pattern=[[-1, S]], channel_multiplier=1).then_inc(masks, 1)

        @block.tensor
        def _(pe):
            pe.wait_ge(w_in, 160)
            pe.matmul(outp[:, 0:2], ones[0:1, :], two[:], start=True, stop=True).then_inc(spread, 1)
            pe.wait_ge(step, 2)
            for t in range(NT):
                if t >= 4:
                    pe.wait_ge(qkv_kept, t - 3)
                for k in range(KT):
                    mm = pe.matmul(duo[t % 4 // 2][:, t % 2 * 512:t % 2 * 512 + 512], xnT[:, k, t * P:(t + 1) * P], w[:, k, :],
                                   start=k == 0, stop=k == KT - 1)
                mm.then_inc(qkv_made, 1)
            for t in range(NT):
                pe.wait_ge(step, 18)
                if t >= 2:
                    pe.wait_ge(kept, t - 1)
                for i in range(3):
                    mm = pe.transpose(duo[2][:, t % 2 * 512 + i * P:t % 2 * 512 + (i + 1) * P],
                                      qn[:, t, i * P:(i + 1) * P], ident[:])
                mm.then_inc(turned, 1)
            pe.wait_ge(kept, NT)
            for i in range(NT + 2):
                if i < NT:
                    if i >= 2:
                        pe.wait_ge(masked, i - 1)
                    for kv in range(KV):
                        rows = slice(kv * DH, kv * DH + DH)
                        for j in range(2):
                            mm = pe.matmul(duo[i % 2][:, (2 * kv + j) * S:(2 * kv + j + 1) * S],
                                           qkT[rows, j, i * P:(i + 1) * P], qkT[rows, 2, i // QT * S:i // QT * S + S],
                                           start=True, stop=True)
                    mm.then_inc(scored, 1)
                if 1 <= i <= NT:
                    g = i - 1
                    pe.wait_ge(exped, H * (g + 1))
                    if g >= 1:
                        pe.wait_ge(p_kept, g)
                    for h in range(H):
                        for k in range(2):
                            mm = pe.transpose(duo[2][:, (2 * h + k) * P:(2 * h + k + 1) * P],
                                              pb[g % 2][:, h, k * P:(k + 1) * P], ident[:])
                    mm.then_inc(p_turned, 1)
                    pe.wait_ge(p_kept, g + 1)
                    if g >= 1:
                        pe.wait_ge(o_kept, g)
                    for h in range(H):
                        for k in range(2):
                            at = NQK + h // 2 * DH
                            mm = pe.matmul(mixp[:, h * DH:(h + 1) * DH], pT[g % 2][:, 2 * h + k, :],
                                           qkv[:, g // QT * QT + k, at:at + DH], start=k == 0, stop=k == 1)
                    mm.then_inc(mixed, 1)
                    pe.wait_ge(o_normed, g + 1)
                    for k in range(KT):
                        mm = pe.transpose(mixp[:, D + k * P:D + (k + 1) * P], o[g % 2][:, k * P:(k + 1) * P], ident[:])
                    mm.then_inc(o_turned, 1)
                if i >= 2:
                    g = i - 2
                    pe.wait_ge(o_kept, g + 1)
                    if g >= 1:
                        pe.wait_ge(blended, g)
                    for k in range(KT):
                        mm = pe.matmul(outp[:, 0:D], oT[g % 2][:, k, :], wo[:, k, :], start=k == 0, stop=k == KT - 1)
                    mm.then_inc(projected, 1)

        @block.scalar
        def _(act):
            act.wait_ge(step, 4)
            act.activation(root[:], var[:], ACT.Sqrt).then_inc(rooted, 1)
            act.wait_ge(step, 9)
            for t in range(NT):
                act.wait_ge(qkv_made, t + 1)
                act.activation(qkv[:, t, :], duo[t % 4 // 2][:, t % 2 * 512:t % 2 * 512 + 512], ACT.Copy,
                               scale=tmp[:, 3, t:t + 1]).then_inc(qkv_kept, 1)
            act.wait_ge(step, 11)
            act.activation(n1[:], n2[:], ACT.Sqrt).then_inc(rooted, 1)
            for t in range(NT):
                act.wait_ge(turned, t + 1)
                act.activation(qkT[:, :, t * P:(t + 1) * P],
                               duo[2][:, t % 2 * 512:t % 2 * 512 + 3 * P].rearrange("p (i n) -> p i n", i=3),
                               ACT.Copy).then_inc(kept, 1)
            act.wait_ge(step, 1)
            act.activation(scale[:], two_c[:, 1:2], ACT.Exp).then_inc(scaled, 1)
            for g in range(NT):
                act.wait_ge(maxed, g + 1)
                if g >= 2:
                    act.wait_ge(p_turned, g - 1)
                for h in range(H):
                    act.activation(pb[g % 2][:, h, :], lg[g % 2][:, h, :], ACT.Exp, bias=bias[:, g, h:h + 1],
                                   scale=scale[:], accum_out=total[:, g, h:h + 1]).then_inc(exped, 1)
                act.wait_ge(p_turned, g + 1)
                if g >= 2:
                    act.wait_ge(mixed, g - 1)
                act.activation(pT[g % 2][:].rearrange("p i n -> p (i n)"), duo[2][:], ACT.Copy).then_inc(p_kept, 1)
                act.wait_ge(o_turned, g + 1)
                if g >= 2:
                    act.wait_ge(projected, g - 1)
                act.activation(oT[g % 2][:], mixp[:, D:2 * D].rearrange("p (k n) -> p k n", k=KT), ACT.Copy).then_inc(o_kept, 1)

        @block.vector
        def _(dve):
            dve.wait_ge(spread, 1)
            dve.tensor_copy(two_c[:], outp[:, 0:2]).then_inc(step, 1)
            dve.wait_ge(w_in, 160)
            for k in range(KT):
                ins = dve.tensor_scalar(w[:, k, :], w[:, k, :], nw[:, k:k + 1], None, ALU.mult)
            ins.then_inc(step, 1)
            for t in range(NT):
                ins = dve.tensor_tensor_reduce(sq[:, t, :], xn[:, t, :], xn[:, t, :], 1.0 / D, 0.0, ALU.mult, ALU.add,
                                               ms[:, t:t + 1])
            ins.then_inc(step, 1)
            dve.wait_ge(step, 3)
            dve.tensor_scalar(var[:], ms[:], 1e-6, None, ALU.add).then_inc(step, 1)
            dve.wait_ge(rooted, 1)
            refine_root(dve, step, 4, var[:], root[:], tmp)
            dve.wait_ge(qkv_kept, NT)
            dve.tensor_tensor(qsq[:], qkv[:, :, 0:NQK], qkv[:, :, 0:NQK], ALU.mult).then_inc(step, 1)
            dve.wait_ge(step, 10)
            dve.tensor_reduce(n2[:], qsq[:].rearrange("p t (h d) -> p (t h) d", d=DH), AX.X, ALU.add).then_inc(step, 1)
            dve.wait_ge(rooted, 2)
            dve.tensor_scalar(n0[:], n1[:], 1e-12, None, ALU.max).then_inc(step, 1)
            dve.wait_ge(step, 12)
            dve.reciprocal(ninv[:], n0[:]).then_inc(step, 1)
            dve.wait_ge(step, 13)
            dve.tensor_tensor(ninv[:], ninv[:], n2[:], ALU.mult).then_inc(step, 1)
            dve.wait_ge(step, 14)
            dve.tensor_tensor(ninv[:], ninv[:], n1[:], ALU.add).then_inc(step, 1)
            dve.wait_ge(step, 15)
            dve.tensor_scalar(n0[:], ninv[:], 0.5, 1e-12, ALU.mult, ALU.max).then_inc(step, 1)
            dve.wait_ge(step, 16)
            dve.reciprocal(n1[:], n0[:]).then_inc(step, 1)
            dve.wait_ge(step, 17)
            dve.tensor_tensor(qn[:].rearrange("p t (h d) -> p (t h) d", d=DH),
                              qkv[:, :, 0:NQK].rearrange("p t (h d) -> p t h d", d=DH),
                              n1[:].unsqueeze(2).broadcast_to([P, NT * 6, DH]), ALU.mult).then_inc(step, 1)
            dve.wait_ge(masks, 1 + QT)
            dve.wait_ge(scaled, 1)
            dve.wait_ge(x_in, 16)
            for g in range(NT + 1):
                if g < NT:
                    dve.wait_ge(scored, g + 1)
                    if g >= 2:
                        dve.wait_ge(exped, H * (g - 1))
                    dve.tensor_tensor(lg[g % 2][:], duo[g % 2][:].rearrange("p (h n) -> p h n", h=H),
                                      cmask[:, g % QT, :].unsqueeze(1).broadcast_to([P, H, S]), ALU.add).then_inc(masked, 1)
                    dve.wait_ge(masked, g + 1)
                    dve.tensor_reduce(top[:, g, :], lg[g % 2][:], AX.X, ALU.max).then_inc(step, 1)
                    dve.wait_ge(step, 19 + 2 * g)
                    dve.tensor_scalar(bias[:, g, :], top[:, g, :], scale[:], -1.0, ALU.mult, ALU.mult).then_inc(maxed, 1)
                    dve.wait_ge(exped, H * (g + 1))
                    dve.reciprocal(inv[:, g, :], total[:, g, :]).then_inc(step, 1)
                    dve.wait_ge(step, 20 + 2 * g)
                    dve.wait_ge(mixed, g + 1)
                    if g >= 2:
                        dve.wait_ge(o_turned, g - 1)
                    dve.tensor_tensor(o[g % 2][:].rearrange("p (h d) -> p h d", d=DH),
                                      mixp[:, 0:D].rearrange("p (h d) -> p h d", d=DH),
                                      inv[:, g, :].unsqueeze(2).broadcast_to([P, H, DH]), ALU.mult).then_inc(o_normed, 1)
                if g >= 1:
                    t = g - 1
                    dve.wait_ge(projected, t + 1)
                    dve.scalar_tensor_tensor(y[:, t, :], outp[:, 0:D], two_c[:, 0:1], xn[:, t, :],
                                             ALU.mult, ALU.add).then_inc(blended, 1)
                    dve.wait_ge(blended, t + 1)
                    dve.tensor_tensor(x[:, t, :], x[:, t, :], y[:, t, :], ALU.add).then_inc(added, 1)


def feed_forward(c, xn, w1, b1, w2, b2, x_rows, out, identb, ones, tag):
    nc = c.nc
    F = 1024
    FT = F // P
    w_in, x_in, wstep, summed, step, rooted = (c.sem(tag + n) for n in ("w_in", "x_in", "wstep", "summed", "step", "rooted"))
    w_turned, w_kept, b_spread, b_kept = (c.sem(tag + n) for n in ("w_turned", "w_kept", "b_spread", "b_kept"))
    x_turned, x_kept, up_made, scaled, gelued, squared = (c.sem(tag + n) for n in
                                                          ("x_turned", "x_kept", "up_made", "scaled", "gelued", "squared"))
    h_turned, h_kept, down_made, added, stored, hstep, biased = (
        c.sem(tag + n) for n in ("h_turned", "h_kept", "down_made", "added", "stored", "hstep", "biased"))
    with ExitStack() as s:
        def sb(n, shape, dt=F32):
            return s.enter_context(nc.sbuf_tensor(tag + n, shape, dt))

        w1_sb, w2_sb = sb("w1", [P, FT, D]), sb("w2", [P, KT, F])
        q1, q2 = sb("q1", [P, FT, D], BF16), sb("q2", [P, KT, F], BF16)
        w1T, w2T = sb("w1T", [P, KT, F], BF16), sb("w2T", [P, FT, D], BF16)
        wsum, mean, wscale = sb("wsum", [P, 2]), sb("mean", [P, 2]), sb("wscale", [P, 2])
        brow, b_all = sb("brow", [1, F + D]), sb("b_all", [P, F + D])
        sq, ms, var, root, tmp = sb("sq", [P, NT, D]), sb("ms", [P, NT]), sb("var", [P, NT]), sb("root", [P, NT]), sb("tmp", [P, 4, NT])
        big, cut, back = sb("big", [P, NT]), sb("cut", [P, NT]), sb("back", [P, NT])
        xs, xq, xqT = sb("xs", [P, NT, D]), sb("xq", [P, NT, D], BF16), sb("xqT", [P, KT, N], BF16)
        h = sb("h", [P, NT, F])
        hq = sb("hq", [P, NT, F], BF16)
        junk = [sb(f"junk{i}", [P, F]) for i in range(2)]
        hqT = [sb(f"hqT{i}", [P, FT, P], BF16) for i in range(2)]
        ms2, var2, root2, tmp2 = sb("ms2", [P, NT]), sb("var2", [P, NT]), sb("root2", [P, NT]), sb("tmp2", [P, 4, NT])
        big2, cut2, back2 = sb("big2", [P, NT]), sb("cut2", [P, NT]), sb("back2", [P, NT])
        x = sb("x", [P, NT, D])
        y = sb("y", [P, NT, D])
        tp = [s.enter_context(nc.psum_tensor(f"{tag}tp{i}", [P, 1024], BF16)) for i in range(2)]
        up = [s.enter_context(nc.psum_tensor(f"{tag}up{i}", [P, 1024], F32)) for i in range(2)]
        down = [s.enter_context(nc.psum_tensor(f"{tag}down{i}", [P, 512], F32)) for i in range(2)]
        block = s.enter_context(nc.Block())

        @block.sync
        def _(sp):
            sp.dma_start(w1_sb[:], w1.rearrange("(k p) n -> p k n", p=P)).then_inc(w_in, 16)
            sp.dma_start(w2_sb[:], w2.rearrange("(k p) n -> p k n", p=P)).then_inc(w_in, 16)
            sp.dma_start(brow[:, 0:F], b1.rearrange("(a n) -> a n", a=1)).then_inc(w_in, 16)
            sp.dma_start(brow[:, F:], b2.rearrange("(a n) -> a n", a=1)).then_inc(w_in, 16)
            sp.dma_start(x[:], x_rows.ap().rearrange("(t p) d -> p t d", p=P)).then_inc(x_in, 16)
            rows = out.rearrange("b s d -> (b s) d").rearrange("(t p) d -> p t d", p=P)
            for t in range(0, NT, 2):
                sp.wait_ge(added, t + 2)
                sp.dma_start(rows[:, t:t + 2, :], y[:, t:t + 2, :]).then_inc(stored, 16)
            sp.wait_ge(stored, 8 * NT)

        @block.tensor
        def _(pe):
            pe.wait_ge(w_in, 64)
            for i, (lo, hi) in enumerate(((0, 512), (512, 1024))):
                pe.matmul(up[0][:, lo:hi], ones[0:1, :], brow[:, lo:hi], start=True, stop=True)
            pe.matmul(up[1][:, 0:D], ones[0:1, :], brow[:, F:], start=True, stop=True).then_inc(b_spread, 1)
            pe.wait_ge(wstep, 2)
            pe.matmul(down[0][:, 0:2], ones[:], wsum[:], start=True, stop=True).then_inc(summed, 1)
            pe.wait_ge(wstep, 10)
            for i in range(4):
                if i >= 2:
                    pe.wait_ge(w_kept, i - 1)
                for j in range(8):
                    if i < 2:
                        mm = pe.transpose(tp[i % 2][:, j * P:(j + 1) * P], q1[:, j, i * P:(i + 1) * P], identb[:])
                    else:
                        f = 4 * (i - 2) + j // 2
                        mm = pe.transpose(tp[i % 2][:, j * P:(j + 1) * P], q2[:, j % 2, f * P:(f + 1) * P], identb[:])
                mm.then_inc(w_turned, 1)
            pe.wait_ge(w_kept, 4)
            pe.wait_ge(step, 16)
            for i in range(KT):
                for t in range(NT):
                    mm = pe.transpose(tp[i][:, t * P:(t + 1) * P], xq[:, t, i * P:(i + 1) * P], identb[:])
                mm.then_inc(x_turned, 1)
            pe.wait_ge(x_kept, KT)
            pe.wait_ge(b_kept, 1)
            for t in range(NT):
                if t >= 2:
                    pe.wait_ge(scaled, t - 1)
                for half in range(2):
                    for k in range(KT):
                        mm = pe.matmul(up[t % 2][:, half * 512:half * 512 + 512], xqT[:, k, t * P:(t + 1) * P],
                                       w1T[:, k, half * 512:half * 512 + 512], start=k == 0, stop=k == KT - 1)
                mm.then_inc(up_made, 1)
            for t in range(NT):
                pe.wait_ge(hstep, 12 + NT + t + 1)
                if t >= 2:
                    pe.wait_ge(h_kept, t - 1)
                for f in range(FT):
                    mm = pe.transpose(tp[t % 2][:, f * P:(f + 1) * P], hq[:, t, f * P:(f + 1) * P], identb[:])
                mm.then_inc(h_turned, 1)
                pe.wait_ge(h_kept, t + 1)
                if t >= 2:
                    pe.wait_ge(added, t - 1)
                for f in range(FT):
                    mm = pe.matmul(down[t % 2][:, 0:D], hqT[t % 2][:, f, :], w2T[:, f, :], start=f == 0, stop=f == FT - 1)
                mm.then_inc(down_made, 1)

        @block.scalar
        def _(act):
            act.wait_ge(b_spread, 1)
            act.activation(b_all[:, 0:F], up[0][:], ACT.Copy)
            act.activation(b_all[:, F:], up[1][:, 0:D], ACT.Copy).then_inc(b_kept, 1)
            act.wait_ge(step, 2)
            act.activation(root[:], var[:], ACT.Sqrt).then_inc(rooted, 1)
            for i in range(4):
                act.wait_ge(w_turned, i + 1)
                if i < 2:
                    act.activation(w1T[:, i, :], tp[i % 2][:], ACT.Copy).then_inc(w_kept, 1)
                else:
                    act.activation(w2T[:, 4 * (i - 2):4 * (i - 1), :].rearrange("p f n -> p (f n)"), tp[i % 2][:],
                                   ACT.Copy).then_inc(w_kept, 1)
            for i in range(KT):
                act.wait_ge(x_turned, i + 1)
                act.activation(xqT[:, i, :], tp[i][:], ACT.Copy).then_inc(x_kept, 1)
            for t in range(NT):
                act.wait_ge(scaled, t + 1)
                act.activation(h[:, t, :], h[:, t, :], ACT.Gelu).then_inc(gelued, 1)
                act.wait_ge(gelued, t + 1)
                if t >= 2:
                    act.wait_ge(squared, t - 1)
                act.activation(junk[t % 2][:], h[:, t, :], ACT.Square, accum_out=ms2[:, t:t + 1]).then_inc(squared, 1)
            act.wait_ge(hstep, NT + 1)
            act.activation(root2[:], var2[:], ACT.Sqrt).then_inc(rooted, 1)
            for t in range(NT):
                act.wait_ge(h_turned, t + 1)
                if t >= 2:
                    act.wait_ge(down_made, t - 1)
                act.activation(hqT[t % 2][:].rearrange("p f n -> p (f n)"), tp[t % 2][:], ACT.Copy).then_inc(h_kept, 1)

        @block.vector
        def _(dve):
            dve.wait_ge(w_in, 64)
            dve.tensor_reduce(wsum[:, 0:1], w1_sb[:].rearrange("p k n -> p (k n)"), AX.X, ALU.add,
                              apply_absolute_value=True).then_inc(wstep, 1)
            dve.tensor_reduce(wsum[:, 1:2], w2_sb[:].rearrange("p k n -> p (k n)"), AX.X, ALU.add,
                              apply_absolute_value=True).then_inc(wstep, 1)
            for t in range(NT):
                ins = dve.tensor_tensor_reduce(sq[:, t, :], xn[:, t, :], xn[:, t, :], 1.0 / D, 0.0, ALU.mult, ALU.add,
                                               ms[:, t:t + 1])
            ins.then_inc(step, 1)
            dve.wait_ge(step, 1)
            dve.tensor_scalar(var[:], ms[:], 1e-6, None, ALU.add).then_inc(step, 1)
            dve.tensor_reduce(big[:], xn[:], AX.X, ALU.max, apply_absolute_value=True).then_inc(step, 1)
            dve.wait_ge(summed, 1)
            dve.tensor_scalar(mean[:], down[0][:, 0:2], 1.0 / (F * D), 1e-5, ALU.mult, ALU.max).then_inc(wstep, 1)
            dve.wait_ge(wstep, 3)
            dve.reciprocal(wscale[:], mean[:]).then_inc(wstep, 1)
            dve.wait_ge(wstep, 4)
            f1, f2 = w1_sb[:].rearrange("p k n -> p (k n)"), w2_sb[:].rearrange("p k n -> p (k n)")
            for i, f in enumerate((f1, f2)):
                dve.tensor_scalar(f, f, wscale[:, i:i + 1], MAGIC, ALU.mult, ALU.add).then_inc(wstep, 1)
            dve.wait_ge(wstep, 6)
            for f in (f1, f2):
                dve.tensor_scalar(f, f, MAGIC, 1.0, ALU.subtract, ALU.min).then_inc(wstep, 1)
            dve.wait_ge(wstep, 8)
            for f, q in ((f1, q1), (f2, q2)):
                dve.tensor_scalar(q[:].rearrange("p k n -> p (k n)"), f, -1.0, None, ALU.max).then_inc(wstep, 1)
            dve.wait_ge(wstep, 10)
            dve.wait_ge(rooted, 1)
            refine_root(dve, step, 3, var[:], root[:], tmp)
            dve.wait_ge(step, 8)
            dve.tensor_tensor(big[:], big[:], tmp[:, 3], ALU.mult).then_inc(step, 1)
            dve.wait_ge(step, 9)
            dve.tensor_scalar(big[:], big[:], 1e-5, None, ALU.max).then_inc(step, 1)
            dve.wait_ge(step, 10)
            dve.reciprocal(cut[:], big[:]).then_inc(step, 1)
            dve.wait_ge(step, 11)
            dve.tensor_scalar(cut[:], cut[:], 127.0, None, ALU.mult).then_inc(step, 1)
            dve.tensor_scalar(back[:], big[:], 1.0 / 127.0, mean[:, 0:1], ALU.mult, ALU.mult).then_inc(step, 1)
            dve.wait_ge(step, 13)
            for t in range(NT):
                ins = dve.tensor_scalar(xs[:, t, :], xn[:, t, :], tmp[:, 3, t:t + 1], cut[:, t:t + 1], ALU.mult, ALU.mult)
            ins.then_inc(step, 1)
            dve.wait_ge(step, 14)
            dve.tensor_scalar(xs[:], xs[:], MAGIC, MAGIC, ALU.add, ALU.subtract).then_inc(step, 1)
            dve.wait_ge(step, 15)
            dve.tensor_scalar(xq[:], xs[:], 127.0, -128.0, ALU.min, ALU.max).then_inc(step, 1)
            dve.wait_ge(b_kept, 1)
            for t in range(NT):
                dve.wait_ge(up_made, t + 1)
                dve.scalar_tensor_tensor(h[:, t, :], up[t % 2][:], back[:, t:t + 1], b_all[:, 0:F],
                                         ALU.mult, ALU.add).then_inc(scaled, 1)
                if t >= 1:
                    dve.wait_ge(gelued, t)
                    dve.tensor_reduce(big2[:, t - 1:t], h[:, t - 1, :], AX.X, ALU.max,
                                      apply_absolute_value=True).then_inc(hstep, 1)
            dve.wait_ge(gelued, NT)
            dve.tensor_reduce(big2[:, NT - 1:NT], h[:, NT - 1, :], AX.X, ALU.max,
                              apply_absolute_value=True).then_inc(hstep, 1)
            dve.wait_ge(squared, NT)
            dve.tensor_scalar(var2[:], ms2[:], 1.0 / F, 1e-6, ALU.mult, ALU.add).then_inc(hstep, 1)
            dve.wait_ge(rooted, 2)
            refine_root(dve, hstep, NT + 1, var2[:], root2[:], tmp2)
            dve.wait_ge(hstep, NT + 6)
            dve.tensor_tensor(big2[:], big2[:], tmp2[:, 3], ALU.mult).then_inc(hstep, 1)
            dve.wait_ge(hstep, NT + 7)
            dve.tensor_scalar(big2[:], big2[:], 1e-5, None, ALU.max).then_inc(hstep, 1)
            dve.wait_ge(hstep, NT + 8)
            dve.reciprocal(cut2[:], big2[:]).then_inc(hstep, 1)
            dve.wait_ge(hstep, NT + 9)
            dve.tensor_scalar(cut2[:], cut2[:], 127.0, None, ALU.mult).then_inc(hstep, 1)
            dve.tensor_scalar(back2[:], big2[:], 1.0 / 127.0, mean[:, 1:2], ALU.mult, ALU.mult).then_inc(hstep, 1)
            dve.wait_ge(hstep, NT + 11)
            dve.wait_ge(x_in, 16)
            dve.tensor_tensor(x[:], x[:], b_all[:, F:].unsqueeze(1).broadcast_to([P, NT, D]), ALU.add).then_inc(hstep, 1)

            def add_out(t):
                dve.wait_ge(down_made, t + 1)
                dve.scalar_tensor_tensor(y[:, t, :], down[t % 2][:, 0:D], back2[:, t:t + 1], x[:, t, :],
                                         ALU.mult, ALU.add).then_inc(added, 1)

            for t in range(NT):
                dve.tensor_scalar(h[:, t, :], h[:, t, :], tmp2[:, 3, t:t + 1], cut2[:, t:t + 1], ALU.mult, ALU.mult).then_inc(biased, 1)
                dve.wait_ge(biased, 2 * t + 1)
                dve.tensor_scalar(h[:, t, :], h[:, t, :], MAGIC, MAGIC, ALU.add, ALU.subtract).then_inc(biased, 1)
                dve.wait_ge(biased, 2 * t + 2)
                dve.tensor_scalar(hq[:, t, :], h[:, t, :], 127.0, -128.0, ALU.min, ALU.max).then_inc(hstep, 1)
                if t >= 2:
                    add_out(t - 2)
            add_out(NT - 2)
            add_out(NT - 1)


def perceiver(nc, a, out, stages=range(1, 7)):
    with ExitStack() as stack:
        c = Ctx(nc)
        first_in = [stack.enter_context(nc.semaphore(f"first_in{i}")) for i in range(2)]
        x_rows = nc.dram_tensor("x_rows", [N, D], F32, kind="Internal")
        o_rows = nc.dram_tensor("o_rows", [B, P, 1024], F32, kind="Internal")
        sum_rows = nc.dram_tensor("sum_rows", [B, P, 1024], F32, kind="Internal")
        q0 = nc.dram_tensor("q0", [3, 256, N], BF16, kind="Internal")
        q1 = nc.dram_tensor("q1", [3, 512, N], BF16, kind="Internal")
        k0 = nc.dram_tensor("k0", [2, 3, 256, CH], BF16, kind="Internal")
        v0 = nc.dram_tensor("v0", [B * S2, 16 * 17], F32, kind="Internal")
        v1 = nc.dram_tensor("v1", [B * S2, 8 * 64], F32, kind="Internal")
        bias_qk = nc.dram_tensor("bias_qk", [S, S2], F32, kind="Internal")
        bias_kq = nc.dram_tensor("bias_kq", [S2, S], F32, kind="Internal")
        ident = stack.enter_context(nc.sbuf_tensor("ident", [P, P], F32))
        identb = stack.enter_context(nc.sbuf_tensor("identb", [P, P], BF16))
        ones = stack.enter_context(nc.sbuf_tensor("ones", [P, P], F32))
        with c.stage():
            constants(c, ident, identb, ones, a["x"], x_rows, "c_")

        def normed(s, tag):
            xn = s.enter_context(nc.sbuf_tensor(tag + "xn", [P, NT, D], F32))
            xnT = s.enter_context(nc.sbuf_tensor(tag + "xnT", [P, KT, N], F32))
            layer_norm(c, x_rows, xn, xnT, ident, tag)
            return xn, xnT

        if 1 in stages:
            with c.stage():
                short = stack.enter_context(nc.sbuf_tensor("short", [1, 1], mybir.dt.int32))
                with ExitStack() as s:
                    mask_in, lead_in = c.sem("mask_in"), [c.sem(f"lead_in{b}") for b in range(B)]
                    m = s.enter_context(nc.sbuf_tensor("m", [P, QT, S2], F32))
                    lead = [s.enter_context(nc.sbuf_tensor(f"lead{b}", [P, LAST // P * D], F32)) for b in range(B)]
                    q_max = s.enter_context(nc.sbuf_tensor("q_max", [P, 1], F32))

                    def prefetch(act):
                        act.dma_start(m[:], a["mask_1x1xSxS2_fk1"][0, 0].rearrange("(i p) k -> p i k", p=P)).then_inc(mask_in, 16)
                        for b in range(B):
                            act.dma_start(lead[b][:], a["ctx_1024"][b, 0:LAST].rearrange("(p t) c -> p (t c)", p=P)
                                          ).then_inc(lead_in[b], 16)

                    with ExitStack() as t:
                        _, xnT = normed(t, "n0_")
                        split_queries(c, xnT, a["L0_xattn_wq"], a["L0_xattn_bq"], 0.25, 256, q0, "q0_", prefetch, q_max[:])
                    scale_mask(c, m, mask_in, LAST, S2, None, bias_qk, bias_kq, ident, "m1_")
                    survey(c, m, mask_in, lead, lead_in, a["L0_xattn_wk"], a["L0_xattn_bk"], q_max[:], 16, short, ident, "sv_")
                    scale_mask(c, m, mask_in, 0, LAST, short, bias_qk, bias_kq, ident, "m0_")
                cross_attention(c, 16, a["ctx_1024"], a["L0_xattn_wk"], a["L0_xattn_bk"], a["L0_xattn_wv"], q0, k0, v0, o_rows,
                                None, bias_qk, bias_kq, short, first_in[0], ident, ones, "a0_")
                project_heads(c, 16, o_rows, None, a["L0_xattn_bv"], a["L0_xattn_wo"], a["L0_xattn_bo"], x_rows, ones, "p0_")
        if 2 in stages:
            with c.stage(), ExitStack() as s:
                _, xnT = normed(s, "n1_")
                channel_attention(c, xnT, a["L0_attn_Wqk"], a["L0_attn_Wv"], a["L0_attn_Wo"], a["L0_attn_tau"], x_rows,
                                  ident, ones, "ch_")
        if 3 in stages:
            with c.stage(), ExitStack() as s:
                _, xnT = normed(s, "n2_")
                gate = s.enter_context(nc.sbuf_tensor("gate", [P, NT, 8], F32))
                onesb = s.enter_context(nc.sbuf_tensor("onesb", [P, P], BF16))
                route(c, xnT, a["L0_ffn_Wg"], gate, ones, onesb, "r_")
                experts(c, xnT, gate, a["L0_ffn_W_in"], a["L0_ffn_W_out"], x_rows, "e_")
        if 4 in stages:
            with c.stage():
                with ExitStack() as s:
                    _, xnT = normed(s, "n3_")
                    split_queries(c, xnT, a["L1_xattn_Wq"], None, 0.125, 512, q1, "q1_")
                cross_attention(c, 8, a["ctx_1024"], a["L1_xattn_Wk"], None, a["L1_xattn_Wv"], q1, None, v1, o_rows,
                                sum_rows, None, None, None, first_in[1], ident, ones, "a1_")
                project_heads(c, 8, o_rows, sum_rows, None, a["L1_xattn_Wo"], a["L1_xattn_bo"], x_rows, ones, "p1_")
        if 5 in stages:
            with c.stage(), ExitStack() as s:
                xn, xnT = normed(s, "n4_")
                self_attention(c, xn, xnT, a["L1_attn_norm_w"], a["L1_attn_Wq"], a["L1_attn_Wk"], a["L1_attn_Wv"],
                               a["L1_attn_Wo"], a["L1_attn_gate"], a["L1_attn_log_temperature"], x_rows, ident, ones, "s_")
        if 6 in stages:
            with c.stage(), ExitStack() as s:
                xn, _ = normed(s, "n5_")
                feed_forward(c, xn, a["L1_ffn_w1"], a["L1_ffn_b1"], a["L1_ffn_w2"], a["L1_ffn_b2"], x_rows, out,
                             identb, ones, "f_")


_INS = ["x", "ctx_1024", "mask_1x1xSxS2_fk1", "L0_xattn_wq", "L0_xattn_bq", "L0_xattn_wk", "L0_xattn_bk",
        "L0_xattn_wv", "L0_xattn_bv", "L0_xattn_wo", "L0_xattn_bo", "L0_attn_Wqk", "L0_attn_Wv", "L0_attn_Wo",
        "L0_attn_tau", "L0_ffn_Wg", "L0_ffn_W_in", "L0_ffn_W_out", "L1_xattn_Wq", "L1_xattn_Wk", "L1_xattn_Wv",
        "L1_xattn_Wo", "L1_xattn_bo", "L1_attn_norm_w", "L1_attn_Wq", "L1_attn_Wk", "L1_attn_Wv", "L1_attn_Wo",
        "L1_attn_gate", "L1_attn_log_temperature", "L1_ffn_w1", "L1_ffn_b1", "L1_ffn_w2", "L1_ffn_b2"]


def kernel(**inputs):
    import numpy as np
    from concourse import bacc
    from concourse.bass_utils import run_bass_kernel_spmd

    nc = bacc.Bacc("TRN2", target_bir_lowering=False, num_devices=1)
    arrays, args = {}, {}
    for name in _INS:
        v = np.ascontiguousarray(inputs[name])
        if v.ndim == 0:
            v = v.reshape(1, 1)
        arrays[name + "_in"] = v
        args[name] = nc.dram_tensor(name + "_in", v.shape, mybir.dt.from_np(v.dtype), kind="ExternalInput").ap()
    out = nc.dram_tensor("out", (B, S, D), F32, kind="ExternalOutput").ap()
    perceiver(nc, args, out)
    r = run_bass_kernel_spmd(nc, [arrays], core_ids=[0])
    return r.results[0]["out"]
```

```python
from contextlib import ExitStack, contextmanager

import concourse.bass as bass
from concourse import mybir

F32 = mybir.dt.float32
BF16 = mybir.dt.bfloat16
U32 = mybir.dt.uint32
ALU = mybir.AluOpType
ACT = mybir.ActivationFunctionType
AX = mybir.AxisListType

P = 128
D = 256
KT = D // P
B = 4
S = 256
QT = S // P
N = B * S
NT = N // P
S2 = 4096
CH = 512
TPC = CH // P
PAIRS = S2 // CH // 2
UNITS = 16
NEG = -1.0e30
LOWEST = -3.0e38
MAGIC = 12582912.0


class Ctx:

    def __init__(self, nc):
        self.nc = nc
        self.stack = None
        self.held = []

    def sem(self, name):
        self.held.append(self.stack.enter_context(self.nc.semaphore(name)))
        return self.held[-1]

    @contextmanager
    def stage(self):
        with ExitStack() as self.stack:
            yield
            with self.nc.Block() as block:
                @block.gpsimd
                def _(pool):
                    for held in self.held:
                        pool.sem_clear(held)
            self.held = []


def constants(c, ident, identb, ones, tag):
    nc = c.nc
    cleared, made = c.sem(tag + "cleared"), c.sem(tag + "made")
    with nc.Block() as block:
        @block.gpsimd
        def _(pool):
            pool.memset(ident[:], 0.0).then_inc(cleared, 1)
            pool.memset(ones[:], 1.0).then_inc(cleared, 1)
            pool.wait_ge(cleared, 2)
            pool.affine_select(out=ident[:], in_=ident[:], compare_op=ALU.not_equal, fill=1.0, base=0,
                               pattern=[[-1, P]], channel_multiplier=1).then_inc(made, 1)
            pool.wait_ge(made, 1)
            pool.tensor_copy(identb[:], ident[:]).then_inc(made, 1)


def layer_norm(c, x_from, x, xn, xnT, ident, tag):
    nc = c.nc
    x_loaded, stats, root, normed = (c.sem(tag + n) for n in ("x_loaded", "stats", "root", "normed"))
    turned, kept = c.sem(tag + "turned"), c.sem(tag + "kept")
    with ExitStack() as s:
        st = s.enter_context(nc.sbuf_tensor(tag + "st", [P, NT, 6], F32))
        mv = s.enter_context(nc.sbuf_tensor(tag + "mv", [P, NT, 2], F32))
        var = s.enter_context(nc.sbuf_tensor(tag + "var", [P, NT], F32))
        std = s.enter_context(nc.sbuf_tensor(tag + "std", [P, NT], F32))
        r = s.enter_context(nc.sbuf_tensor(tag + "r", [P, 5, NT], F32))
        ps = [s.enter_context(nc.psum_tensor(f"{tag}ps{i}", [P, 512], F32)) for i in range(8)]
        block = s.enter_context(nc.Block())

        @block.sync
        def _(sp):
            if x_from is not None:
                sp.dma_start(x[:], x_from.rearrange("(t p) d -> p t d", p=P)).then_inc(x_loaded, 16)

        @block.vector
        def _(dve):
            if x_from is not None:
                dve.wait_ge(x_loaded, 16)
            for t in range(NT):
                dve.bn_stats(st[:, t, :], x[:, t, :]).then_inc(stats, 1)
            dve.wait_ge(stats, NT)
            for t in range(NT):
                dve.bn_aggr(mv[:, t, :], st[:, t, :]).then_inc(stats, 1)
            dve.wait_ge(stats, 2 * NT)
            dve.tensor_scalar(var[:], mv[:, :, 1], 1e-5, None, ALU.add).then_inc(stats, 1)
            dve.wait_ge(root, 1)
            dve.reciprocal(r[:, 0, :], std[:]).then_inc(stats, 1)
            dve.wait_ge(stats, 2 * NT + 2)
            dve.tensor_tensor(r[:, 1, :], r[:, 0, :], r[:, 0, :], ALU.mult).then_inc(stats, 1)
            dve.wait_ge(stats, 2 * NT + 3)
            dve.tensor_tensor(r[:, 2, :], r[:, 1, :], var[:], ALU.mult).then_inc(stats, 1)
            dve.wait_ge(stats, 2 * NT + 4)
            dve.tensor_scalar(r[:, 3, :], r[:, 2, :], -0.5, 1.5, ALU.mult, ALU.add).then_inc(stats, 1)
            dve.wait_ge(stats, 2 * NT + 5)
            dve.tensor_tensor(r[:, 4, :], r[:, 3, :], r[:, 0, :], ALU.mult).then_inc(stats, 1)
            dve.wait_ge(stats, 2 * NT + 6)
            for t in range(NT):
                dve.tensor_scalar(xn[:, t, :], x[:, t, :], mv[:, t, 0:1], r[:, 4, t:t + 1],
                                  ALU.subtract, ALU.mult).then_inc(normed, 1)

        @block.tensor
        def _(pe):
            for t in range(NT):
                pe.wait_ge(normed, t + 1)
                for k in range(KT):
                    mm = pe.transpose(ps[t][:, k * P:(k + 1) * P], xn[:, t, k * P:(k + 1) * P], ident[:])
                mm.then_inc(turned, 1)

        @block.scalar
        def _(act):
            act.wait_ge(stats, 2 * NT + 1)
            act.activation(std[:], var[:], ACT.Sqrt).then_inc(root, 1)
            for t in range(NT):
                act.wait_ge(turned, t + 1)
                act.activation(xnT[:, :, t * P:(t + 1) * P],
                               ps[t][:, 0:D].rearrange("p (k n) -> p k n", k=KT), ACT.Copy).then_inc(kept, 1)
            act.wait_ge(kept, NT)


def split_queries(c, xnT, w_q, b_q, scale, HD, qs, tag, prefetch=None, measure=None, x=None,
                  x_to=None):
    nc = c.nc
    G = HD // P
    w_loaded, q_ready, q_cut, q_left, q_stored = (c.sem(tag + n) for n in
                                                  ("w_loaded", "q_ready", "q_cut", "q_left", "q_stored"))
    with ExitStack() as s:
        w = s.enter_context(nc.sbuf_tensor(tag + "w", [P, KT, HD], F32))
        bias = s.enter_context(nc.sbuf_tensor(tag + "bias", [P, G], F32))
        q = s.enter_context(nc.sbuf_tensor(tag + "q", [P, G, N], F32))
        rest = s.enter_context(nc.sbuf_tensor(tag + "rest", [P, G, N], F32))
        parts = s.enter_context(nc.sbuf_tensor(tag + "parts", [P, 3, G, N], BF16))
        ps = [s.enter_context(nc.psum_tensor(f"{tag}ps{i}", [P, 512], F32)) for i in range(8)]
        block = s.enter_context(nc.Block())
        loads = 32 if b_q is not None else 16
        halves = N // 512

        @block.sync
        def _(sp):
            sp.dma_start(w[:], w_q.rearrange("(k p) n -> p k n", p=P)).then_inc(w_loaded, 16)
            if b_q is not None:
                sp.dma_start(bias[:], b_q.rearrange("(g p) -> p g", p=P),
                             allow_slow_non_contiguous=True).then_inc(w_loaded, 16)
            if x_to is not None:
                sp.dma_start(x_to.rearrange("(t p) d -> p t d", p=P), x[:]).then_inc(q_stored, 16)
            for i, part_of in enumerate((1, 3, 4)):
                sp.wait_ge(q_cut, part_of * G)
                sp.dma_start(qs.ap()[i].rearrange("(g p) n -> p g n", p=P), parts[:, i]).then_inc(q_stored, 16)
            sp.wait_ge(q_stored, 48 if x_to is None else 64)

        @block.tensor
        def _(pe):
            pe.wait_ge(w_loaded, loads)
            for g in range(G):
                for half in range(halves):
                    for k in range(KT):
                        mm = pe.matmul(ps[(g * halves + half) % 8][:], w[:, k, g * P:(g + 1) * P],
                                       xnT[:, k, half * 512:(half + 1) * 512], start=k == 0, stop=k == KT - 1)
                    mm.then_inc(q_ready, 1)

        @block.scalar
        def _(act):
            if prefetch is not None:
                prefetch(act)
            act.wait_ge(w_loaded, loads)
            for g in range(G):
                for half in range(halves):
                    act.wait_ge(q_ready, g * halves + half + 1)
                    act.activation(q[:, g, half * 512:(half + 1) * 512], ps[(g * halves + half) % 8][:],
                                   ACT.Identity, bias=bias[:, g:g + 1] if b_q is not None else 0.0).then_inc(q_left, 1)

        @block.vector
        def _(dve):
            dve.wait_ge(q_left, G * halves)
            for g in range(G):
                dve.tensor_scalar(parts[:, 0, g, :], q[:, g, :], scale, None, ALU.mult).then_inc(q_cut, 1)
            dve.wait_ge(q_cut, G)
            for g in range(G):
                dve.scalar_tensor_tensor(rest[:, g, :], q[:, g, :], scale, parts[:, 0, g, :],
                                         ALU.mult, ALU.subtract).then_inc(q_cut, 1)
            dve.wait_ge(q_cut, 2 * G)
            for g in range(G):
                dve.tensor_copy(parts[:, 1, g, :], rest[:, g, :]).then_inc(q_cut, 1)
            dve.wait_ge(q_cut, 3 * G)
            for g in range(G):
                dve.tensor_tensor(parts[:, 2, g, :], rest[:, g, :], parts[:, 1, g, :],
                                  ALU.subtract).then_inc(q_cut, 1)
            if measure is not None:
                measure(dve, q[:].rearrange("p g n -> p (g n)"))


LAST = S2 - 2 * CH


def scale_mask(c, m, mask_in, lo, hi, short, bias_qk, bias_kq, ident, tag):
    nc = c.nc
    scaled, turned, kept, stored = (c.sem(tag + n) for n in ("scaled", "turned", "kept", "stored"))
    KEYS = (hi - lo) // P
    with ExitStack() as s:
        mT = s.enter_context(nc.sbuf_tensor(tag + "mT", [P, KEYS, S], F32))
        ps = [s.enter_context(nc.psum_tensor(f"{tag}ps{i}", [P, 512], F32)) for i in range(8)]
        block = s.enter_context(nc.Block())

        def where_needed(eng, run):
            if short is None:
                run()
            else:
                last_only = eng.value_load(short[0:1, 0:1], min_val=0, max_val=1)
                with eng.If(last_only == 0):
                    run()

        @block.sync
        def _(sp):
            def run():
                sp.wait_ge(scaled, QT)
                sp.dma_start(bias_qk.ap()[:, lo:hi].rearrange("(i p) k -> p i k", p=P), m[:, :, lo:hi]).then_inc(stored, 16)
                sp.wait_ge(kept, KEYS // 2)
                sp.dma_start(bias_kq.ap()[lo:hi].rearrange("(t p) q -> p t q", p=P), mT[:]).then_inc(stored, 16)
                sp.wait_ge(stored, 32)

            where_needed(sp, run)

        @block.vector
        def _(dve):
            def run():
                dve.wait_ge(mask_in, 16)
                for i in range(QT):
                    dve.tensor_scalar(m[:, i, lo:hi], m[:, i, lo:hi], -1.0e9, None, ALU.mult).then_inc(scaled, 1)

            where_needed(dve, run)

        @block.tensor
        def _(pe):
            def run():
                pe.wait_ge(scaled, QT)
                for t in range(KEYS):
                    if t % 2 == 0 and t >= 16:
                        pe.wait_ge(kept, t // 2 - 7)
                    for i in range(QT):
                        at = (t % 2) * S + i * P
                        mm = pe.transpose(ps[t // 2 % 8][:, at:at + P], m[:, i, lo + t * P:lo + (t + 1) * P], ident[:])
                    mm.then_inc(turned, 1)

            where_needed(pe, run)

        @block.scalar
        def _(act):
            def run():
                for t in range(0, KEYS, 2):
                    act.wait_ge(turned, t + 2)
                    act.activation(mT[:, t:t + 2, :], ps[t // 2 % 8][:].rearrange("p (t q) -> p t q", t=2),
                                   ACT.Copy).then_inc(kept, 1)

            where_needed(act, run)


def survey(c, low, lead, lead_in, part, w_k, b_k, q_max, dh, short, ident, tag):
    nc = c.nc
    w_in, step, turned = c.sem(tag + "w_in"), c.sem(tag + "step"), c.sem(tag + "turned")
    with ExitStack() as s:
        def sb(n, shape, dt=F32):
            return s.enter_context(nc.sbuf_tensor(tag + n, shape, dt))

        wk, bk = sb("wk", [P, KT * D]), sb("bk", [1, D])
        pack, most, row, term = sb("pack", [P, 8]), sb("most", [8, 1]), sb("row", [1, 8]), sb("term", [1, 8])
        ps = [s.enter_context(nc.psum_tensor(f"{tag}ps{i}", [P, 512], F32)) for i in range(2)]
        block = s.enter_context(nc.Block())

        @block.sync
        def _(sp):
            sp.dma_start(wk[:].rearrange("p (k n) -> p k n", k=KT), w_k.rearrange("(k p) n -> p k n", p=P)).then_inc(w_in, 16)
            sp.dma_start(bk[:], b_k.rearrange("(a n) -> a n", a=1)).then_inc(w_in, 16)

        @block.tensor
        def _(pe):
            pe.wait_ge(step, 4)
            pe.transpose(ps[0][0:8, 0:P], pack[:], ident[:]).then_inc(turned, 1)
            pe.wait_ge(step, 5)
            pe.transpose(ps[1][0:1, 0:8], most[:], ident[0:8, 0:8]).then_inc(turned, 1)

        @block.vector
        def _(dve):
            dve.memset(pack[:], 0.0).then_inc(step, 1)
            dve.wait_ge(step, 1)
            dve.wait_ge(w_in, 32)
            dve.tensor_copy(pack[:, 3:4], q_max)
            dve.tensor_reduce(pack[:, 4:5], wk[:], AX.X, ALU.max, apply_absolute_value=True)
            dve.tensor_reduce(pack[0:1, 5:6], bk[:], AX.X, ALU.max, apply_absolute_value=True)
            dve.wait_ge(lead_in[B - 1], 16)
            dve.tensor_reduce(part[:, B - 1:B], lead[B - 1][:], AX.X, ALU.max, apply_absolute_value=True).then_inc(step, 1)
            dve.wait_ge(step, 2)
            dve.tensor_reduce(pack[:, 0:1], low[:, 0:QT], AX.X, ALU.min)
            dve.tensor_reduce(pack[:, 1:2], low[:, QT:2 * QT], AX.X, ALU.max)
            dve.tensor_reduce(pack[:, 2:3], part[:], AX.X, ALU.max).then_inc(step, 1)
            dve.wait_ge(step, 3)
            dve.tensor_scalar(pack[:, 0:1], pack[:, 0:1], -1.0, None, ALU.mult).then_inc(step, 1)
            dve.wait_ge(turned, 1)
            dve.tensor_reduce(most[:], ps[0][0:8, 0:P], AX.X, ALU.max).then_inc(step, 1)
            dve.wait_ge(turned, 2)
            dve.tensor_copy(row[:], ps[1][0:1, 0:8]).then_inc(step, 1)
            dve.wait_ge(step, 6)
            dve.scalar_tensor_tensor(term[:, 0:1], row[:, 2:3], float(D), row[:, 4:5], ALU.mult, ALU.mult).then_inc(step, 1)
            dve.wait_ge(step, 7)
            dve.tensor_tensor(term[:, 1:2], term[:, 0:1], row[:, 5:6], ALU.add).then_inc(step, 1)
            dve.wait_ge(step, 8)
            dve.scalar_tensor_tensor(term[:, 2:3], term[:, 1:2], float(dh), row[:, 3:4], ALU.mult, ALU.mult).then_inc(step, 1)
            dve.wait_ge(step, 9)
            dve.tensor_scalar(term[:, 3:4], row[:, 0:1], -1.0, None, ALU.is_le)
            dve.tensor_scalar(term[:, 4:5], row[:, 1:2], 0.0, None, ALU.is_le)
            dve.tensor_scalar(term[:, 5:6], term[:, 2:3], 1.0e8, None, ALU.is_le).then_inc(step, 1)
            dve.wait_ge(step, 10)
            dve.tensor_tensor(term[:, 6:7], term[:, 3:4], term[:, 4:5], ALU.mult).then_inc(step, 1)
            dve.wait_ge(step, 11)
            dve.tensor_tensor(short[:], term[:, 6:7], term[:, 5:6], ALU.mult).then_inc(step, 1)
            dve.wait_ge(step, 12)


def cross_attention(c, H, ctx, w_k, b_k, w_v, qs, k_rows, v_rows, o_rows, sum_rows, bias_qk, bias_kq, short,
                    first_in, ident, ones, tag):
    nc = c.nc
    masked = bias_qk is not None
    small = H == 16
    dh = 16 if small else 64
    HD = H * dh
    G = HD // P
    VW = dh + 1 if small else dh
    HV = H * VW
    VU = G
    TPV = TPC // VU
    UM = H * QT
    SETS = H * TPC // 4
    HS = 4 if small else 2
    TS = 4 // HS
    CHUNKS = 2 * PAIRS
    SLOT_K, SLOT_Q = (0, 0, 1, 1, 0, 2), (0, 1, 0, 1, 2, 0)
    KQ = 6 * dh if small else P
    STEPS = "tkkvv" if small else "tkkvkvkvv"
    ACT_STEPS = "kksvsv" if small else "kksvskvkvsvs"
    POOL_STEPS = "rrtt" if small else "rrttrtrt"
    NPARTS = 3 if small else 2
    ND = 6 if small else 4
    NDQ = 6 if small else 8
    NDO = 1 if small else 2
    ONE, M0, S0 = 16, 2 * UM, 2 * SETS

    def sem(n):
        return c.sem(tag + n)

    w_loaded, ones_set, ones_put = sem("w_loaded"), sem("ones_set"), sem("ones_put")
    ctx_in, q_in, max_in, o_out, k_out = sem("ctx_in"), sem("q_in"), sem("max_in"), sem("o_out"), sem("k_out")
    bias_in, v_out, v_in, biasT_in = ([sem(f"{n}{u}") for u in range(2)] for n in
                                      ("bias_in", "v_out", "v_in", "biasT_in"))
    keys_in = [[sem(f"keys_in{u}{half}") for half in range(2)] for u in range(2)]
    ctx_turned, ctxT_kept = sem("ctx_turned"), sem("ctxT_kept")
    k_made, k_kept, k_half, k_rest, k_cut2, k_cut3 = (sem(n) for n in
                                                      ("k_made", "k_kept", "k_half", "k_rest", "k_cut2", "k_cut3"))
    v_made, v_kept = sem("v_made"), sem("v_kept")
    scored, reduced, folded, best_reset = sem("scored"), sem("reduced"), sem("folded"), sem("best_reset")
    negated, max_turned, max_cut, acc_reset = sem("negated"), sem("max_turned"), sem("max_cut"), sem("acc_reset")
    out_reset, set_scored, biased, probs, used = (sem(n) for n in ("out_reset", "set_scored", "biased", "probs", "used"))
    summed, sums_made, o_kept, inverted = sem("summed"), sem("sums_made"), sem("o_kept"), sem("inverted")

    LOADS = 32 if b_k is None else 48

    def choose(eng, run):
        if short is None:
            run()
        else:
            last_only = eng.value_load(short[0:1, 0:1], min_val=0, max_val=1)
            with eng.If(last_only == 0):
                run()

    settled = {n: sem("settled_" + n) for n in ("sp", "dve", "pe", "pool")}

    def settle(eng, n):
        eng.sem_inc(settled[n], 1)

    with ExitStack() as s:
        def sb(n, shape, dt=F32):
            return s.enter_context(nc.sbuf_tensor(tag + n, shape, dt))

        keys = sb("keys", [P, PAIRS, 2 * UNITS, CH], BF16)
        query = sb("query", [P, H if small else 3 * H, S], BF16)
        ctx_sb = sb("ctx_sb", [P, TPC, D])
        ctxT = sb("ctxT", [P, KT, CH])
        work = sb("work", [P, 4096])
        value = [sb(f"value{u}", [P, TPC, HV]) for u in range(2)]
        v_stage = [sb(f"v_stage{u}", [P, TPV, H, VW]) for u in range(2)]
        wk, wv = sb("wk", [P, KT, HD]), sb("wv", [P, KT, HD])
        bk = sb("bk", [P, G])
        best, best_c, neg = sb("best", [P, UM]), sb("best_c", [P, UM]), sb("neg", [P, UM])
        neg_rest, neg_parts = sb("neg_rest", [UM, P]), sb("neg_parts", [UM, 3, P], BF16)
        if masked:
            bias = [sb(f"bias{u}", [P, QT, CH]) for u in range(2)]
            biasT = [sb(f"biasT{u}", [P, TPC, S]) for u in range(2)]
            junk = [sb(f"junk{u}", [P, CH], BF16) for u in range(2)]
        if not small:
            shift, onesb = sb("shift", [P, H, S], BF16), sb("onesb", [P, P], BF16)
            acc = sb("acc", [P, H, S])
        kf = [work[:, g * CH:(g + 1) * CH] for g in range(2)]
        rest = [work[:, (2 + g) * CH:(3 + g) * CH] for g in range(2)]
        kparts = work[:, 2048:4096].bitcast(BF16)[:, 0:NPARTS * G * CH].rearrange("p (i g n) -> p i g n", i=NPARTS, g=G)
        out_sb = value[0][:].rearrange("p t c -> p (t c)")[:, 0:1024]
        sum_sb = None if small else value[0][:].rearrange("p t c -> p (t c)")[:, 1024:2048]
        slot = [work[:, i * 1024:(i + 1) * 1024] for i in range(4)]
        bank = [s.enter_context(nc.psum_tensor(f"{tag}bank{i}", [P, 512], F32)) for i in range(4)]
        duo = [s.enter_context(nc.psum_tensor(f"{tag}duo{i}", [P, 1024], F32)) for i in range(2)]
        quad = [duo[i // 2][:, i % 2 * 512:i % 2 * 512 + 512] for i in range(4)]
        block = s.enter_context(nc.Block())

        @block.sync
        def _(sp):
            sp.dma_start(wk[:], w_k.rearrange("(k p) n -> p k n", p=P)).then_inc(w_loaded, 16)
            sp.dma_start(wv[:], w_v.rearrange("(k p) n -> p k n", p=P)).then_inc(w_loaded, 16)
            if b_k is not None:
                sp.dma_start(bk[:], b_k.rearrange("(g p) -> p g", p=P),
                             allow_slow_non_contiguous=True).then_inc(w_loaded, 16)
            for half in range(2):
                sp.sem_inc(keys_in[1][half], ONE)
            sp.sem_inc(o_out, ONE)
            sp.sem_inc(v_out[0], ONE)
            sp.sem_inc(v_out[1], ONE)
            def run():
                if small:
                    sp.wait_ge(ones_set, 1)
                    for p in range(PAIRS):
                        for u in range(4):
                            sp.dma_start(keys[KQ:KQ + 3, p, u * 8:(u + 1) * 8, :],
                                         work[KQ:KQ + 3, 0:2048].bitcast(BF16).rearrange("p (a n) -> p a n", a=8)
                                         ).then_inc(ones_put, 16)
                with sp.Fori(0, B) as b:
                    sp.wait_ge(o_kept, b + ONE)
                    mine = bass.ds(b * S, S)
                    if small:
                        for i, part in enumerate(SLOT_Q):
                            sp.dma_start(query[i * dh:(i + 1) * dh, :, :],
                                         qs.ap()[part, :, mine].rearrange("(h d) q -> d h q", d=dh)).then_inc(q_in, 16)
                    else:
                        for part in range(2):
                            for row in (0, dh):
                                sp.dma_start(query[row:row + dh, part * H:(part + 1) * H, :],
                                             qs.ap()[part, :, mine].rearrange("(h d) q -> d h q", d=dh)).then_inc(q_in, 16)
                        for odd in range(2):
                            for top, part in ((0, 0 if odd else 2), (dh, 2 if odd else 0)):
                                sp.dma_start(query[top:top + dh, 2 * H + odd:3 * H:2, :],
                                             qs.ap()[part, :, mine].rearrange("(h o d) q -> o d h q", d=dh, o=2)[odd]
                                             ).then_inc(q_in, 16)

                    def load_bias(p, u):
                        if masked:
                            sp.wait_ge(reduced, (b * CHUNKS + p * 2) * UM + (u * UM - UM + M0))
                            settle(sp, "sp")
                            sp.dma_start(bias[u][:], bias_qk.ap()[:, bass.ds(p * 2 * CH + u * CH, CH)]
                                         .rearrange("(i q) k -> q i k", q=P)).then_inc(bias_in[u], 16)

                    def store_chunk(p, u):
                        n = b * CHUNKS + p * 2

                        def store_values(v):
                            sp.wait_ge(v_kept, n * VU + (u * VU + v + 1 + ONE))
                            rows = bass.ds(b * S2 + p * 2 * CH + (u * CH + v * TPV * P), TPV * P)
                            sp.dma_start(v_rows.ap()[rows, :].rearrange("(t k) c -> k t c", k=P),
                                         v_stage[v % 2][:].rearrange("p t h w -> p t (h w)")).then_inc(v_out[v % 2], 16)

                        def store_keys(half):
                            gs = slice(half * G // 2, (half + 1) * G // 2)
                            sp.wait_ge(k_cut2, n * G + u * G + gs.stop)
                            sp.wait_ge(k_cut3, n * G + u * G + gs.stop)
                            if small:
                                rows = k_rows.ap()[u, :, half * P:(half + 1) * P, :]
                                sp.dma_start(rows.rearrange("i k n -> k i n"), kparts[:, :, half]).then_inc(k_out, 16)
                                sp.wait_ge(k_out, n * 32 + (u * 32 + half * 16 + 16))
                                at = u * UNITS + half * 8
                                for i, part in enumerate(SLOT_K):
                                    sp.dma_start(keys[i * dh:(i + 1) * dh, bass.ds(p, 1), at:at + 8, :]
                                                 .rearrange("d p h n -> d (p h) n"),
                                                 rows[part].rearrange("(h d) n -> d h n", d=dh)).then_inc(keys_in[u][half], 16)
                            else:
                                for part in range(2):
                                    for odd in range(2):
                                        to, at = dh * (1 - odd), u * UNITS + half * 8 + 2 * odd + part
                                        sp.dma_start(keys[to:to + dh, bass.ds(p, 1), at:u * UNITS + half * 8 + 8:4, :]
                                                     .rearrange("d p h n -> d (p h) n"),
                                                     kparts[dh * odd:dh * odd + dh, part, gs]).then_inc(keys_in[u][half], 16)

                        if not small:
                            store_values(0)
                        store_keys(0)
                        if not small:
                            store_values(1)
                        store_keys(1)
                        for v in range(VU - 2, VU):
                            store_values(v)

                    load_bias(0, 0)
                    with sp.Fori(0, PAIRS - 1) as p:
                        store_chunk(p, 0)
                        load_bias(p, 1)
                        store_chunk(p, 1)
                        load_bias(p + 1, 0)
                    store_chunk(PAIRS - 1, 0)
                    load_bias(PAIRS - 1, 1)
                    store_chunk(PAIRS - 1, 1)
                    sp.wait_ge(max_cut, b * 4 + 4)
                    for i in range(3):
                        row = query[KQ + i:KQ + i + 1] if small else shift[i:i + 1]
                        sp.dma_start(row.rearrange("o h (i q) -> o (h i) q", i=QT), neg_parts[:, i, :]).then_inc(max_in, 16)
                    for i in range(2):
                        sp.wait_ge(v_out[i], b * (CHUNKS * VU * 8) + (CHUNKS * VU * 8 + ONE))
                    sp.wait_ge(o_out, b * (NDO * 16) + ONE)
                    settle(sp, "sp")
                    with sp.Fori(0, PAIRS) as p:
                        n = b * CHUNKS + p * 2
                        for u in range(2):
                            sp.wait_ge(used, n * SETS + (u * SETS - SETS + S0))
                            rows = bass.ds(b * S2 + p * 2 * CH + u * CH, CH)
                            sp.dma_start(value[u][:], v_rows.ap()[rows, :].rearrange("(t k) c -> k t c", k=P)).then_inc(v_in[u], 16)
                            if masked:
                                sp.dma_start(biasT[u][:], bias_kq.ap()[bass.ds(p * 2 * CH + u * CH, CH), :]
                                             .rearrange("(t k) q -> k t q", k=P)).then_inc(biasT_in[u], 16)
                    sp.wait_ge(o_kept, b + 1 + ONE)
                    sp.dma_start(o_rows.ap()[bass.ds(b, 1)].rearrange("b p n -> (b p) n"), out_sb).then_inc(o_out, 16)
                    if not small:
                        sp.wait_ge(inverted, b + 1)
                        sp.dma_start(sum_rows.ap()[bass.ds(b, 1)].rearrange("b p n -> (b p) n"), sum_sb).then_inc(o_out, 16)
                sp.wait_ge(o_out, B * NDO * 16 + ONE)

            choose(sp, run)

        @block.gpsimd
        def _(pool):
            if small:
                pool.memset(work[96:128, 0:2048].bitcast(BF16), 1.0).then_inc(ones_set, 1)
                for u in range(2):
                    pool.wait_ge(ones_set, u + 1)
                    pool.memset(v_stage[u][:], 1.0).then_inc(ones_set, 1)
            else:
                pool.memset(onesb[:], 1.0).then_inc(ones_set, 1)
                pool.wait_ge(ones_set, 1)
                pool.memset(shift[:], 0.0).then_inc(ones_set, 1)
            pool.sem_inc(k_rest, ONE)
            def run():
                with pool.Fori(0, B) as b:
                    pool.wait_ge(ctx_turned, b * CHUNKS + ONE)
                    pool.dma_start(ctx_sb[:], ctx[bass.ds(b, 1), 0:CH, :]
                                   .rearrange("b (t k) c -> k (b t) c", k=P)).then_inc(first_in, 16)
                    if not small:
                        pool.wait_ge(o_kept, b + ONE)
                        settle(pool, "pool")
                        pool.memset(acc[:], 0.0).then_inc(acc_reset, 1)
                        pool.wait_ge(acc_reset, b + 1)
                        settle(pool, "pool")
                    with pool.Fori(0, PAIRS) as p:
                        for u in range(2):
                            m = (b * CHUNKS + p * 2) * G + u * G

                            def finished(before):
                                step, g = before
                                if not small and step == "r":
                                    pool.wait_ge(k_rest, m + (g + 1 + ONE))
                                elif not small:
                                    pool.wait_ge(k_cut3, m + (g + 1))

                            def first_rest(g):
                                pool.wait_ge(k_kept, m + (g + 1 + ONE))
                                if small:
                                    pool.tensor_tensor(rest[g % 2], kf[g % 2], kparts[:, 0, g], ALU.subtract).then_inc(k_rest, 1)
                                else:
                                    even, odd = slice(0, dh), slice(dh, P)
                                    pool.tensor_tensor(rest[g % 2][even], kf[g % 2][even],
                                                       keys[even, bass.ds(p, 1), u * UNITS + 4 * g, :].rearrange("d p n -> d (p n)"),
                                                       ALU.subtract).then_inc(k_half, 1)
                                    pool.wait_ge(k_half, m + (g + 1))
                                    pool.tensor_tensor(rest[g % 2][odd], kf[g % 2][odd],
                                                       keys[odd, bass.ds(p, 1), u * UNITS + 4 * g + 2, :].rearrange("d p n -> d (p n)"),
                                                       ALU.subtract).then_inc(k_rest, 1)

                            def third_part(g):
                                pool.wait_ge(k_cut2, m + (g + 1))
                                pool.tensor_tensor(kparts[:, NPARTS - 1, g], rest[g % 2], kparts[:, NPARTS - 2, g],
                                                   ALU.subtract).then_inc(k_cut3, 1)

                            for x, step in enumerate(POOL_STEPS):
                                if x > 0:
                                    finished((POOL_STEPS[x - 1], POOL_STEPS[:x - 1].count(POOL_STEPS[x - 1])))
                                if step == "r":
                                    first_rest(POOL_STEPS[:x].count(step))
                                else:
                                    third_part(POOL_STEPS[:x].count(step))
                            finished(("t", G - 1))

            choose(pool, run)

        @block.scalar
        def _(act):
            act.sem_inc(k_kept, ONE)
            act.sem_inc(v_kept, ONE)
            act.sem_inc(o_kept, ONE)
            if not masked:
                act.sem_inc(probs, S0)
            act.wait_ge(w_loaded, LOADS)
            act.wait_ge(ones_set, 3 if small else 2)
            def run():
                if small:
                    act.wait_ge(ones_put, PAIRS * 4 * 16)
                with act.Fori(0, B) as b:
                    def make_pair(p, last):
                        for u in range(2):
                            n = b * CHUNKS + p * 2

                            def kparts_free(g):
                                done = b * PAIRS + p
                                if g % (G // 2) == 0:
                                    before = keys_in[1 - u][g // (G // 2)]
                                    act.wait_ge(before, done * (ND * 16) + (ND * 16 if u == 1 else ONE))

                            def second_part(g):
                                if not small:
                                    kparts_free(g)
                                act.wait_ge(k_rest, n * G + (u * G + g + 1 + ONE))
                                act.activation(kparts[:, NPARTS - 2, g], rest[g % 2], ACT.Copy).then_inc(k_cut2, 1)

                            act.wait_ge(ctx_turned, n + (u + 1 + ONE))
                            if u == 0 or not last:
                                nxt = (p * 2 + u + 1) * CH
                                act.dma_start(ctx_sb[:], ctx[bass.ds(b, 1), bass.ds(nxt, CH), :]
                                              .rearrange("b (t k) c -> k (b t) c", k=P)).then_inc(ctx_in, 16)

                            for k in range(KT):
                                ins = act.activation(ctxT[:, k, :], bank[k][:], ACT.Copy)
                            ins.then_inc(ctxT_kept, 1)

                            def keep_keys(g):
                                act.wait_ge(k_made, n * G + (u * G + g + 1))
                                act.wait_ge(k_rest, n * G + (u * G + g - 1 + ONE))
                                shifted = bk[:, g:g + 1] if b_k is not None else 0.0
                                act.activation(kf[g % 2], bank[2 + g % 2][:], ACT.Identity, bias=shifted)
                                if small:
                                    kparts_free(g)
                                    act.activation(kparts[:, 0, g], bank[2 + g % 2][:], ACT.Identity,
                                                   bias=shifted).then_inc(k_kept, 1)
                                else:
                                    for odd in range(2):
                                        rows = slice(odd * dh, odd * dh + dh)
                                        for slab in range(2):
                                            at = u * UNITS + 4 * g + 2 * odd + slab
                                            ins = act.activation(keys[rows, bass.ds(p, 1), at, :].rearrange("d p n -> d (p n)"),
                                                                 bank[2 + g % 2][rows, :], ACT.Copy)
                                    ins.then_inc(k_kept, 1)

                            def keep_values(v):
                                act.wait_ge(v_made, n * VU + (u * VU + v + 1))
                                act.wait_ge(v_out[v % 2], n * (VU * 8) + ((u * VU // 2 + v // 2) * 16 + ONE))
                                act.activation(v_stage[v % 2][:, :, :, 0:dh],
                                               bank[v % 2][:].rearrange("p (t h w) -> p t h w", t=TPV, h=H),
                                               ACT.Copy).then_inc(v_kept, 1)

                            for x, step in enumerate(ACT_STEPS):
                                g = ACT_STEPS[:x].count(step)
                                if step == "k":
                                    keep_keys(g)
                                elif step == "v":
                                    keep_values(g)
                                else:
                                    second_part(g)

                    with act.Fori(0, PAIRS - 1) as p:
                        make_pair(p, False)
                    make_pair(PAIRS - 1, True)
                    with act.Fori(0, PAIRS) as p:
                        for i in range(2 * SETS):
                            m = (b * CHUNKS + p * 2) * SETS
                            if masked:
                                act.wait_ge(biased, m + (i + 1 + S0))
                                act.activation(slot[i % 4], slot[i % 4], ACT.Exp).then_inc(probs, 1)
                            else:
                                act.wait_ge(set_scored, m + (i + 1))
                                act.wait_ge(used, m + (i - 3 + S0))
                                act.wait_ge(summed, m * TS + ((i - 3) * TS + S0))
                                act.activation(slot[i % 4], duo[i % 2][:], ACT.Exp).then_inc(probs, 1)
                    act.wait_ge(used, b * (CHUNKS * SETS) + (CHUNKS * SETS + S0))
                    if not small:
                        act.wait_ge(sums_made, b + 1)
                    act.activation(out_sb[:, 0:512], bank[0][:], ACT.Copy)
                    ins = act.activation(out_sb[:, 512:1024], bank[1][:], ACT.Copy)
                    if not small:
                        act.activation(sum_sb[:, 0:512], bank[2][:], ACT.Copy)
                        ins = act.activation(sum_sb[:, 512:1024], bank[3][:], ACT.Copy)
                    ins.then_inc(o_kept, 1)

            choose(act, run)

        @block.vector
        def _(dve):
            dve.sem_inc(reduced, M0)
            if masked:
                dve.sem_inc(biased, S0)
            if not small:
                dve.sem_inc(summed, S0)
            def run():
                with dve.Fori(0, B) as b:
                    dve.memset(best[:], LOWEST).then_inc(best_reset, 1)
                    dve.wait_ge(best_reset, b + 1)
                    settle(dve, "dve")
                    with dve.Fori(0, PAIRS) as p:
                        for u in range(2):
                            n = b * CHUNKS + p * 2
                            if masked:
                                dve.wait_ge(bias_in[u], (b * PAIRS + p) * 16 + 16)
                            for i in range(UM):
                                dve.wait_ge(scored, n * UM + (u * UM + i + 1))
                                if masked:
                                    dve.wait_ge(reduced, n * UM + (u * UM + i - 1 + M0))
                                    settle(dve, "dve")
                                    dve.tensor_tensor_reduce(junk[i % 2][:], quad[i % 4], bias[u][:, i % QT, :], 1.0, LOWEST,
                                                             ALU.add, ALU.max, best_c[:, i:i + 1]).then_inc(reduced, 1)
                                else:
                                    dve.tensor_reduce(best_c[:, i:i + 1], quad[i % 4], AX.X, ALU.max).then_inc(reduced, 1)
                            dve.wait_ge(reduced, n * UM + (u * UM + UM + M0))
                            dve.tensor_tensor(best[:], best[:], best_c[:], ALU.max).then_inc(folded, 1)
                            dve.wait_ge(folded, n + (u + 1))
                    dve.tensor_scalar(neg[:], best[:], -1.0, None, ALU.mult).then_inc(negated, 1)
                    dve.wait_ge(v_kept, b * (CHUNKS * VU) + (CHUNKS * VU + ONE))
                    dve.memset(bank[0][:], 0.0)
                    dve.memset(bank[1][:], 0.0).then_inc(out_reset, 1)
                    dve.wait_ge(max_turned, b + 1)
                    dve.tensor_copy(neg_parts[:, 0, :], quad[0][0:UM, 0:P]).then_inc(max_cut, 1)
                    dve.wait_ge(max_cut, b * 4 + 1)
                    dve.tensor_tensor(neg_rest[:], quad[0][0:UM, 0:P], neg_parts[:, 0, :], ALU.subtract).then_inc(max_cut, 1)
                    dve.wait_ge(max_cut, b * 4 + 2)
                    dve.tensor_copy(neg_parts[:, 1, :], neg_rest[:]).then_inc(max_cut, 1)
                    dve.wait_ge(max_cut, b * 4 + 3)
                    dve.tensor_tensor(neg_parts[:, 2, :], neg_rest[:], neg_parts[:, 1, :], ALU.subtract).then_inc(max_cut, 1)
                    dve.wait_ge(out_reset, b + 1)
                    if not small:
                        dve.wait_ge(acc_reset, b + 1)
                    settle(dve, "dve")
                    with dve.Fori(0, PAIRS) as p:
                        m = (b * CHUNKS + p * 2) * SETS
                        for i in range(2 * SETS):
                            u, at = i // SETS, i % SETS
                            if masked:
                                if at == 0:
                                    dve.wait_ge(biasT_in[u], (b * PAIRS + p) * 16 + 16)
                                dve.wait_ge(set_scored, m + (i + 1))
                                dve.wait_ge(used, m + (i - 3 + S0))
                                dve.tensor_tensor(slot[i % 4].rearrange("p (h q) -> p h q", h=HS),
                                                  duo[i % 2][:].rearrange("p (h q) -> p h q", h=HS),
                                                  biasT[u][:, at // 4:at // 4 + 1, :].broadcast_to([P, HS, S]),
                                                  ALU.add).then_inc(biased, 1)
                            elif not small:
                                pair = at // 2
                                dve.wait_ge(probs, m + (i + 1 + S0))
                                for t in range(TS):
                                    dve.wait_ge(summed, m * TS + (i * TS + t + S0))
                                    both = acc[:, 2 * pair:2 * pair + 2, :].rearrange("p h q -> p (h q)")
                                    dve.tensor_tensor(both, both, slot[i % 4][:, t * 512:(t + 1) * 512],
                                                      ALU.add).then_inc(summed, 1)
                    if not small:
                        dve.wait_ge(o_kept, b + 1 + ONE)
                        settle(dve, "dve")
                        dve.reciprocal(sum_sb, sum_sb).then_inc(inverted, 1)
                        dve.wait_ge(inverted, b + 1)
                        settle(dve, "dve")

            choose(dve, run)

        @block.tensor
        def _(pe):
            pe.sem_inc(ctx_turned, ONE)
            pe.sem_inc(used, S0)
            pe.wait_ge(w_loaded, LOADS)
            if not small:
                pe.wait_ge(ones_set, 2)
            PS0 = 0 if masked else S0

            def run():
                with pe.Fori(0, B) as b:
                    def counted(p):
                        return b * CHUNKS + p * 2

                    def turn(p, u):
                        n = counted(p)
                        if u == 0 and isinstance(p, int) and p == 0:
                            pe.wait_ge(first_in, b * 16 + 16)
                        else:
                            pe.wait_ge(ctx_in, b * ((CHUNKS - 1) * 16) + (p * 32 + u * 16))
                        pe.wait_ge(v_kept, n * VU + (u * VU + ONE))
                        for k in range(KT):
                            for t in range(TPC):
                                mm = pe.transpose(bank[k][:, t * P:(t + 1) * P], ctx_sb[:, t, k * P:(k + 1) * P], ident[:])
                        mm.then_inc(ctx_turned, 1)

                    def make_keys(p, u, g):
                        n = counted(p)
                        pe.wait_ge(ctxT_kept, n + (u + 1))
                        pe.wait_ge(k_kept, n * G + (u * G + g - 1 + ONE))
                        for k in range(KT):
                            mm = pe.matmul(bank[2 + g % 2][:], wk[:, k, g * P:(g + 1) * P], ctxT[:, k, :],
                                           start=k == 0, stop=k == KT - 1)
                        mm.then_inc(k_made, 1)

                    def make_values(p, u, v):
                        n = counted(p)
                        if v >= 2:
                            pe.wait_ge(v_kept, n * VU + (u * VU + v - 1 + ONE))
                        for t in range(TPV):
                            for k in range(KT):
                                at = (v * TPV + t) * P
                                mm = pe.matmul(bank[v % 2][:, t * HD:(t + 1) * HD], ctxT[:, k, at:at + P], wv[:, k, :],
                                               start=k == 0, stop=k == KT - 1)
                        mm.then_inc(v_made, 1)

                    def score(p, u, i):
                        n = counted(p)
                        h, q = i // QT, slice(i % QT * P, i % QT * P + P)
                        if i % (UM // 2) == 0:
                            half = i // (UM // 2)
                            pe.wait_ge(keys_in[u][half], (b * PAIRS + p) * (ND * 16) + (ND * 16 + ONE * u))
                            pe.wait_ge(k_kept, n * G + (u * G + (half + 1) * G // 2 + ONE))
                        pe.wait_ge(reduced, n * UM + (u * UM + i - 3 + M0))
                        if small:
                            mm = pe.matmul(quad[i % 4], query[0:KQ, h, q],
                                           keys[0:KQ, bass.ds(p, 1), u * UNITS + h, :].rearrange("k p n -> k (p n)"),
                                           start=True, stop=True)
                        else:
                            for x, (tile, slab) in enumerate(((0, 0), (1, 0), (2, 1))):
                                mm = pe.matmul(quad[i % 4], query[:, tile * H + h, q],
                                               keys[:, bass.ds(p, 1), u * UNITS + 2 * h + slab, :].rearrange("k p n -> k (p n)"),
                                               start=x == 0, stop=x == 2)
                        mm.then_inc(scored, 1)

                    GAP = 2 if small else 1
                    EARLY = 3

                    def make(p, u, first, last):
                        for x in range(first, min(last, len(STEPS))):
                            g = STEPS[:x].count(STEPS[x])
                            if STEPS[x] == "t":
                                turn(p, u)
                            elif STEPS[x] == "k":
                                make_keys(p, u, g)
                            else:
                                make_values(p, u, g)

                    def score_chunk(p, u, after, later):
                        for i in range(UM):
                            score(p, u, i)
                            if after is not None and i % GAP == 0 and i < 10 * GAP:
                                x = EARLY + i // GAP
                                make(*after, x, x + 1)
                            if later is not None and i >= 10 * GAP and i % (2 * GAP) == 0:
                                x = i // (2 * GAP) - 5
                                make(*later, x, min(x + 1, EARLY))

                    make(0, 0, 0, len(STEPS))
                    make(0, 1, 0, EARLY)
                    pe.wait_ge(q_in, b * (NDQ * 16) + NDQ * 16)
                    settle(pe, "pe")
                    with pe.Fori(0, PAIRS - 1) as p:
                        score_chunk(p, 0, (p, 1), (p + 1, 0))
                        score_chunk(p, 1, (p + 1, 0), (p + 1, 1))
                    score_chunk(PAIRS - 1, 0, (PAIRS - 1, 1), None)
                    score_chunk(PAIRS - 1, 1, None, None)

                    pe.wait_ge(negated, b + 1)
                    pe.transpose(quad[0][0:UM, 0:P], neg[:], ident[:]).then_inc(max_turned, 1)
                    pe.wait_ge(max_in, b * 48 + 48)
                    pe.wait_ge(out_reset, b + 1)
                    settle(pe, "pe")

                    with pe.Fori(0, PAIRS) as p:
                        m = (b * CHUNKS + p * 2) * SETS

                        def score_set(i):
                            u, at = i // SETS, i % SETS
                            pe.wait_ge(biased if masked else probs, m + (i - 1 + S0))
                            for x in range(4):
                                t, h = (at // 4, at % 4 * 4 + x) if small else (at % 2 * 2 + x // 2, at // 2 * 2 + x % 2)
                                out = duo[i % 2][:, x * S:(x + 1) * S]
                                if small:
                                    mm = pe.matmul(out, keys[0:KQ + 3, bass.ds(p, 1), u * UNITS + h, t * P:(t + 1) * P]
                                                   .rearrange("k p n -> k (p n)"), query[0:KQ + 3, h, :], start=True, stop=True)
                                else:
                                    for y, (tile, slab) in enumerate(((0, 0), (1, 0), (2, 1))):
                                        pe.matmul(out, keys[:, bass.ds(p, 1), u * UNITS + 2 * h + slab, t * P:(t + 1) * P]
                                                  .rearrange("k p n -> k (p n)"), query[:, tile * H + h, :], start=y == 0, stop=False)
                                    mm = pe.matmul(out, onesb[:], shift[:, h, :], start=False, stop=True)
                            mm.then_inc(set_scored, 1)

                        def use_set(i):
                            u, at = i // SETS, i % SETS
                            if at == 0:
                                pe.wait_ge(v_in[u], (b * PAIRS + p) * 16 + 16)
                            pe.wait_ge(probs, m + (i + 1 + PS0))
                            for x in range(4):
                                if small:
                                    t, h, group, row = at // 4, at % 4 * 4 + x, at % 4, x * 32
                                else:
                                    t, h, group, row = at % 2 * 2 + x // 2, at // 2 * 2 + x % 2, at // 2, x % 2 * 64
                                mm = pe.matmul(bank[group // 2][row:row + VW, group % 2 * S:group % 2 * S + S],
                                               value[u][:, t, h * VW:(h + 1) * VW], slot[i % 4][:, x * S:(x + 1) * S],
                                               start=False, stop=True, skip_group_check=True)
                            mm.then_inc(used, 1)

                        for i in range(2 * SETS):
                            score_set(i)
                            if i >= 2:
                                use_set(i - 2)
                        use_set(2 * SETS - 2)
                        use_set(2 * SETS - 1)

                    if not small:
                        pe.wait_ge(summed, b * (CHUNKS * SETS * TS) + (CHUNKS * SETS * TS + S0))
                        for h in range(H):
                            row, group = h % 2 * 64, h // 2
                            mm = pe.matmul(bank[2 + group // 2][row:row + 64, group % 2 * S:group % 2 * S + S],
                                           ones[:, 0:64], acc[:, h, :], start=True, stop=True, skip_group_check=True)
                        mm.then_inc(sums_made, 1)
                    pe.wait_ge(o_kept, b + 1 + ONE)

            choose(pe, run)


def project_heads(c, H, o_rows, sum_rows, b_v, w_o, b_o, x_from, x, ones, tag):
    nc = c.nc
    small = H == 16
    o_in, w_in, x_in = c.sem(tag + "o_in"), c.sem(tag + "w_in"), c.sem(tag + "x_in")
    cleared, chosen, spread = c.sem(tag + "cleared"), c.sem(tag + "chosen"), c.sem(tag + "spread")
    inverted, normed, projected, added = (c.sem(tag + n) for n in ("inverted", "normed", "projected", "added"))
    W = 4 * S
    with ExitStack() as s:
        def sb(n, shape, dt=F32):
            return s.enter_context(nc.sbuf_tensor(tag + n, shape, dt))

        o = sb("o", [P, B, W])
        inv = sb("inv", [P, B, W])
        on = sb("on", [P, B, W])
        wo = sb("wo", [P, 4, D])
        bo = sb("bo", [1, D])
        bv = sb("bv", [P, 4])
        if small:
            pick = sb("pick", [P, P])
        else:
            sums = sb("sums", [P, B, W])
        ps = [s.enter_context(nc.psum_tensor(f"{tag}ps{i}", [P, 512], F32)) for i in range(8)]
        block = s.enter_context(nc.Block())
        NW = 9 if small else 2

        @block.sync
        def _(sp):
            sp.dma_start(o[:], o_rows.ap().rearrange("b p n -> p b n")).then_inc(o_in, 16)
            if not small:
                sp.dma_start(sums[:], sum_rows.ap().rearrange("b p n -> p b n")).then_inc(o_in, 16)
            sp.dma_start(bo[:], b_o.rearrange("(a n) -> a n", a=1)).then_inc(w_in, 16)
            if small:
                sp.wait_ge(cleared, 2)
                for j in range(4):
                    sp.dma_start(wo[32 * j:32 * j + 16, :, :],
                                 w_o.rearrange("(g j d) n -> j d g n", j=4, d=16)[j]).then_inc(w_in, 16)
                    sp.dma_start(bv[32 * j:32 * j + 16, :],
                                 b_v.rearrange("(g j d) -> j d g", j=4, d=16)[j],
                                 allow_slow_non_contiguous=True).then_inc(w_in, 16)
            else:
                sp.dma_start(wo[:], w_o.rearrange("(g p) n -> p g n", p=P)).then_inc(w_in, 16)
            sp.dma_start(x[:], x_from.rearrange("(t p) d -> p t d", p=P)).then_inc(x_in, 16)

        @block.gpsimd
        def _(pool):
            if small:
                pool.memset(wo[:], 0.0).then_inc(cleared, 1)
                pool.memset(bv[:], 0.0).then_inc(cleared, 1)
                pool.memset(pick[:], 0.0).then_inc(cleared, 1)
                pool.wait_ge(cleared, 3)
                view = pick[:].rearrange("k (j d) -> k j d", j=4)
                pool.affine_select(out=view, in_=view, compare_op=ALU.not_equal, fill=1.0, base=-16,
                                   pattern=[[-32, 4], [0, 32]], channel_multiplier=1).then_inc(chosen, 1)

        @block.tensor
        def _(pe):
            if small:
                pe.wait_ge(o_in, 16)
                pe.wait_ge(chosen, 1)
                for i in range(2 * B):
                    pe.matmul(ps[i][:], pick[:], o[:, i // 2, i % 2 * 512:i % 2 * 512 + 512],
                              start=True, stop=True).then_inc(spread, 1)
            pe.wait_ge(w_in, 16 * NW)
            for t in range(NT):
                pe.wait_ge(normed, 2 * (t // QT) + 2)
                if small:
                    pe.wait_ge(inverted, 2 * t + 2)
                for g in range(4):
                    at = g * S + t % QT * P
                    pe.matmul(ps[t][:, 0:D], on[:, t // QT, at:at + P], wo[:, g, :], start=g == 0, stop=False)
                pe.matmul(ps[t][:, 0:D], ones[0:1, :], bo[:], start=False, stop=True).then_inc(projected, 1)

        @block.vector
        def _(dve):
            dve.wait_ge(o_in, 16 if small else 32)
            dve.wait_ge(w_in, 16 * NW)
            for i in range(2 * B):
                cols = slice(i % 2 * 512, i % 2 * 512 + 512)
                if small:
                    dve.wait_ge(spread, i + 1)
                    dve.reciprocal(inv[:, i // 2, cols], ps[i][:]).then_inc(inverted, 1)
                    dve.wait_ge(inverted, 2 * i + 1)
                    dve.tensor_tensor(inv[:, i // 2, cols], inv[:, i // 2, cols], o[:, i // 2, cols],
                                      ALU.mult).then_inc(inverted, 1)
                    dve.wait_ge(inverted, 2 * i + 2)
                    for g in range(i % 2 * 2, i % 2 * 2 + 2):
                        ins = dve.tensor_scalar(on[:, i // 2, g * S:(g + 1) * S], inv[:, i // 2, g * S:(g + 1) * S],
                                                bv[:, g:g + 1], None, ALU.add)
                    ins.then_inc(normed, 1)
                else:
                    dve.tensor_tensor(on[:, i // 2, cols], sums[:, i // 2, cols], o[:, i // 2, cols],
                                      ALU.mult).then_inc(normed, 1)
            dve.wait_ge(x_in, 16)
            for t in range(NT):
                dve.wait_ge(projected, t + 1)
                dve.tensor_tensor(x[:, t, :], ps[t][:, 0:D], x[:, t, :], ALU.add).then_inc(added, 1)


def short_attention(c, ctx, w_k, b_k, w_v, qs, k_rows, v_rows, o_rows, bias_qk, bias_kq, short, ident, tag):
    nc = c.nc
    H, dh = 16, 16
    HD = H * dh
    G = HD // P
    VW = dh + 1
    HV = H * VW
    VU = 2
    TPV = TPC // VU
    UM = H * QT
    SETS = H * TPC // 4
    SLOT_K, SLOT_Q = (0, 0, 1, 1, 0, 2), (0, 1, 0, 1, 2, 0)
    KQ = 6 * dh
    ND = 6
    STEPS, ACT_STEPS = "tkkvv", "kksvsv"
    EARLY, GAP = 3, 2
    ONE, M0, S0 = 16, 2 * UM, 2 * SETS

    def sem(n):
        return c.sem(tag + n)

    w_loaded, ones_set, ones_put, bias_in = sem("w_loaded"), sem("ones_set"), sem("ones_put"), sem("bias_in")
    ctx_in, q_in, max_in, o_out, biasT_in = (sem(n) for n in ("ctx_in", "q_in", "max_in", "o_out", "biasT_in"))
    v_out, v_in = ([sem(f"{n}{u}") for u in range(2)] for n in ("v_out", "v_in"))
    keys_in = [[sem(f"keys_in{u}{half}") for half in range(2)] for u in range(2)]
    ctx_turned, ctxT_kept, k_out = sem("ctx_turned"), sem("ctxT_kept"), sem("k_out")
    k_made, k_kept, k_rest, k_cut2, k_cut3 = (sem(n) for n in ("k_made", "k_kept", "k_rest", "k_cut2", "k_cut3"))
    v_made, v_kept, scored, reduced, folded = (sem(n) for n in ("v_made", "v_kept", "scored", "reduced", "folded"))
    max_turned, max_cut, out_reset, set_scored = (sem(n) for n in ("max_turned", "max_cut", "out_reset", "set_scored"))
    biased, probs, used, o_kept = (sem(n) for n in ("biased", "probs", "used", "o_kept"))
    settled = {n: sem("settled_" + n) for n in ("sp", "dve")}

    def settle(eng, n):
        eng.sem_inc(settled[n], 1)

    def where_short(eng, run):
        last_only = eng.value_load(short[0:1, 0:1], min_val=0, max_val=1)
        with eng.If(last_only == 1):
            run()

    with ExitStack() as s:
        def sb(n, shape, dt=F32):
            return s.enter_context(nc.sbuf_tensor(tag + n, shape, dt))

        keys = sb("keys", [P, B, 2 * UNITS, CH], BF16)
        query = sb("query", [P, B, H, S], BF16)
        room = sb("room", [P, 2 * TPC * HV])
        ctx_sb = room[:, 0:TPC * D].rearrange("p (t c) -> p t c", t=TPC)
        ctxT = room[:, TPC * D:2 * TPC * D].rearrange("p (k n) -> p k n", k=KT)
        value = [room[:, u * TPC * HV:(u + 1) * TPC * HV].rearrange("p (t c) -> p t c", t=TPC) for u in range(2)]
        work = sb("work", [P, 4096])
        kf = [work[:, g * CH:(g + 1) * CH] for g in range(2)]
        rest = [work[:, (2 + g) * CH:(3 + g) * CH] for g in range(2)]
        kparts = work[:, 2048:4096].bitcast(BF16)[:, 0:3 * G * CH].rearrange("p (i g n) -> p i g n", i=3, g=G)
        slot = [work[:, i * 1024:(i + 1) * 1024] for i in range(4)]
        stage = sb("stage", [P, 2 * TPV * HV])
        v_stage = [stage[:, u * TPV * HV:(u + 1) * TPV * HV].rearrange("p (t h w) -> p t h w", t=TPV, h=H) for u in range(2)]
        out_sb = stage[:, 0:1024]
        bias_sb = sb("bias_sb", [P, 2, 2 * CH])
        bias = [bias_sb[:, u, :].rearrange("p (i k) -> p i k", i=QT) for u in range(2)]
        biasT = [bias_sb[:, u, :].rearrange("p (t q) -> p t q", t=TPC) for u in range(2)]
        wk, wv, bk = sb("wk", [P, KT, HD]), sb("wv", [P, KT, HD]), sb("bk", [P, G])
        junk = [sb(f"junk{u}", [P, CH], BF16) for u in range(2)]
        best = sb("best", [P, 2, UM])
        neg = sb("neg", [P, B, UM])
        neg_rest, neg_parts = sb("neg_rest", [P, P]), sb("neg_parts", [P, 3, P], BF16)
        bank = [s.enter_context(nc.psum_tensor(f"{tag}bank{i}", [P, 512], F32)) for i in range(4)]
        duo = [s.enter_context(nc.psum_tensor(f"{tag}duo{i}", [P, 1024], F32)) for i in range(2)]
        quad = [duo[i // 2][:, i % 2 * 512:i % 2 * 512 + 512] for i in range(4)]
        block = s.enter_context(nc.Block())

        @block.sync
        def _(sp):
            def store_chunk(b, u):
                n = b * 2 + u

                def store_keys(half):
                    sp.wait_ge(k_cut2, n * G + half + 1)
                    sp.wait_ge(k_cut3, n * G + half + 1)
                    rows = k_rows.ap()[u, :, half * P:(half + 1) * P, :]
                    sp.dma_start(rows.rearrange("i k n -> k i n"), kparts[:, :, half]).then_inc(k_out, 16)
                    sp.wait_ge(k_out, n * 32 + (half * 16 + 16))
                    at = u * UNITS + half * 8
                    for i, part in enumerate(SLOT_K):
                        sp.dma_start(keys[i * dh:(i + 1) * dh, bass.ds(b, 1), at:at + 8, :].rearrange("d b h n -> d (b h) n"),
                                     rows[part].rearrange("(h d) n -> d h n", d=dh)).then_inc(keys_in[u][half], 16)

                store_keys(0)
                store_keys(1)
                for v in range(VU):
                    sp.wait_ge(v_kept, n * VU + (v + 1 + ONE))
                    rows = bass.ds(b * S2 + (LAST + u * CH + v * TPV * P), TPV * P)
                    sp.dma_start(v_rows.ap()[rows, :].rearrange("(t k) c -> k t c", k=P),
                                 v_stage[v % 2].rearrange("p t h w -> p t (h w)")).then_inc(v_out[v % 2], 16)

            def run():
                for half in range(2):
                    sp.sem_inc(keys_in[1][half], ONE)
                for v in range(2):
                    sp.sem_inc(v_out[v], ONE)
                sp.dma_start(ctx_sb, ctx[0, LAST:LAST + CH].rearrange("(t k) c -> k t c", k=P)).then_inc(ctx_in, 16)
                sp.dma_start(wk[:], w_k.rearrange("(k p) n -> p k n", p=P)).then_inc(w_loaded, 16)
                sp.dma_start(wv[:], w_v.rearrange("(k p) n -> p k n", p=P)).then_inc(w_loaded, 16)
                sp.dma_start(bk[:], b_k.rearrange("(g p) -> p g", p=P), allow_slow_non_contiguous=True).then_inc(w_loaded, 16)
                for u in range(2):
                    sp.dma_start(bias[u], bias_qk.ap()[:, LAST + u * CH:LAST + (u + 1) * CH]
                                 .rearrange("(i q) k -> q i k", q=P)).then_inc(bias_in, 16)
                for b in range(B):
                    for i, part in enumerate(SLOT_Q):
                        sp.dma_start(query[i * dh:(i + 1) * dh, b, :, :],
                                     qs.ap()[part, :, b * S:(b + 1) * S].rearrange("(h d) q -> d h q", d=dh)).then_inc(q_in, 16)
                store_chunk(0, 0)
                store_chunk(0, 1)
                sp.wait_ge(ones_set, 3)
                for b in range(B):
                    for at in range(0, 2 * UNITS, 8):
                        if b or at:
                            sp.dma_start(keys[KQ:KQ + 3, b, at:at + 8, :], keys[KQ:KQ + 3, 0, 0:8, :]).then_inc(ones_put, 16)
                with sp.Fori(1, B) as b:
                    for u in range(2):
                        store_chunk(b, u)
                sp.wait_ge(max_cut, 4)
                for i in range(3):
                    sp.dma_start(query[KQ + i:KQ + i + 1].rearrange("o b h (i q) -> o (b h i) q", i=QT),
                                 neg_parts[:, i, :]).then_inc(max_in, 16)
                for u in range(2):
                    sp.dma_start(biasT[u], bias_kq.ap()[LAST + u * CH:LAST + (u + 1) * CH, :]
                                 .rearrange("(t k) q -> k t q", k=P)).then_inc(biasT_in, 16)
                for v in range(2):
                    sp.wait_ge(v_out[v], 2 * B * 16 + ONE)
                with sp.Fori(0, B) as b:
                    for u in range(2):
                        sp.wait_ge(used, b * (2 * SETS) + (u * SETS - SETS + S0))
                        rows = bass.ds(b * S2 + (LAST + u * CH), CH)
                        sp.dma_start(value[u], v_rows.ap()[rows, :].rearrange("(t k) c -> k t c", k=P)).then_inc(v_in[u], 16)
                    sp.wait_ge(o_kept, b + 1 + ONE)
                    sp.dma_start(o_rows.ap()[bass.ds(b, 1)].rearrange("b p n -> (b p) n"), out_sb).then_inc(o_out, 16)
                sp.wait_ge(o_out, B * 16 + ONE)

            where_short(sp, run)

        @block.gpsimd
        def _(pool):
            def run():
                for u in range(2):
                    pool.memset(v_stage[u], 1.0).then_inc(ones_set, 1)
                    pool.wait_ge(ones_set, u + 1)
                pool.memset(keys[KQ:P, 0, 0:8, :], 1.0).then_inc(ones_set, 1)
                pool.wait_ge(ones_set, 3)
                with pool.Fori(0, B) as b:
                    for u in range(2):
                        m = b * (2 * G) + u * G
                        for g in range(G):
                            pool.wait_ge(k_kept, m + (g + 1 + ONE))
                            pool.tensor_tensor(rest[g], kf[g], kparts[:, 0, g], ALU.subtract).then_inc(k_rest, 1)
                        for g in range(G):
                            pool.wait_ge(k_cut2, m + (g + 1))
                            pool.tensor_tensor(kparts[:, 2, g], rest[g], kparts[:, 1, g], ALU.subtract).then_inc(k_cut3, 1)

            where_short(pool, run)

        @block.scalar
        def _(act):
            def make_chunk(b, u, following):
                n = b * 2 + u
                act.wait_ge(ctx_turned, n + 1)
                if following is not None:
                    fb, fu = following
                    act.dma_start(ctx_sb, ctx[bass.ds(fb, 1), LAST + fu * CH:LAST + (fu + 1) * CH, :]
                                  .rearrange("b (t k) c -> k (b t) c", k=P)).then_inc(ctx_in, 16)
                for k in range(KT):
                    ins = act.activation(ctxT[:, k, :], bank[k][:], ACT.Copy)
                ins.then_inc(ctxT_kept, 1)
                for x, step in enumerate(ACT_STEPS):
                    g = ACT_STEPS[:x].count(step)
                    if step == "k":
                        act.wait_ge(k_made, n * G + g + 1)
                        act.wait_ge(k_rest, n * G + (g - 1 + ONE))
                        act.wait_ge(keys_in[1 - u][g], b * (ND * 16) + (ND * 16 if u == 1 else ONE))
                        act.activation(kf[g], bank[2 + g][:], ACT.Identity, bias=bk[:, g:g + 1])
                        act.activation(kparts[:, 0, g], bank[2 + g][:], ACT.Identity, bias=bk[:, g:g + 1]).then_inc(k_kept, 1)
                    elif step == "s":
                        act.wait_ge(k_rest, n * G + (g + 1 + ONE))
                        act.activation(kparts[:, 1, g], rest[g], ACT.Copy).then_inc(k_cut2, 1)
                    else:
                        act.wait_ge(v_made, n * VU + g + 1)
                        act.wait_ge(v_out[g], n * 16 + ONE)
                        act.activation(v_stage[g][:, :, :, 0:dh], bank[g][:].rearrange("p (t h w) -> p t h w", t=TPV, h=H),
                                       ACT.Copy).then_inc(v_kept, 1)

            def run():
                act.sem_inc(k_kept, ONE)
                act.sem_inc(v_kept, ONE)
                act.sem_inc(k_rest, ONE)
                act.sem_inc(o_out, ONE)
                act.sem_inc(o_kept, ONE)
                act.wait_ge(w_loaded, 48)
                act.wait_ge(ones_set, 2)
                with act.Fori(0, B - 1) as b:
                    make_chunk(b, 0, (b, 1))
                    make_chunk(b, 1, (b + 1, 0))
                make_chunk(B - 1, 0, (B - 1, 1))
                make_chunk(B - 1, 1, None)
                with act.Fori(0, B) as b:
                    for i in range(2 * SETS):
                        act.wait_ge(biased, b * (2 * SETS) + (i + 1 + S0))
                        act.activation(slot[i % 4], slot[i % 4], ACT.Exp).then_inc(probs, 1)
                    act.wait_ge(used, b * (2 * SETS) + (2 * SETS + S0))
                    act.wait_ge(o_out, b * 16 + ONE)
                    act.activation(out_sb[:, 0:512], bank[0][:], ACT.Copy)
                    act.activation(out_sb[:, 512:1024], bank[1][:], ACT.Copy).then_inc(o_kept, 1)

            where_short(act, run)

        @block.vector
        def _(dve):
            def run():
                dve.sem_inc(reduced, M0)
                dve.sem_inc(biased, S0)
                dve.wait_ge(bias_in, 32)
                with dve.Fori(0, B) as b:
                    for u in range(2):
                        n = b * (2 * UM) + u * UM
                        for i in range(UM):
                            dve.wait_ge(scored, n + (i + 1))
                            dve.wait_ge(reduced, n + (i - 1 + M0))
                            settle(dve, "dve")
                            dve.tensor_tensor_reduce(junk[i % 2][:], quad[i % 4], bias[u][:, i % QT, :], 1.0, LOWEST,
                                                     ALU.add, ALU.max, best[:, u, i:i + 1]).then_inc(reduced, 1)
                    dve.wait_ge(reduced, b * (2 * UM) + (2 * UM + M0))
                    mine = neg[:, bass.ds(b, 1), :].rearrange("p b i -> p (b i)")
                    dve.tensor_tensor(mine, best[:, 0, :], best[:, 1, :], ALU.max).then_inc(folded, 1)
                    dve.wait_ge(folded, b + 1)
                dve.tensor_scalar(neg[:], neg[:], -1.0, None, ALU.mult).then_inc(folded, 1)
                dve.wait_ge(max_turned, 1)
                dve.tensor_copy(neg_parts[:, 0, :], quad[0][:, 0:P]).then_inc(max_cut, 1)
                dve.wait_ge(max_cut, 1)
                dve.tensor_tensor(neg_rest[:], quad[0][:, 0:P], neg_parts[:, 0, :], ALU.subtract).then_inc(max_cut, 1)
                dve.wait_ge(max_cut, 2)
                dve.tensor_copy(neg_parts[:, 1, :], neg_rest[:]).then_inc(max_cut, 1)
                dve.wait_ge(max_cut, 3)
                dve.tensor_tensor(neg_parts[:, 2, :], neg_rest[:], neg_parts[:, 1, :], ALU.subtract).then_inc(max_cut, 1)
                dve.wait_ge(biasT_in, 32)
                dve.wait_ge(v_kept, 2 * B * VU + ONE)
                with dve.Fori(0, B) as b:
                    for i in range(2 * SETS):
                        u, at = i // SETS, i % SETS
                        dve.wait_ge(set_scored, b * (2 * SETS) + (i + 1))
                        dve.wait_ge(used, b * (2 * SETS) + (i - 3 + S0))
                        dve.tensor_tensor(slot[i % 4].rearrange("p (h q) -> p h q", h=4),
                                          duo[i % 2][:].rearrange("p (h q) -> p h q", h=4),
                                          biasT[u][:, at // 4:at // 4 + 1, :].broadcast_to([P, 4, S]),
                                          ALU.add).then_inc(biased, 1)
                        if i == 1:
                            dve.wait_ge(o_kept, b + ONE)
                            settle(dve, "dve")
                            dve.memset(bank[0][:], 0.0)
                            dve.memset(bank[1][:], 0.0).then_inc(out_reset, 1)

            where_short(dve, run)

        @block.tensor
        def _(pe):
            def turn(b, u):
                n = b * 2 + u
                pe.wait_ge(ctx_in, n * 16 + 16)
                pe.wait_ge(v_kept, n * VU + ONE)
                for k in range(KT):
                    for t in range(TPC):
                        mm = pe.transpose(bank[k][:, t * P:(t + 1) * P], ctx_sb[:, t, k * P:(k + 1) * P], ident[:])
                mm.then_inc(ctx_turned, 1)

            def make_keys(b, u, g):
                n = b * 2 + u
                pe.wait_ge(ctxT_kept, n + 1)
                pe.wait_ge(k_kept, n * G + (g - 1 + ONE))
                for k in range(KT):
                    mm = pe.matmul(bank[2 + g][:], wk[:, k, g * P:(g + 1) * P], ctxT[:, k, :], start=k == 0, stop=k == KT - 1)
                mm.then_inc(k_made, 1)

            def make_values(b, u, v):
                for t in range(TPV):
                    for k in range(KT):
                        at = (v * TPV + t) * P
                        mm = pe.matmul(bank[v][:, t * HD:(t + 1) * HD], ctxT[:, k, at:at + P], wv[:, k, :],
                                       start=k == 0, stop=k == KT - 1)
                mm.then_inc(v_made, 1)

            def make(b, u, first, last):
                for x in range(first, min(last, len(STEPS))):
                    if STEPS[x] == "t":
                        turn(b, u)
                    elif STEPS[x] == "k":
                        make_keys(b, u, STEPS[:x].count("k"))
                    else:
                        make_values(b, u, STEPS[:x].count("v"))

            def score_chunk(b, u, after, later):
                n = b * 2 + u
                for i in range(UM):
                    h, q = i // QT, slice(i % QT * P, i % QT * P + P)
                    if i % (UM // 2) == 0:
                        pe.wait_ge(keys_in[u][i // (UM // 2)], b * (ND * 16) + (ND * 16 + ONE * u))
                    pe.wait_ge(reduced, n * UM + (i - 3 + M0))
                    pe.matmul(quad[i % 4], query[0:KQ, bass.ds(b, 1), h, q].rearrange("k b q -> k (b q)"),
                              keys[0:KQ, bass.ds(b, 1), u * UNITS + h, :].rearrange("k b n -> k (b n)"),
                              start=True, stop=True).then_inc(scored, 1)
                    if after is not None and i % GAP == 0 and i < 10 * GAP:
                        x = EARLY + i // GAP
                        make(*after, x, x + 1)
                    if later is not None and i >= 10 * GAP and i % (2 * GAP) == 0:
                        x = i // (2 * GAP) - 5
                        make(*later, x, min(x + 1, EARLY))

            def score_set(b, i):
                u, t, first = i // SETS, i % SETS // 4, i % 4 * 4
                pe.wait_ge(biased, b * (2 * SETS) + (i - 1 + S0))
                for x in range(4):
                    mm = pe.matmul(duo[i % 2][:, x * S:(x + 1) * S],
                                   keys[0:KQ + 3, bass.ds(b, 1), u * UNITS + first + x, t * P:(t + 1) * P]
                                   .rearrange("k b n -> k (b n)"),
                                   query[0:KQ + 3, bass.ds(b, 1), first + x, :].rearrange("k b q -> k (b q)"),
                                   start=True, stop=True)
                mm.then_inc(set_scored, 1)

            def use_set(b, i):
                u, t, group = i // SETS, i % SETS // 4, i % 4
                if i % SETS == 0:
                    pe.wait_ge(v_in[u], b * 16 + 16)
                if i == 0:
                    pe.wait_ge(out_reset, b + 1)
                pe.wait_ge(probs, b * (2 * SETS) + (i + 1))
                for x in range(4):
                    h = group * 4 + x
                    mm = pe.matmul(bank[group // 2][x * 32:x * 32 + VW, group % 2 * S:group % 2 * S + S],
                                   value[u][:, t, h * VW:(h + 1) * VW], slot[i % 4][:, x * S:(x + 1) * S],
                                   start=False, stop=True, skip_group_check=True)
                mm.then_inc(used, 1)

            def run():
                pe.sem_inc(used, S0)
                pe.wait_ge(w_loaded, 48)
                make(0, 0, 0, len(STEPS))
                make(0, 1, 0, EARLY)
                pe.wait_ge(q_in, B * ND * 16)
                with pe.Fori(0, B - 1) as b:
                    score_chunk(b, 0, (b, 1), (b + 1, 0))
                    score_chunk(b, 1, (b + 1, 0), (b + 1, 1))
                score_chunk(B - 1, 0, (B - 1, 1), None)
                score_chunk(B - 1, 1, None, None)
                pe.wait_ge(folded, B + 1)
                pe.transpose(quad[0][:, 0:P], neg[:].rearrange("p b i -> p (b i)"), ident[:]).then_inc(max_turned, 1)
                pe.wait_ge(ones_put, (B * 4 - 1) * 16)
                pe.wait_ge(max_in, 48)
                with pe.Fori(0, B) as b:
                    for i in range(2 * SETS):
                        score_set(b, i)
                        if i >= 2:
                            use_set(b, i - 2)
                    use_set(b, 2 * SETS - 2)
                    use_set(b, 2 * SETS - 1)

            where_short(pe, run)


def channel_attention(c, xnT, w_qk, w_v, w_o, tau, x, ident, ones, tag):
    nc = c.nc
    DH = 16
    w_in, picks, tau_col = c.sem(tag + "w_in"), c.sem(tag + "picks"), c.sem(tag + "tau_col")
    qk_made, qk_kept, v_made, v_kept = (c.sem(tag + n) for n in ("qk_made", "qk_kept", "v_made", "v_kept"))
    gram_made, step, norms, exped, mixed, mix_kept = (c.sem(tag + n) for n in
                                                     ("gram_made", "step", "norms", "exped", "mixed", "mix_kept"))
    projected, added = c.sem(tag + "projected"), c.sem(tag + "added")
    GB = B * KT
    with ExitStack() as s:
        def sb(n, shape, dt=F32):
            return s.enter_context(nc.sbuf_tensor(tag + n, shape, dt))

        wqk, wv, wo = sb("wqk", [P, KT, D]), sb("wv", [P, KT, D]), sb("wo", [P, KT, D])
        tau_sb = sb("tau_sb", [16, 1])
        pick = sb("pick", [16, D])
        tau_c = sb("tau_c", [P, KT])
        same = sb("same", [P, P])
        off = sb("off", [P, P])
        qk = sb("qk", [P, NT, D])
        vT = sb("vT", [P, KT, N])
        gram, diag, logit = sb("gram", [P, GB, P]), sb("diag", [P, GB, P]), sb("logit", [P, GB, P])
        q2 = sb("q2", [P, GB])
        top, negtop, total, inv = (sb(n, [P, GB]) for n in ("top", "negtop", "total", "inv"))
        attn = sb("attn", [P, GB, P])
        mix = sb("mix", [P, GB, D])
        ps = [s.enter_context(nc.psum_tensor(f"{tag}ps{i}", [P, 512], F32)) for i in range(8)]
        block = s.enter_context(nc.Block())

        @block.sync
        def _(sp):
            for w, src in ((wqk, w_qk), (wv, w_v), (wo, w_o)):
                sp.dma_start(w[:], src.rearrange("(k p) n -> p k n", p=P)).then_inc(w_in, 16)
            sp.dma_start(tau_sb[:], tau.rearrange("h a b -> h (a b)")).then_inc(w_in, 16)

        @block.gpsimd
        def _(pool):
            pool.memset(pick[:], 1.0).then_inc(picks, 1)
            pool.wait_ge(picks, 1)
            pool.affine_select(out=pick[:], in_=pick[:], compare_op=ALU.is_ge, fill=0.0, base=0,
                               pattern=[[1, D]], channel_multiplier=-DH).then_inc(picks, 1)
            pool.wait_ge(picks, 2)
            pool.affine_select(out=pick[:], in_=pick[:], compare_op=ALU.is_ge, fill=0.0, base=DH - 1,
                               pattern=[[-1, D]], channel_multiplier=DH).then_inc(picks, 1)

        @block.tensor
        def _(pe):
            pe.wait_ge(w_in, 64)
            pe.wait_ge(picks, 3)
            for k in range(KT):
                pe.matmul(ps[7][:, k:k + 1], pick[:, k * P:(k + 1) * P], tau_sb[:], start=True, stop=True)
            pe.matmul(ps[7][:, P:2 * P], pick[:, 0:P], pick[:, 0:P], start=True, stop=True).then_inc(tau_col, 1)
            for t in range(NT):
                if t >= 4:
                    pe.wait_ge(qk_kept, t - 3)
                for k in range(KT):
                    mm = pe.matmul(ps[t % 4][:, 0:D], xnT[:, k, t * P:(t + 1) * P], wqk[:, k, :],
                                   start=k == 0, stop=k == KT - 1)
                mm.then_inc(qk_made, 1)
            for i in range(KT * 2):
                if i >= 2:
                    pe.wait_ge(v_kept, i - 1)
                for k in range(KT):
                    mm = pe.matmul(ps[4 + i % 2][:], wv[:, k, i // 2 * P:(i // 2 + 1) * P],
                                   xnT[:, k, i % 2 * 512:i % 2 * 512 + 512], start=k == 0, stop=k == KT - 1)
                mm.then_inc(v_made, 1)
            pe.wait_ge(qk_kept, NT)
            for i in range(GB):
                b, m = i // KT, i % KT
                for t in range(QT):
                    rows = qk[:, b * QT + t, m * P:(m + 1) * P]
                    mm = pe.matmul(ps[i // 4][:, i % 4 * P:(i % 4 + 1) * P], rows, rows, start=t == 0, stop=t == QT - 1)
                mm.then_inc(gram_made, 1)
            pe.wait_ge(step, 3)
            for i in range(2):
                mm = pe.matmul(ps[2 + i][:], ones[:], diag[:, 4 * i:4 * i + 4, :].rearrange("p i n -> p (i n)"),
                               start=True, stop=True)
            mm.then_inc(norms, 1)
            pe.wait_ge(v_kept, 2 * KT)
            for i in range(GB):
                if i >= 4:
                    pe.wait_ge(mix_kept, i - 3)
                pe.wait_ge(step, 13 + i)
                pe.matmul(ps[4 + i % 4][:, 0:D], attn[:, i, :], wo[:, i % KT, :], start=True, stop=True).then_inc(mixed, 1)
            pe.wait_ge(mix_kept, GB)
            for t in range(NT):
                if t >= 4:
                    pe.wait_ge(added, t - 3)
                for k in range(KT):
                    mm = pe.matmul(ps[t % 4][:, 0:D], vT[:, k, t * P:(t + 1) * P], mix[:, t // QT * KT + k, :],
                                   start=k == 0, stop=k == KT - 1)
                mm.then_inc(projected, 1)

        @block.scalar
        def _(act):
            for t in range(NT):
                act.wait_ge(qk_made, t + 1)
                act.activation(qk[:, t, :], ps[t % 4][:, 0:D], ACT.Copy).then_inc(qk_kept, 1)
            for i in range(KT * 2):
                act.wait_ge(v_made, i + 1)
                act.activation(vT[:, i // 2, i % 2 * 512:i % 2 * 512 + 512], ps[4 + i % 2][:], ACT.Copy).then_inc(v_kept, 1)
            act.wait_ge(step, 11)
            for i in range(GB):
                act.activation(attn[:, i, :], logit[:, i, :], ACT.Exp, bias=negtop[:, i:i + 1],
                               accum_out=total[:, i:i + 1]).then_inc(exped, 1)
            for i in range(GB):
                act.wait_ge(mixed, i + 1)
                act.activation(mix[:, i, :], ps[4 + i % 4][:, 0:D], ACT.Copy).then_inc(mix_kept, 1)

        @block.vector
        def _(dve):
            dve.wait_ge(tau_col, 1)
            dve.tensor_copy(tau_c[:], ps[7][:, 0:KT])
            dve.tensor_copy(same[:], ps[7][:, P:2 * P]).then_inc(step, 1)
            dve.wait_ge(step, 1)
            dve.tensor_scalar(off[:], same[:], -LOWEST, LOWEST, ALU.mult, ALU.add)
            dve.wait_ge(gram_made, GB)
            for i in range(2):
                ins = dve.tensor_copy(gram[:, 4 * i:4 * i + 4, :].rearrange("p i n -> p (i n)"), ps[i][:])
            ins.then_inc(step, 1)
            dve.wait_ge(step, 2)
            dve.tensor_tensor(diag[:], gram[:], ident[:].unsqueeze(1).broadcast_to([P, GB, P]), ALU.mult).then_inc(step, 1)
            dve.wait_ge(step, 3)
            dve.tensor_reduce(q2[:], diag[:], AX.X, ALU.add).then_inc(step, 1)
            dve.wait_ge(step, 4)
            for i in range(GB):
                ins = dve.tensor_scalar(logit[:, i, :], gram[:, i, :], 2.0, q2[:, i:i + 1], ALU.mult, ALU.subtract)
            ins.then_inc(step, 1)
            dve.wait_ge(step, 5)
            dve.wait_ge(norms, 1)
            for i in range(2):
                half = logit[:, 4 * i:4 * i + 4, :].rearrange("p i n -> p (i n)")
                ins = dve.tensor_tensor(half, half, ps[2 + i][:], ALU.subtract)
            ins.then_inc(step, 1)
            dve.wait_ge(step, 6)
            for m in range(KT):
                ins = dve.tensor_scalar(logit[:, m:GB:KT, :], logit[:, m:GB:KT, :], 1.0 / 16.0, tau_c[:, m:m + 1],
                                        ALU.mult, ALU.mult)
            ins.then_inc(step, 1)
            dve.wait_ge(step, 7)
            dve.tensor_tensor(logit[:], logit[:], same[:].unsqueeze(1).broadcast_to([P, GB, P]), ALU.mult).then_inc(step, 1)
            dve.wait_ge(step, 8)
            dve.tensor_tensor(logit[:], logit[:], off[:].unsqueeze(1).broadcast_to([P, GB, P]), ALU.add).then_inc(step, 1)
            dve.wait_ge(step, 9)
            dve.tensor_reduce(top[:], logit[:], AX.X, ALU.max).then_inc(step, 1)
            dve.wait_ge(step, 10)
            dve.tensor_scalar(negtop[:], top[:], -1.0, None, ALU.mult).then_inc(step, 1)
            dve.wait_ge(exped, GB)
            dve.reciprocal(inv[:], total[:]).then_inc(step, 1)
            dve.wait_ge(step, 12)
            for i in range(GB):
                dve.tensor_scalar(attn[:, i, :], attn[:, i, :], inv[:, i:i + 1], None, ALU.mult).then_inc(step, 1)
            for t in range(NT):
                dve.wait_ge(projected, t + 1)
                dve.tensor_tensor(x[:, t, :], ps[t % 4][:, 0:D], x[:, t, :], ALU.add).then_inc(added, 1)


E, CAP = 8, 320


def route(c, xnT, w_g, gates, seat_in, seat_out, inputs, onesb, tag):
    nc = c.nc
    blank, cleared = c.sem(tag + "blank"), c.sem(tag + "cleared")
    w_in, built, logits, step, exped, counted = (c.sem(tag + n) for n in
                                                 ("w_in", "built", "logits", "step", "exped", "counted"))
    with ExitStack() as s:
        def sb(n, shape, dt=F32):
            return s.enter_context(nc.sbuf_tensor(tag + n, shape, dt))

        wg = sb("wg", [P, KT, E])
        lg, pr = sb("lg", [P, NT, E]), sb("pr", [P, NT, E])
        top, total, inv = sb("top", [P, NT]), sb("total", [P, NT]), sb("inv", [P, NT])
        best8, at8, at8f = sb("best8", [P, NT, E]), sb("at8", [P, NT, E], U32), sb("at8f", [P, NT, E])
        iota = sb("iota", [P, E])
        one = sb("one", [P, 2, NT, E])
        oneb = sb("oneb", [P, 2 * NT, E], BF16)
        upto = sb("upto", [P, P], BF16)
        seat = sb("seat", [P, 2, NT, E])
        place = sb("place", [P, 2 * NT])
        kept = sb("kept", [P, 2, NT])
        den, rden, seatf, away = sb("den", [P, NT]), sb("rden", [P, NT]), sb("seatf", [P, 2, NT]), sb("away", [P, 2, NT])
        zero = sb("zero", [P, E * CAP * D // P])
        ps = [s.enter_context(nc.psum_tensor(f"{tag}ps{i}", [P, 512], F32)) for i in range(2)]
        block = s.enter_context(nc.Block())

        @block.sync
        def _(sp):
            sp.dma_start(wg[:], w_g.rearrange("(k p) n -> p k n", p=P)).then_inc(w_in, 16)
            sp.wait_ge(blank, 1)
            sp.dma_start(inputs.ap().rearrange("(p r) d -> p (r d)", p=P), zero[:]).then_inc(cleared, 16)
            sp.wait_ge(cleared, 16)

        @block.gpsimd
        def _(pool):
            pool.memset(upto[:], 1.0).then_inc(built, 1)
            pool.memset(onesb[:], 1.0).then_inc(built, 1)
            for e in range(E):
                pool.memset(iota[:, e:e + 1], float(e)).then_inc(built, 1)
            pool.wait_ge(built, 2 + E)
            pool.affine_select(out=upto[:], in_=upto[:], compare_op=ALU.is_ge, fill=0.0, base=0,
                               pattern=[[1, P]], channel_multiplier=-1).then_inc(built, 1)

        @block.tensor
        def _(pe):
            pe.wait_ge(w_in, 16)
            for t in range(NT):
                for k in range(KT):
                    mm = pe.matmul(ps[0][:, t * E:(t + 1) * E], xnT[:, k, t * P:(t + 1) * P], wg[:, k, :],
                                   start=k == 0, stop=k == KT - 1)
            mm.then_inc(logits, 1)
            pe.wait_ge(built, 3 + E)
            pe.wait_ge(step, 11)
            for j in range(2 * NT):
                for i in range(j):
                    pe.matmul(ps[1][:, j * E:(j + 1) * E], onesb[:], oneb[:, i, :], start=i == 0, stop=False)
                mm = pe.matmul(ps[1][:, j * E:(j + 1) * E], upto[:], oneb[:, j, :], start=j == 0, stop=True)
            mm.then_inc(counted, 1)

        @block.scalar
        def _(act):
            act.wait_ge(step, 3)
            act.activation(pr[:], lg[:], ACT.Exp).then_inc(exped, 1)

        @block.vector
        def _(dve):
            def wide(a, n=NT):
                return a.unsqueeze(2).broadcast_to([P, n, E])

            dve.memset(zero[:], 0.0).then_inc(blank, 1)
            dve.wait_ge(logits, 1)
            dve.tensor_copy(lg[:].rearrange("p t e -> p (t e)"), ps[0][:, 0:NT * E]).then_inc(step, 1)
            dve.wait_ge(step, 1)
            dve.tensor_reduce(top[:], lg[:], AX.X, ALU.max).then_inc(step, 1)
            dve.wait_ge(step, 2)
            dve.tensor_tensor(lg[:], lg[:], wide(top[:]), ALU.subtract).then_inc(step, 1)
            dve.wait_ge(exped, 1)
            dve.tensor_reduce(total[:], pr[:], AX.X, ALU.add).then_inc(step, 1)
            dve.wait_ge(step, 4)
            dve.reciprocal(inv[:], total[:]).then_inc(step, 1)
            dve.wait_ge(step, 5)
            dve.tensor_tensor(pr[:], pr[:], wide(inv[:]), ALU.mult).then_inc(step, 1)
            dve.wait_ge(step, 6)
            for t in range(NT):
                ins = dve.max(best8[:, t, :], pr[:, t, :])
            ins.then_inc(step, 1)
            dve.wait_ge(step, 7)
            for t in range(NT):
                ins = dve.max_index(at8[:, t, :], best8[:, t, :], pr[:, t, :])
            ins.then_inc(step, 1)
            dve.wait_ge(step, 8)
            dve.tensor_copy(at8f[:], at8[:]).then_inc(step, 1)
            dve.wait_ge(step, 9)
            dve.wait_ge(built, 2 + E)
            for j in range(2):
                ins = dve.tensor_tensor(one[:, j], wide(at8f[:, :, j]), iota[:].unsqueeze(1).broadcast_to([P, NT, E]),
                                        ALU.is_equal)
            ins.then_inc(step, 1)
            dve.wait_ge(step, 10)
            dve.tensor_copy(oneb[:].rearrange("p (j t) e -> p j t e", j=2), one[:]).then_inc(step, 1)
            dve.wait_ge(counted, 1)
            dve.tensor_tensor(seat[:].rearrange("p j t e -> p (j t e)"), one[:].rearrange("p j t e -> p (j t e)"),
                              ps[1][:, 0:2 * NT * E], ALU.mult).then_inc(step, 1)
            dve.wait_ge(step, 12)
            dve.tensor_reduce(place[:], seat[:].rearrange("p j t e -> p (j t) e"), AX.X, ALU.add).then_inc(step, 1)
            dve.wait_ge(step, 13)
            dve.tensor_scalar(kept[:].rearrange("p j t -> p (j t)"), place[:], float(CAP), None, ALU.is_le).then_inc(step, 1)
            dve.wait_ge(step, 14)
            for j in range(2):
                ins = dve.tensor_tensor(gates[:, j], best8[:, :, j], kept[:, j], ALU.mult)
                dve.scalar_tensor_tensor(seatf[:, j], at8f[:, :, j], float(CAP), place[:, j * NT:(j + 1) * NT],
                                         ALU.mult, ALU.add)
            dve.tensor_scalar(away[:], kept[:], -float(4 * E * CAP), float(4 * E * CAP), ALU.mult, ALU.add).then_inc(step, 1)
            dve.wait_ge(step, 15)
            dve.scalar_tensor_tensor(seatf[:], seatf[:], 1.0, kept[:], ALU.subtract, ALU.mult)
            dve.tensor_tensor(den[:], gates[:, 0], gates[:, 1], ALU.add).then_inc(step, 1)
            dve.wait_ge(step, 16)
            dve.tensor_copy(seat_out[:].rearrange("p (j t) -> p j t", j=2), seatf[:])
            dve.tensor_tensor(seat_in[:].rearrange("p (j t) -> p j t", j=2), seatf[:], away[:], ALU.add)
            dve.tensor_scalar(den[:], den[:], 1e-9, None, ALU.max).then_inc(step, 1)
            dve.wait_ge(step, 17)
            dve.reciprocal(rden[:], den[:]).then_inc(step, 1)
            dve.wait_ge(step, 18)
            dve.tensor_tensor(gates[:], gates[:], rden[:].unsqueeze(1).broadcast_to([P, 2, NT]), ALU.mult).then_inc(step, 1)
            dve.wait_ge(step, 19)


def experts(c, xn, gates, seat_in, seat_out, inputs, outputs, w_in_all, w_out_all, x, moved, ident, tag):
    nc = c.nc
    F = 512
    FT = F // P
    ONE = 16
    TILES = ((0, P), (P, P), (2 * P, CAP - 2 * P))
    TAIL = TILES[-1][1]
    scattered, gathered = moved
    hidden, gelued, gated, out_made, out_kept, added = (
        c.sem(tag + n) for n in ("hidden", "gelued", "gated", "out_made", "out_kept", "added"))
    turned, xT_kept, all_stored = c.sem(tag + "turned"), c.sem(tag + "xT_kept"), c.sem(tag + "all_stored")
    rows_in, win_in, wout_in, o_out = ([c.sem(f"{tag}{n}{u}") for u in range(2)] for n in
                                       ("rows_in", "win_in", "wout_in", "o_out"))
    with ExitStack() as s:
        def sb(n, shape, dt=F32):
            return s.enter_context(nc.sbuf_tensor(tag + n, shape, dt))

        win = [sb(f"win{u}", [P, KT, 2 * F]) for u in range(2)]
        wout = [sb(f"wout{u}", [P, FT, D]) for u in range(2)]
        rows = [sb(f"rows{u}", [P, len(TILES), D]) for u in range(2)]
        xT = [sb(f"xT{u}", [P, KT, CAP]) for u in range(2)]
        ga = [sb(f"ga{i}", [P, CAP]) for i in range(2)]
        hid = [sb(f"hid{u}", [P, FT, CAP]) for u in range(2)]
        out = [sb(f"out{u}", [P, len(TILES), D]) for u in range(2)]
        back = sb("back", [P, 2 * NT, D])
        ps = [s.enter_context(nc.psum_tensor(f"{tag}ps{i}", [P, 512], F32)) for i in range(8)]
        block = s.enter_context(nc.Block())

        def seats(dram, e, u):
            at = e * (2 * CAP) + u * CAP
            return (dram.ap()[bass.ds(at, 2 * P), :].rearrange("(t p) d -> p t d", p=P),
                    dram.ap()[bass.ds(at + 2 * P, TAIL), :])

        @block.sync
        def _(sp):
            def load_rows(e, u):
                whole, tail = seats(inputs, e, u)
                sp.dma_start(rows[u][:, 0:2, :], whole).then_inc(rows_in[u], 16)
                sp.dma_start(rows[u][0:TAIL, 2, :], tail).then_inc(rows_in[u], 16)

            def load_weights(e, u):
                sp.dma_start(win[u][:], w_in_all[bass.ds(e * 2 + u, 1)].rearrange("e (k p) n -> p (e k) n", p=P)).then_inc(win_in[u], 16)
                sp.dma_start(wout[u][:], w_out_all[bass.ds(e * 2 + u, 1)].rearrange("e (k p) n -> p (e k) n", p=P)).then_inc(wout_in[u], 16)

            def store(e, u):
                sp.wait_ge(out_kept, e * 2 + (u + 1 + ONE))
                whole, tail = seats(outputs, e, u)
                sp.dma_start(whole, out[u][:, 0:2, :]).then_inc(o_out[u], 16)
                sp.dma_start(tail, out[u][0:TAIL, 2, :]).then_inc(o_out[u], 16)

            for u in range(2):
                sp.sem_inc(o_out[u], ONE)
            for u in range(2):
                load_weights(0, u)
            sp.wait_ge(scattered, 2 * NT * 16)
            for u in range(2):
                load_rows(0, u)
            with sp.Fori(1, E // 2) as e:
                for u in range(2):
                    sp.wait_ge(out_made, e * 2 + (u - 1))
                    load_rows(e, u)
                    load_weights(e, u)
                    store(e - 1, u)
            for u in range(2):
                store(E // 2 - 1, u)
            for u in range(2):
                sp.wait_ge(o_out[u], E // 2 * 32 + ONE)
            sp.sem_inc(all_stored, 1)

        @block.gpsimd
        def _(pool):
            for i in range(2 * NT):
                pool.indirect_dma_start(out=inputs.ap(), out_offset=bass.IndirectOffsetOnAxis(ap=seat_in[:, i:i + 1], axis=0),
                                        in_=xn[:, i % NT, :], in_offset=None, bounds_check=E * CAP - 1,
                                        oob_is_err=False).then_inc(scattered, 16)
            pool.wait_ge(all_stored, 1)
            for half in range(2):
                for i in range(2 * NT):
                    if i % NT // (NT // 2) == half:
                        pool.indirect_dma_start(out=back[:, i, :], out_offset=None, in_=outputs.ap(),
                                                in_offset=bass.IndirectOffsetOnAxis(ap=seat_out[:, i:i + 1], axis=0)
                                                ).then_inc(gathered[half], 16)

        @block.tensor
        def _(pe):
            def turn(e, u):
                pe.wait_ge(rows_in[u], e * 32 + 32)
                pe.wait_ge(xT_kept, e * 2 + (u + ONE))
                for k in range(KT):
                    for t, (at, n) in enumerate(TILES):
                        mm = pe.transpose(ps[6 + k][:, at:at + n], rows[u][0:n, t, k * P:(k + 1) * P], ident[0:n, 0:n])
                mm.then_inc(turned, 1)

            def hidden_tile(e, u, f):
                pe.wait_ge(gated, e * (2 * FT) + (u * FT + f - 1 + ONE))
                for part in range(2):
                    at = part * F + f * P
                    for k in range(KT):
                        mm = pe.matmul(ps[2 * (f % 2) + part][:, 0:CAP], win[u][:, k, at:at + P], xT[u][:, k, :],
                                       start=k == 0, stop=k == KT - 1)
                mm.then_inc(hidden, 1)

            def outs(e, u):
                pe.wait_ge(wout_in[u], e * 16 + 16)
                pe.wait_ge(gated, e * (2 * FT) + (u * FT + FT + ONE))
                pe.wait_ge(out_kept, e * 2 + (u + ONE))
                for t, (at, n) in enumerate(TILES):
                    for f in range(FT):
                        mm = pe.matmul(ps[4 + t // 2][0:n, t % 2 * D:t % 2 * D + D], hid[u][:, f, at:at + n], wout[u][:, f, :],
                                       start=f == 0, stop=f == FT - 1)
                mm.then_inc(out_made, 1)

            def expert(e, u, before, following):
                pe.wait_ge(win_in[u], e * 16 + 16)
                pe.wait_ge(xT_kept, e * 2 + (u + 1 + ONE))
                for f in range(FT):
                    hidden_tile(e, u, f)
                    if f == 0 and before is not None:
                        outs(*before)
                    if f == 2 and following is not None:
                        turn(*following)

            last = E // 2 - 1
            turn(0, 0)
            expert(0, 0, None, (0, 1))
            expert(0, 1, (0, 0), (1, 0))
            with pe.Fori(1, last) as e:
                expert(e, 0, (e - 1, 1), (e, 1))
                expert(e, 1, (e, 0), (e + 1, 0))
            expert(last, 0, (last - 1, 1), (last, 1))
            expert(last, 1, (last, 0), None)
            outs(last, 1)

        @block.scalar
        def _(act):
            def keep_turned(e, u):
                act.wait_ge(turned, e * 2 + (u + 1))
                for k in range(KT):
                    ins = act.activation(xT[u][:, k, :], ps[6 + k][:, 0:CAP], ACT.Copy)
                ins.then_inc(xT_kept, 1)

            def expert(e, u, following):
                for f in range(FT):
                    act.wait_ge(hidden, e * (2 * FT) + (u * FT + f + 1))
                    act.wait_ge(gated, e * (2 * FT) + (u * FT + f - 1 + ONE))
                    act.activation(ga[f % 2][:], ps[2 * (f % 2)][:, 0:CAP], ACT.Gelu).then_inc(gelued, 1)
                    if f == 2 and following is not None:
                        keep_turned(*following)

            last = E // 2 - 1
            act.sem_inc(xT_kept, ONE)
            keep_turned(0, 0)
            with act.Fori(0, last) as e:
                expert(e, 0, (e, 1))
                expert(e, 1, (e + 1, 0))
            expert(last, 0, (last, 1))
            expert(last, 1, None)

        @block.vector
        def _(dve):
            def keep_outputs(e, u):
                dve.wait_ge(out_made, e * 2 + (u + 1))
                dve.wait_ge(o_out[u], e * 32 + ONE)
                dve.tensor_copy(out[u][:, 0:2, :].rearrange("p t d -> p (t d)"), ps[4][:])
                dve.tensor_copy(out[u][0:TAIL, 2, :], ps[5][0:TAIL, 0:D]).then_inc(out_kept, 1)

            def expert(e, u, before):
                for f in range(FT):
                    dve.wait_ge(gelued, e * (2 * FT) + (u * FT + f + 1))
                    dve.tensor_tensor(hid[u][:, f, :], ps[2 * (f % 2) + 1][:, 0:CAP], ga[f % 2][:], ALU.mult).then_inc(gated, 1)
                    if f == 0 and before is not None:
                        keep_outputs(*before)

            last = E // 2 - 1
            dve.sem_inc(gated, ONE)
            dve.sem_inc(out_kept, ONE)
            expert(0, 0, None)
            expert(0, 1, (0, 0))
            with dve.Fori(1, E // 2) as e:
                expert(e, 0, (e - 1, 1))
                expert(e, 1, (e, 0))
            keep_outputs(last, 1)
            for half in range(2):
                dve.wait_ge(gathered[half], NT * 16)
                for j in range(2):
                    for t in range(half * NT // 2, (half + 1) * NT // 2):
                        if j == 1:
                            dve.wait_ge(added, half * NT + t - half * NT // 2 + 1)
                        dve.scalar_tensor_tensor(x[:, t, :], back[:, j * NT + t, :], gates[:, j, t:t + 1], x[:, t, :],
                                                 ALU.mult, ALU.add).then_inc(added, 1)


def refine_root(dve, step, at, var, root, tmp):
    dve.reciprocal(tmp[:, 0], root).then_inc(step, 1)
    dve.wait_ge(step, at + 1)
    dve.tensor_tensor(tmp[:, 1], tmp[:, 0], tmp[:, 0], ALU.mult).then_inc(step, 1)
    dve.wait_ge(step, at + 2)
    dve.tensor_tensor(tmp[:, 2], tmp[:, 1], var, ALU.mult).then_inc(step, 1)
    dve.wait_ge(step, at + 3)
    dve.tensor_scalar(tmp[:, 1], tmp[:, 2], -0.5, 1.5, ALU.mult, ALU.add).then_inc(step, 1)
    dve.wait_ge(step, at + 4)
    dve.tensor_tensor(tmp[:, 3], tmp[:, 1], tmp[:, 0], ALU.mult).then_inc(step, 1)


def self_attention(c, xn, xnT, norm_w, w_q, w_k, w_v, w_o, gate, log_t, x, ident, ones, tag):
    nc = c.nc
    H, KV, DH = 4, 2, 64
    NQK = (H + KV) * DH
    w_in, step, rooted, spread, scaled = (c.sem(tag + n) for n in ("w_in", "step", "rooted", "spread", "scaled"))
    masks, qkv_made, qkv_kept, turned, kept = (c.sem(tag + n) for n in ("masks", "qkv_made", "qkv_kept", "turned", "kept"))
    scored, masked, maxed, exped, p_turned, p_kept = (c.sem(tag + n) for n in
                                                     ("scored", "masked", "maxed", "exped", "p_turned", "p_kept"))
    mixed, o_normed, o_turned, o_kept, projected, blended, added = (
        c.sem(tag + n) for n in ("mixed", "o_normed", "o_turned", "o_kept", "projected", "blended", "added"))
    with ExitStack() as s:
        def sb(n, shape, dt=F32):
            return s.enter_context(nc.sbuf_tensor(tag + n, shape, dt))

        w = sb("w", [P, KT, NQK + KV * DH])
        wo, nw = sb("wo", [P, KT, D]), sb("nw", [P, KT])
        two, two_c = sb("two", [1, 2]), sb("two_c", [P, 2])
        scale = sb("scale", [P, 1])
        cmask = sb("cmask", [P, QT, S])
        sq, ms, var, root, tmp = sb("sq", [P, NT, D]), sb("ms", [P, NT]), sb("var", [P, NT]), sb("root", [P, NT]), sb("tmp", [P, 4, NT])
        qkv = sb("qkv", [P, NT, NQK + KV * DH])
        qsq, qn = sb("qsq", [P, NT, NQK]), sb("qn", [P, NT, NQK])
        n2, n1, n0, ninv = (sb(n, [P, NT * 6]) for n in ("n2", "n1", "n0", "ninv"))
        qkT = sb("qkT", [P, 3, N])
        lg = [sb(f"lg{i}", [P, H, S]) for i in range(2)]
        pb = [sb(f"pb{i}", [P, H, S]) for i in range(2)]
        top, bias, total, inv = (sb(n, [P, NT, H]) for n in ("top", "bias", "total", "inv"))
        pT = [sb(f"pT{i}", [P, 2 * H, P]) for i in range(2)]
        o = [sb(f"o{i}", [P, D]) for i in range(2)]
        oT = [sb(f"oT{i}", [P, KT, P]) for i in range(2)]
        y = sb("y", [P, NT, D])
        duo = [s.enter_context(nc.psum_tensor(f"{tag}duo{i}", [P, 1024], F32)) for i in range(3)]
        mixp = s.enter_context(nc.psum_tensor(tag + "mixp", [P, 512], F32))
        outp = s.enter_context(nc.psum_tensor(tag + "outp", [P, 512], F32))
        block = s.enter_context(nc.Block())

        @block.sync
        def _(sp):
            for j in range(2):
                for kv in range(KV):
                    h = 2 * kv + j
                    sp.dma_start(w[:, :, (j * KV + kv) * DH:(j * KV + kv + 1) * DH],
                                 w_q.rearrange("(k p) n -> p k n", p=P)[:, :, h * DH:(h + 1) * DH]).then_inc(w_in, 16)
            sp.dma_start(w[:, :, H * DH:NQK], w_k.rearrange("(k p) n -> p k n", p=P)).then_inc(w_in, 16)
            sp.dma_start(w[:, :, NQK:], w_v.rearrange("(k p) n -> p k n", p=P)).then_inc(w_in, 16)
            sp.dma_start(wo[:], w_o.rearrange("(k p) n -> p k n", p=P)).then_inc(w_in, 16)
            sp.dma_start(nw[:], norm_w.rearrange("(k p) -> p k", p=P), allow_slow_non_contiguous=True).then_inc(w_in, 16)
            sp.dma_start(two[:, 0:1], gate).then_inc(w_in, 16)
            sp.dma_start(two[:, 1:2], log_t).then_inc(w_in, 16)

        @block.gpsimd
        def _(pool):
            pool.memset(cmask[:], 0.0).then_inc(masks, 1)
            pool.wait_ge(masks, 1)
            for i in range(QT):
                pool.affine_select(out=cmask[:, i, :], in_=cmask[:, i, :], compare_op=ALU.is_ge, fill=NEG, base=i * P,
                                   pattern=[[-1, S]], channel_multiplier=1).then_inc(masks, 1)

        @block.tensor
        def _(pe):
            pe.wait_ge(w_in, 160)
            pe.matmul(outp[:, 0:2], ones[0:1, :], two[:], start=True, stop=True).then_inc(spread, 1)
            pe.wait_ge(step, 2)
            for t in range(NT):
                if t >= 4:
                    pe.wait_ge(qkv_kept, t - 3)
                for k in range(KT):
                    mm = pe.matmul(duo[t % 4 // 2][:, t % 2 * 512:t % 2 * 512 + 512], xnT[:, k, t * P:(t + 1) * P], w[:, k, :],
                                   start=k == 0, stop=k == KT - 1)
                mm.then_inc(qkv_made, 1)
            for t in range(NT):
                pe.wait_ge(step, 18)
                if t >= 2:
                    pe.wait_ge(kept, t - 1)
                for i in range(3):
                    mm = pe.transpose(duo[2][:, t % 2 * 512 + i * P:t % 2 * 512 + (i + 1) * P],
                                      qn[:, t, i * P:(i + 1) * P], ident[:])
                mm.then_inc(turned, 1)
            pe.wait_ge(kept, NT)
            for i in range(NT + 2):
                if i < NT:
                    if i >= 2:
                        pe.wait_ge(masked, i - 1)
                    for kv in range(KV):
                        rows = slice(kv * DH, kv * DH + DH)
                        for j in range(2):
                            mm = pe.matmul(duo[i % 2][:, (2 * kv + j) * S:(2 * kv + j + 1) * S],
                                           qkT[rows, j, i * P:(i + 1) * P], qkT[rows, 2, i // QT * S:i // QT * S + S],
                                           start=True, stop=True)
                    mm.then_inc(scored, 1)
                if 1 <= i <= NT:
                    g = i - 1
                    pe.wait_ge(exped, H * (g + 1))
                    if g >= 1:
                        pe.wait_ge(p_kept, g)
                    for h in range(H):
                        for k in range(2):
                            mm = pe.transpose(duo[2][:, (2 * h + k) * P:(2 * h + k + 1) * P],
                                              pb[g % 2][:, h, k * P:(k + 1) * P], ident[:])
                    mm.then_inc(p_turned, 1)
                    pe.wait_ge(p_kept, g + 1)
                    if g >= 1:
                        pe.wait_ge(o_kept, g)
                    for h in range(H):
                        for k in range(2):
                            at = NQK + h // 2 * DH
                            mm = pe.matmul(mixp[:, h * DH:(h + 1) * DH], pT[g % 2][:, 2 * h + k, :],
                                           qkv[:, g // QT * QT + k, at:at + DH], start=k == 0, stop=k == 1)
                    mm.then_inc(mixed, 1)
                    pe.wait_ge(o_normed, g + 1)
                    for k in range(KT):
                        mm = pe.transpose(mixp[:, D + k * P:D + (k + 1) * P], o[g % 2][:, k * P:(k + 1) * P], ident[:])
                    mm.then_inc(o_turned, 1)
                if i >= 2:
                    g = i - 2
                    pe.wait_ge(o_kept, g + 1)
                    if g >= 1:
                        pe.wait_ge(blended, g)
                    for k in range(KT):
                        mm = pe.matmul(outp[:, 0:D], oT[g % 2][:, k, :], wo[:, k, :], start=k == 0, stop=k == KT - 1)
                    mm.then_inc(projected, 1)

        @block.scalar
        def _(act):
            act.wait_ge(step, 4)
            act.activation(root[:], var[:], ACT.Sqrt).then_inc(rooted, 1)
            act.wait_ge(step, 9)
            for t in range(NT):
                act.wait_ge(qkv_made, t + 1)
                act.activation(qkv[:, t, :], duo[t % 4 // 2][:, t % 2 * 512:t % 2 * 512 + 512], ACT.Copy,
                               scale=tmp[:, 3, t:t + 1]).then_inc(qkv_kept, 1)
            act.wait_ge(step, 11)
            act.activation(n1[:], n2[:], ACT.Sqrt).then_inc(rooted, 1)
            for t in range(NT):
                act.wait_ge(turned, t + 1)
                act.activation(qkT[:, :, t * P:(t + 1) * P],
                               duo[2][:, t % 2 * 512:t % 2 * 512 + 3 * P].rearrange("p (i n) -> p i n", i=3),
                               ACT.Copy).then_inc(kept, 1)
            act.wait_ge(step, 1)
            act.activation(scale[:], two_c[:, 1:2], ACT.Exp).then_inc(scaled, 1)
            for g in range(NT):
                act.wait_ge(maxed, g + 1)
                if g >= 2:
                    act.wait_ge(p_turned, g - 1)
                for h in range(H):
                    act.activation(pb[g % 2][:, h, :], lg[g % 2][:, h, :], ACT.Exp, bias=bias[:, g, h:h + 1],
                                   scale=scale[:], accum_out=total[:, g, h:h + 1]).then_inc(exped, 1)
                act.wait_ge(p_turned, g + 1)
                if g >= 2:
                    act.wait_ge(mixed, g - 1)
                act.activation(pT[g % 2][:].rearrange("p i n -> p (i n)"), duo[2][:], ACT.Copy).then_inc(p_kept, 1)
                act.wait_ge(o_turned, g + 1)
                if g >= 2:
                    act.wait_ge(projected, g - 1)
                act.activation(oT[g % 2][:], mixp[:, D:2 * D].rearrange("p (k n) -> p k n", k=KT), ACT.Copy).then_inc(o_kept, 1)

        @block.vector
        def _(dve):
            dve.wait_ge(spread, 1)
            dve.tensor_copy(two_c[:], outp[:, 0:2]).then_inc(step, 1)
            dve.wait_ge(w_in, 160)
            for k in range(KT):
                ins = dve.tensor_scalar(w[:, k, :], w[:, k, :], nw[:, k:k + 1], None, ALU.mult)
            ins.then_inc(step, 1)
            for t in range(NT):
                ins = dve.tensor_tensor_reduce(sq[:, t, :], xn[:, t, :], xn[:, t, :], 1.0 / D, 0.0, ALU.mult, ALU.add,
                                               ms[:, t:t + 1])
            ins.then_inc(step, 1)
            dve.wait_ge(step, 3)
            dve.tensor_scalar(var[:], ms[:], 1e-6, None, ALU.add).then_inc(step, 1)
            dve.wait_ge(rooted, 1)
            refine_root(dve, step, 4, var[:], root[:], tmp)
            dve.wait_ge(qkv_kept, NT)
            dve.tensor_tensor(qsq[:], qkv[:, :, 0:NQK], qkv[:, :, 0:NQK], ALU.mult).then_inc(step, 1)
            dve.wait_ge(step, 10)
            dve.tensor_reduce(n2[:], qsq[:].rearrange("p t (h d) -> p (t h) d", d=DH), AX.X, ALU.add).then_inc(step, 1)
            dve.wait_ge(rooted, 2)
            dve.tensor_scalar(n0[:], n1[:], 1e-12, None, ALU.max).then_inc(step, 1)
            dve.wait_ge(step, 12)
            dve.reciprocal(ninv[:], n0[:]).then_inc(step, 1)
            dve.wait_ge(step, 13)
            dve.tensor_tensor(ninv[:], ninv[:], n2[:], ALU.mult).then_inc(step, 1)
            dve.wait_ge(step, 14)
            dve.tensor_tensor(ninv[:], ninv[:], n1[:], ALU.add).then_inc(step, 1)
            dve.wait_ge(step, 15)
            dve.tensor_scalar(n0[:], ninv[:], 0.5, 1e-12, ALU.mult, ALU.max).then_inc(step, 1)
            dve.wait_ge(step, 16)
            dve.reciprocal(n1[:], n0[:]).then_inc(step, 1)
            dve.wait_ge(step, 17)
            dve.tensor_tensor(qn[:].rearrange("p t (h d) -> p (t h) d", d=DH),
                              qkv[:, :, 0:NQK].rearrange("p t (h d) -> p t h d", d=DH),
                              n1[:].unsqueeze(2).broadcast_to([P, NT * 6, DH]), ALU.mult).then_inc(step, 1)
            dve.wait_ge(masks, 1 + QT)
            dve.wait_ge(scaled, 1)
            for g in range(NT + 1):
                if g < NT:
                    dve.wait_ge(scored, g + 1)
                    if g >= 2:
                        dve.wait_ge(exped, H * (g - 1))
                    dve.tensor_tensor(lg[g % 2][:], duo[g % 2][:].rearrange("p (h n) -> p h n", h=H),
                                      cmask[:, g % QT, :].unsqueeze(1).broadcast_to([P, H, S]), ALU.add).then_inc(masked, 1)
                    dve.wait_ge(masked, g + 1)
                    dve.tensor_reduce(top[:, g, :], lg[g % 2][:], AX.X, ALU.max).then_inc(step, 1)
                    dve.wait_ge(step, 19 + 2 * g)
                    dve.tensor_scalar(bias[:, g, :], top[:, g, :], scale[:], -1.0, ALU.mult, ALU.mult).then_inc(maxed, 1)
                    dve.wait_ge(exped, H * (g + 1))
                    dve.reciprocal(inv[:, g, :], total[:, g, :]).then_inc(step, 1)
                    dve.wait_ge(step, 20 + 2 * g)
                    dve.wait_ge(mixed, g + 1)
                    if g >= 2:
                        dve.wait_ge(o_turned, g - 1)
                    dve.tensor_tensor(o[g % 2][:].rearrange("p (h d) -> p h d", d=DH),
                                      mixp[:, 0:D].rearrange("p (h d) -> p h d", d=DH),
                                      inv[:, g, :].unsqueeze(2).broadcast_to([P, H, DH]), ALU.mult).then_inc(o_normed, 1)
                if g >= 1:
                    t = g - 1
                    dve.wait_ge(projected, t + 1)
                    dve.scalar_tensor_tensor(y[:, t, :], outp[:, 0:D], two_c[:, 0:1], xn[:, t, :],
                                             ALU.mult, ALU.add).then_inc(blended, 1)
                    dve.wait_ge(blended, t + 1)
                    dve.tensor_tensor(x[:, t, :], x[:, t, :], y[:, t, :], ALU.add).then_inc(added, 1)


def feed_forward(c, xn, w1, b1, w2, b2, x, out, identb, ones, tag):
    nc = c.nc
    F = 1024
    FT = F // P
    w_in, wstep, summed, step, rooted = (c.sem(tag + n) for n in ("w_in", "wstep", "summed", "step", "rooted"))
    w_turned, w_kept, b_spread, b_kept = (c.sem(tag + n) for n in ("w_turned", "w_kept", "b_spread", "b_kept"))
    x_turned, x_kept, up_made, scaled, gelued, squared = (c.sem(tag + n) for n in
                                                          ("x_turned", "x_kept", "up_made", "scaled", "gelued", "squared"))
    h_turned, h_kept, down_made, added, stored, hstep, biased = (
        c.sem(tag + n) for n in ("h_turned", "h_kept", "down_made", "added", "stored", "hstep", "biased"))
    with ExitStack() as s:
        def sb(n, shape, dt=F32):
            return s.enter_context(nc.sbuf_tensor(tag + n, shape, dt))

        w1_sb, w2_sb = sb("w1", [P, FT, D]), sb("w2", [P, KT, F])
        q1, q2 = sb("q1", [P, FT, D], BF16), sb("q2", [P, KT, F], BF16)
        w1T, w2T = sb("w1T", [P, KT, F], BF16), sb("w2T", [P, FT, D], BF16)
        wsum, mean, wscale = sb("wsum", [P, 2]), sb("mean", [P, 2]), sb("wscale", [P, 2])
        brow, b_all = sb("brow", [1, F + D]), sb("b_all", [P, F + D])
        sq, ms, var, root, tmp = sb("sq", [P, NT, D]), sb("ms", [P, NT]), sb("var", [P, NT]), sb("root", [P, NT]), sb("tmp", [P, 4, NT])
        big, cut, back = sb("big", [P, NT]), sb("cut", [P, NT]), sb("back", [P, NT])
        xs, xq, xqT = sb("xs", [P, NT, D]), sb("xq", [P, NT, D], BF16), sb("xqT", [P, KT, N], BF16)
        h = sb("h", [P, NT, F])
        hq = sb("hq", [P, NT, F], BF16)
        junk = [sb(f"junk{i}", [P, F]) for i in range(2)]
        hqT = [sb(f"hqT{i}", [P, FT, P], BF16) for i in range(2)]
        ms2, var2, root2, tmp2 = sb("ms2", [P, NT]), sb("var2", [P, NT]), sb("root2", [P, NT]), sb("tmp2", [P, 4, NT])
        big2, cut2, back2 = sb("big2", [P, NT]), sb("cut2", [P, NT]), sb("back2", [P, NT])
        y = sb("y", [P, NT, D])
        tp = [s.enter_context(nc.psum_tensor(f"{tag}tp{i}", [P, 1024], BF16)) for i in range(2)]
        up = [s.enter_context(nc.psum_tensor(f"{tag}up{i}", [P, 1024], F32)) for i in range(2)]
        down = [s.enter_context(nc.psum_tensor(f"{tag}down{i}", [P, 512], F32)) for i in range(2)]
        block = s.enter_context(nc.Block())

        @block.sync
        def _(sp):
            sp.dma_start(w1_sb[:], w1.rearrange("(k p) n -> p k n", p=P)).then_inc(w_in, 16)
            sp.dma_start(w2_sb[:], w2.rearrange("(k p) n -> p k n", p=P)).then_inc(w_in, 16)
            sp.dma_start(brow[:, 0:F], b1.rearrange("(a n) -> a n", a=1)).then_inc(w_in, 16)
            sp.dma_start(brow[:, F:], b2.rearrange("(a n) -> a n", a=1)).then_inc(w_in, 16)
            rows = out.rearrange("b s d -> (b s) d").rearrange("(t p) d -> p t d", p=P)
            for t in range(0, NT, 2):
                sp.wait_ge(added, t + 2)
                sp.dma_start(rows[:, t:t + 2, :], y[:, t:t + 2, :]).then_inc(stored, 16)
            sp.wait_ge(stored, 8 * NT)

        @block.tensor
        def _(pe):
            pe.wait_ge(w_in, 64)
            for i, (lo, hi) in enumerate(((0, 512), (512, 1024))):
                pe.matmul(up[0][:, lo:hi], ones[0:1, :], brow[:, lo:hi], start=True, stop=True)
            pe.matmul(up[1][:, 0:D], ones[0:1, :], brow[:, F:], start=True, stop=True).then_inc(b_spread, 1)
            pe.wait_ge(wstep, 2)
            pe.matmul(down[0][:, 0:2], ones[:], wsum[:], start=True, stop=True).then_inc(summed, 1)
            pe.wait_ge(wstep, 10)
            for i in range(4):
                if i >= 2:
                    pe.wait_ge(w_kept, i - 1)
                for j in range(8):
                    if i < 2:
                        mm = pe.transpose(tp[i % 2][:, j * P:(j + 1) * P], q1[:, j, i * P:(i + 1) * P], identb[:])
                    else:
                        f = 4 * (i - 2) + j // 2
                        mm = pe.transpose(tp[i % 2][:, j * P:(j + 1) * P], q2[:, j % 2, f * P:(f + 1) * P], identb[:])
                mm.then_inc(w_turned, 1)
            pe.wait_ge(w_kept, 4)
            pe.wait_ge(step, 16)
            for i in range(KT):
                for t in range(NT):
                    mm = pe.transpose(tp[i][:, t * P:(t + 1) * P], xq[:, t, i * P:(i + 1) * P], identb[:])
                mm.then_inc(x_turned, 1)
            pe.wait_ge(x_kept, KT)
            pe.wait_ge(b_kept, 1)
            for t in range(NT):
                if t >= 2:
                    pe.wait_ge(scaled, t - 1)
                for half in range(2):
                    for k in range(KT):
                        mm = pe.matmul(up[t % 2][:, half * 512:half * 512 + 512], xqT[:, k, t * P:(t + 1) * P],
                                       w1T[:, k, half * 512:half * 512 + 512], start=k == 0, stop=k == KT - 1)
                mm.then_inc(up_made, 1)
            for t in range(NT):
                pe.wait_ge(hstep, 12 + NT + t + 1)
                if t >= 2:
                    pe.wait_ge(h_kept, t - 1)
                for f in range(FT):
                    mm = pe.transpose(tp[t % 2][:, f * P:(f + 1) * P], hq[:, t, f * P:(f + 1) * P], identb[:])
                mm.then_inc(h_turned, 1)
                pe.wait_ge(h_kept, t + 1)
                if t >= 2:
                    pe.wait_ge(added, t - 1)
                for f in range(FT):
                    mm = pe.matmul(down[t % 2][:, 0:D], hqT[t % 2][:, f, :], w2T[:, f, :], start=f == 0, stop=f == FT - 1)
                mm.then_inc(down_made, 1)

        @block.scalar
        def _(act):
            act.wait_ge(b_spread, 1)
            act.activation(b_all[:, 0:F], up[0][:], ACT.Copy)
            act.activation(b_all[:, F:], up[1][:, 0:D], ACT.Copy).then_inc(b_kept, 1)
            act.wait_ge(step, 2)
            act.activation(root[:], var[:], ACT.Sqrt).then_inc(rooted, 1)
            for i in range(4):
                act.wait_ge(w_turned, i + 1)
                if i < 2:
                    act.activation(w1T[:, i, :], tp[i % 2][:], ACT.Copy).then_inc(w_kept, 1)
                else:
                    act.activation(w2T[:, 4 * (i - 2):4 * (i - 1), :].rearrange("p f n -> p (f n)"), tp[i % 2][:],
                                   ACT.Copy).then_inc(w_kept, 1)
            for i in range(KT):
                act.wait_ge(x_turned, i + 1)
                act.activation(xqT[:, i, :], tp[i][:], ACT.Copy).then_inc(x_kept, 1)
            for t in range(NT):
                act.wait_ge(scaled, t + 1)
                act.activation(h[:, t, :], h[:, t, :], ACT.Gelu).then_inc(gelued, 1)
                act.wait_ge(gelued, t + 1)
                if t >= 2:
                    act.wait_ge(squared, t - 1)
                act.activation(junk[t % 2][:], h[:, t, :], ACT.Square, accum_out=ms2[:, t:t + 1]).then_inc(squared, 1)
            act.wait_ge(hstep, NT + 1)
            act.activation(root2[:], var2[:], ACT.Sqrt).then_inc(rooted, 1)
            for t in range(NT):
                act.wait_ge(h_turned, t + 1)
                if t >= 2:
                    act.wait_ge(down_made, t - 1)
                act.activation(hqT[t % 2][:].rearrange("p f n -> p (f n)"), tp[t % 2][:], ACT.Copy).then_inc(h_kept, 1)

        @block.vector
        def _(dve):
            dve.wait_ge(w_in, 64)
            dve.tensor_reduce(wsum[:, 0:1], w1_sb[:].rearrange("p k n -> p (k n)"), AX.X, ALU.add,
                              apply_absolute_value=True).then_inc(wstep, 1)
            dve.tensor_reduce(wsum[:, 1:2], w2_sb[:].rearrange("p k n -> p (k n)"), AX.X, ALU.add,
                              apply_absolute_value=True).then_inc(wstep, 1)
            for t in range(NT):
                ins = dve.tensor_tensor_reduce(sq[:, t, :], xn[:, t, :], xn[:, t, :], 1.0 / D, 0.0, ALU.mult, ALU.add,
                                               ms[:, t:t + 1])
            ins.then_inc(step, 1)
            dve.wait_ge(step, 1)
            dve.tensor_scalar(var[:], ms[:], 1e-6, None, ALU.add).then_inc(step, 1)
            dve.tensor_reduce(big[:], xn[:], AX.X, ALU.max, apply_absolute_value=True).then_inc(step, 1)
            dve.wait_ge(summed, 1)
            dve.tensor_scalar(mean[:], down[0][:, 0:2], 1.0 / (F * D), 1e-5, ALU.mult, ALU.max).then_inc(wstep, 1)
            dve.wait_ge(wstep, 3)
            dve.reciprocal(wscale[:], mean[:]).then_inc(wstep, 1)
            dve.wait_ge(wstep, 4)
            f1, f2 = w1_sb[:].rearrange("p k n -> p (k n)"), w2_sb[:].rearrange("p k n -> p (k n)")
            for i, f in enumerate((f1, f2)):
                dve.tensor_scalar(f, f, wscale[:, i:i + 1], MAGIC, ALU.mult, ALU.add).then_inc(wstep, 1)
            dve.wait_ge(wstep, 6)
            for f in (f1, f2):
                dve.tensor_scalar(f, f, MAGIC, 1.0, ALU.subtract, ALU.min).then_inc(wstep, 1)
            dve.wait_ge(wstep, 8)
            for f, q in ((f1, q1), (f2, q2)):
                dve.tensor_scalar(q[:].rearrange("p k n -> p (k n)"), f, -1.0, None, ALU.max).then_inc(wstep, 1)
            dve.wait_ge(wstep, 10)
            dve.wait_ge(rooted, 1)
            refine_root(dve, step, 3, var[:], root[:], tmp)
            dve.wait_ge(step, 8)
            dve.tensor_tensor(big[:], big[:], tmp[:, 3], ALU.mult).then_inc(step, 1)
            dve.wait_ge(step, 9)
            dve.tensor_scalar(big[:], big[:], 1e-5, None, ALU.max).then_inc(step, 1)
            dve.wait_ge(step, 10)
            dve.reciprocal(cut[:], big[:]).then_inc(step, 1)
            dve.wait_ge(step, 11)
            dve.tensor_scalar(cut[:], cut[:], 127.0, None, ALU.mult).then_inc(step, 1)
            dve.tensor_scalar(back[:], big[:], 1.0 / 127.0, mean[:, 0:1], ALU.mult, ALU.mult).then_inc(step, 1)
            dve.wait_ge(step, 13)
            for t in range(NT):
                ins = dve.tensor_scalar(xs[:, t, :], xn[:, t, :], tmp[:, 3, t:t + 1], cut[:, t:t + 1], ALU.mult, ALU.mult)
            ins.then_inc(step, 1)
            dve.wait_ge(step, 14)
            dve.tensor_scalar(xs[:], xs[:], MAGIC, MAGIC, ALU.add, ALU.subtract).then_inc(step, 1)
            dve.wait_ge(step, 15)
            dve.tensor_scalar(xq[:], xs[:], 127.0, -128.0, ALU.min, ALU.max).then_inc(step, 1)
            dve.wait_ge(b_kept, 1)
            for t in range(NT):
                dve.wait_ge(up_made, t + 1)
                dve.scalar_tensor_tensor(h[:, t, :], up[t % 2][:], back[:, t:t + 1], b_all[:, 0:F],
                                         ALU.mult, ALU.add).then_inc(scaled, 1)
                if t >= 1:
                    dve.wait_ge(gelued, t)
                    dve.tensor_reduce(big2[:, t - 1:t], h[:, t - 1, :], AX.X, ALU.max,
                                      apply_absolute_value=True).then_inc(hstep, 1)
            dve.wait_ge(gelued, NT)
            dve.tensor_reduce(big2[:, NT - 1:NT], h[:, NT - 1, :], AX.X, ALU.max,
                              apply_absolute_value=True).then_inc(hstep, 1)
            dve.wait_ge(squared, NT)
            dve.tensor_scalar(var2[:], ms2[:], 1.0 / F, 1e-6, ALU.mult, ALU.add).then_inc(hstep, 1)
            dve.wait_ge(rooted, 2)
            refine_root(dve, hstep, NT + 1, var2[:], root2[:], tmp2)
            dve.wait_ge(hstep, NT + 6)
            dve.tensor_tensor(big2[:], big2[:], tmp2[:, 3], ALU.mult).then_inc(hstep, 1)
            dve.wait_ge(hstep, NT + 7)
            dve.tensor_scalar(big2[:], big2[:], 1e-5, None, ALU.max).then_inc(hstep, 1)
            dve.wait_ge(hstep, NT + 8)
            dve.reciprocal(cut2[:], big2[:]).then_inc(hstep, 1)
            dve.wait_ge(hstep, NT + 9)
            dve.tensor_scalar(cut2[:], cut2[:], 127.0, None, ALU.mult).then_inc(hstep, 1)
            dve.tensor_scalar(back2[:], big2[:], 1.0 / 127.0, mean[:, 1:2], ALU.mult, ALU.mult).then_inc(hstep, 1)
            dve.wait_ge(hstep, NT + 11)
            dve.tensor_tensor(x[:], x[:], b_all[:, F:].unsqueeze(1).broadcast_to([P, NT, D]), ALU.add).then_inc(hstep, 1)

            def add_out(t):
                dve.wait_ge(down_made, t + 1)
                dve.scalar_tensor_tensor(y[:, t, :], down[t % 2][:, 0:D], back2[:, t:t + 1], x[:, t, :],
                                         ALU.mult, ALU.add).then_inc(added, 1)

            for t in range(NT):
                dve.tensor_scalar(h[:, t, :], h[:, t, :], tmp2[:, 3, t:t + 1], cut2[:, t:t + 1], ALU.mult, ALU.mult).then_inc(biased, 1)
                dve.wait_ge(biased, 2 * t + 1)
                dve.tensor_scalar(h[:, t, :], h[:, t, :], MAGIC, MAGIC, ALU.add, ALU.subtract).then_inc(biased, 1)
                dve.wait_ge(biased, 2 * t + 2)
                dve.tensor_scalar(hq[:, t, :], h[:, t, :], 127.0, -128.0, ALU.min, ALU.max).then_inc(hstep, 1)
                if t >= 2:
                    add_out(t - 2)
            add_out(NT - 2)
            add_out(NT - 1)


def perceiver(nc, a, out, stages=range(1, 7)):
    with ExitStack() as stack:
        c = Ctx(nc)
        first_in = [stack.enter_context(nc.semaphore(f"first_in{i}")) for i in range(2)]
        x_rows = nc.dram_tensor("x_rows", [N, D], F32, kind="Internal")
        o_rows = nc.dram_tensor("o_rows", [B, P, 1024], F32, kind="Internal")
        sum_rows = nc.dram_tensor("sum_rows", [B, P, 1024], F32, kind="Internal")
        q0 = nc.dram_tensor("q0", [3, 256, N], BF16, kind="Internal")
        q1 = nc.dram_tensor("q1", [3, 512, N], BF16, kind="Internal")
        k0 = nc.dram_tensor("k0", [2, 3, 256, CH], BF16, kind="Internal")
        v0 = nc.dram_tensor("v0", [B * S2, 16 * 17], F32, kind="Internal")
        v1 = nc.dram_tensor("v1", [B * S2, 8 * 64], F32, kind="Internal")
        bias_qk = nc.dram_tensor("bias_qk", [S, S2], F32, kind="Internal")
        bias_kq = nc.dram_tensor("bias_kq", [S2, S], F32, kind="Internal")
        inputs = nc.dram_tensor("inputs", [E * CAP, D], F32, kind="Internal")
        outputs = nc.dram_tensor("outputs", [E * CAP, D], F32, kind="Internal")
        scattered = stack.enter_context(nc.semaphore("scattered"))
        gathered = [stack.enter_context(nc.semaphore(f"gathered{i}")) for i in range(2)]
        ident = stack.enter_context(nc.sbuf_tensor("ident", [P, P], F32))
        identb = stack.enter_context(nc.sbuf_tensor("identb", [P, P], BF16))
        ones = stack.enter_context(nc.sbuf_tensor("ones", [P, P], F32))
        with c.stage():
            constants(c, ident, identb, ones, "c_")
        x_in = a["x"].rearrange("b s d -> (b s) d")

        def tile_of_rows(s, name):
            return s.enter_context(nc.sbuf_tensor(name, [P, NT, D], F32))

        def normed(s, x, tag, x_from=None):
            xn = tile_of_rows(s, tag + "xn")
            xnT = s.enter_context(nc.sbuf_tensor(tag + "xnT", [P, KT, N], F32))
            layer_norm(c, x_from, x, xn, xnT, ident, tag)
            return xn, xnT

        if 1 in stages:
            with c.stage():
                short = stack.enter_context(nc.sbuf_tensor("short", [1, 1], mybir.dt.int32))
                with ExitStack() as s:
                    mask_in, lead_in = c.sem("mask_in"), [c.sem(f"lead_in{b}") for b in range(B)]
                    m = s.enter_context(nc.sbuf_tensor("m", [P, QT, S2], F32))
                    lead = [s.enter_context(nc.sbuf_tensor(f"lead{b}", [P, LAST // P * D], F32)) for b in range(B)]
                    q_max = s.enter_context(nc.sbuf_tensor("q_max", [P, 1], F32))
                    part = s.enter_context(nc.sbuf_tensor("part", [P, B], F32))
                    low = s.enter_context(nc.sbuf_tensor("low", [P, 2 * QT], F32))

                    def prefetch(act):
                        act.dma_start(m[:], a["mask_1x1xSxS2_fk1"][0, 0].rearrange("(i p) k -> p i k", p=P)).then_inc(mask_in, 16)
                        for b in range(B):
                            act.dma_start(lead[b][:], a["ctx_1024"][b, 0:LAST].rearrange("(p t) c -> p (t c)", p=P)
                                          ).then_inc(lead_in[b], 16)

                    def measure(dve, q):
                        dve.wait_ge(mask_in, 16)
                        dve.tensor_reduce(low[:, 0:QT], m[:, :, 0:LAST], AX.X, ALU.min)
                        dve.tensor_reduce(low[:, QT:2 * QT], m[:, :, LAST:S2], AX.X, ALU.min)
                        dve.tensor_reduce(q_max[:], q, AX.X, ALU.max, apply_absolute_value=True)
                        for b in range(B - 1):
                            dve.wait_ge(lead_in[b], 16)
                            dve.tensor_reduce(part[:, b:b + 1], lead[b][:], AX.X, ALU.max, apply_absolute_value=True)

                    with ExitStack() as t:
                        _, xnT = normed(t, tile_of_rows(t, "x0"), "n0_", x_in)
                        split_queries(c, xnT, a["L0_xattn_wq"], a["L0_xattn_bq"], 0.25, 256, q0, "q0_", prefetch, measure)
                    scale_mask(c, m, mask_in, LAST, S2, None, bias_qk, bias_kq, ident, "m1_")
                    survey(c, low, lead, lead_in, part, a["L0_xattn_wk"], a["L0_xattn_bk"], q_max[:], 16, short, ident, "sv_")
                    scale_mask(c, m, mask_in, 0, LAST, short, bias_qk, bias_kq, ident, "m0_")
                short_attention(c, a["ctx_1024"], a["L0_xattn_wk"], a["L0_xattn_bk"], a["L0_xattn_wv"], q0, k0, v0, o_rows,
                                bias_qk, bias_kq, short, ident, "b0_")
                cross_attention(c, 16, a["ctx_1024"], a["L0_xattn_wk"], a["L0_xattn_bk"], a["L0_xattn_wv"], q0, k0, v0, o_rows,
                                None, bias_qk, bias_kq, short, first_in[0], ident, ones, "a0_")
                middle = stack.enter_context(ExitStack())
                x = tile_of_rows(middle, "x1")
                project_heads(c, 16, o_rows, None, a["L0_xattn_bv"], a["L0_xattn_wo"], a["L0_xattn_bo"], x_in, x, ones, "p0_")
        if 2 in stages:
            with c.stage(), ExitStack() as s:
                _, xnT = normed(s, x, "n1_")
                channel_attention(c, xnT, a["L0_attn_Wqk"], a["L0_attn_Wv"], a["L0_attn_Wo"], a["L0_attn_tau"], x,
                                  ident, ones, "ch_")
        if 3 in stages:
            with c.stage(), ExitStack() as s:
                xn, xnT = normed(s, x, "n2_")
                gates = s.enter_context(nc.sbuf_tensor("gates", [P, 2, NT], F32))
                seat_in, seat_out = (s.enter_context(nc.sbuf_tensor(n, [P, 2 * NT], U32)) for n in ("seat_in", "seat_out"))
                onesb = s.enter_context(nc.sbuf_tensor("onesb", [P, P], BF16))
                route(c, xnT, a["L0_ffn_Wg"], gates, seat_in, seat_out, inputs, onesb, "r_")
                experts(c, xn, gates, seat_in, seat_out, inputs, outputs, a["L0_ffn_W_in"], a["L0_ffn_W_out"], x,
                        (scattered, gathered), ident, "e_")
        if 4 in stages:
            with c.stage():
                with ExitStack() as s:
                    _, xnT = normed(s, x, "n3_")
                    split_queries(c, xnT, a["L1_xattn_Wq"], None, 0.125, 512, q1, "q1_", x=x, x_to=x_rows.ap())
                middle.close()
                cross_attention(c, 8, a["ctx_1024"], a["L1_xattn_Wk"], None, a["L1_xattn_Wv"], q1, None, v1, o_rows,
                                sum_rows, None, None, None, first_in[1], ident, ones, "a1_")
                x = tile_of_rows(stack, "x2")
                project_heads(c, 8, o_rows, sum_rows, None, a["L1_xattn_Wo"], a["L1_xattn_bo"], x_rows.ap(), x, ones, "p1_")
        if 5 in stages:
            with c.stage(), ExitStack() as s:
                xn, xnT = normed(s, x, "n4_")
                self_attention(c, xn, xnT, a["L1_attn_norm_w"], a["L1_attn_Wq"], a["L1_attn_Wk"], a["L1_attn_Wv"],
                               a["L1_attn_Wo"], a["L1_attn_gate"], a["L1_attn_log_temperature"], x, ident, ones, "s_")
        if 6 in stages:
            with c.stage(), ExitStack() as s:
                xn, _ = normed(s, x, "n5_")
                feed_forward(c, xn, a["L1_ffn_w1"], a["L1_ffn_b1"], a["L1_ffn_w2"], a["L1_ffn_b2"], x, out,
                             identb, ones, "f_")


_INS = ["x", "ctx_1024", "mask_1x1xSxS2_fk1", "L0_xattn_wq", "L0_xattn_bq", "L0_xattn_wk", "L0_xattn_bk",
        "L0_xattn_wv", "L0_xattn_bv", "L0_xattn_wo", "L0_xattn_bo", "L0_attn_Wqk", "L0_attn_Wv", "L0_attn_Wo",
        "L0_attn_tau", "L0_ffn_Wg", "L0_ffn_W_in", "L0_ffn_W_out", "L1_xattn_Wq", "L1_xattn_Wk", "L1_xattn_Wv",
        "L1_xattn_Wo", "L1_xattn_bo", "L1_attn_norm_w", "L1_attn_Wq", "L1_attn_Wk", "L1_attn_Wv", "L1_attn_Wo",
        "L1_attn_gate", "L1_attn_log_temperature", "L1_ffn_w1", "L1_ffn_b1", "L1_ffn_w2", "L1_ffn_b2"]


def kernel(**inputs):
    import numpy as np
    from concourse import bacc
    from concourse.bass_utils import run_bass_kernel_spmd

    nc = bacc.Bacc("TRN2", target_bir_lowering=False, num_devices=1)
    arrays, args = {}, {}
    for name in _INS:
        v = np.ascontiguousarray(inputs[name])
        if v.ndim == 0:
            v = v.reshape(1, 1)
        arrays[name + "_in"] = v
        args[name] = nc.dram_tensor(name + "_in", v.shape, mybir.dt.from_np(v.dtype), kind="ExternalInput").ap()
    out = nc.dram_tensor("out", (B, S, D), F32, kind="ExternalOutput").ap()
    perceiver(nc, args, out)
    r = run_bass_kernel_spmd(nc, [arrays], core_ids=[0])
    return r.results[0]["out"]
```
